# Optimizing a Trainium2 kernel written in Bass

```python
import numpy as np
import jax
import jax.numpy as jnp

def _softmax(x, axis=-1):
    return jax.nn.softmax(x, axis=axis)

def _gelu(x):
    return jax.nn.gelu(x, approximate=True)

def _silu(x):
    return jax.nn.silu(x)

def _sigmoid(x):
    return jax.nn.sigmoid(x)

def _layernorm(x, axis=-1, eps=1e-05):
    m = jnp.mean(x, axis=axis, keepdims=True)
    v = jnp.var(x, axis=axis, keepdims=True)
    return (x - m) / jnp.sqrt(v + eps)

def _scatter_add(tgt, idx, src, axis=0):
    return tgt.at[idx].add(src)

def _segment_sum(src, seg, n):
    return jax.ops.segment_sum(src, seg, n)
kernel_name = 'mk_prb_d2_jaxref_r4_68b412'

def setup_inputs(seed: int=0):
    np.random.seed(seed)
    _w = jnp.asarray

    def _L0_attn_setup():
        import jax, jax.numpy as jnp
        import numpy as np
        B, S, D = (2, 512, 512)
        N_HEADS, N_KV_HEADS = (16, 4)
        HEAD_DIM = D // N_HEADS

        def _apply_rope(xh, positions):
            Dh = xh.shape[-1]
            half = Dh // 2
            freqs = 1.0 / 10000.0 ** (jnp.arange(half, dtype=jnp.float32) / half)
            angles = positions[:, None].astype(jnp.float32) * freqs[None, :]
            cos, sin = (jnp.cos(angles), jnp.sin(angles))
            xp = xh.reshape(*xh.shape[:-1], half, 2)
            x0, x1 = (xp[..., 0], xp[..., 1])
            r0 = x0 * cos - x1 * sin
            r1 = x0 * sin + x1 * cos
            return jnp.stack([r0, r1], axis=-1).reshape(xh.shape)
        key = jax.random.key(seed)
        ks = jax.random.split(key, 5)
        x = jax.random.normal(ks[0], (B, S, D), dtype=jnp.float32)
        W_q = jax.random.normal(ks[1], (D, D), dtype=jnp.float32) * 0.02
        W_k = jax.random.normal(ks[2], (D, N_KV_HEADS * HEAD_DIM), dtype=jnp.float32) * 0.02
        W_v = jax.random.normal(ks[3], (D, N_KV_HEADS * HEAD_DIM), dtype=jnp.float32) * 0.02
        W_o = jax.random.normal(ks[4], (D, D), dtype=jnp.float32) * 0.02
        return {'x': x, 'W_q': W_q, 'W_k': W_k, 'W_v': W_v, 'W_o': W_o}
    _L0_attn_in = _L0_attn_setup()

    def _L0_ffn_setup():
        import jax, jax.numpy as jnp
        import numpy as np
        B, S, D, H = (4, 512, 512, 2048)

        def fwht(x):
            orig_shape = x.shape
            n = orig_shape[-1]
            x = x.reshape(-1, n)
            h = 1
            while h < n:
                xb = x.reshape(-1, n // (2 * h), 2, h)
                a = xb[:, :, 0, :]
                b = xb[:, :, 1, :]
                x = jnp.stack([a + b, a - b], axis=2).reshape(-1, n)
                h *= 2
            scale = jnp.asarray(1.0 / np.sqrt(n), dtype=x.dtype)
            return (x * scale).reshape(orig_shape)
        key = jax.random.key(seed)
        kx, k1, k2, k3 = jax.random.split(key, 4)
        x = jax.random.normal(kx, (B, S, D), dtype=jnp.float32)
        W1 = jax.random.normal(k1, (H, D), dtype=jnp.float32) * (1.0 / np.sqrt(D))
        W2 = jax.random.normal(k2, (D, H), dtype=jnp.float32) * (1.0 / np.sqrt(H))
        W3 = jax.random.normal(k3, (H, D), dtype=jnp.float32) * (1.0 / np.sqrt(D))
        return {'x': x, 'W1': W1, 'W2': W2, 'W3': W3}
    _L0_ffn_in = _L0_ffn_setup()

    def _L1_attn_setup():
        import jax, jax.numpy as jnp
        import numpy as np
        D_MODEL = 512
        N_HEADS = 16
        N_KV = 4
        HEAD_DIM = 128
        SUB = 64
        WINDOW = 128
        THETA = 10000.0
        NEG = jnp.float32(-1e+30)

        def _rope_tables(seq_len):
            inv_freq = 1.0 / THETA ** (jnp.arange(0, HEAD_DIM, 2, dtype=jnp.float32) / HEAD_DIM)
            freqs = jnp.arange(seq_len, dtype=jnp.float32)[:, None] * inv_freq[None, :]
            emb = jnp.concatenate([freqs, freqs], axis=-1)
            return (jnp.cos(emb), jnp.sin(emb))

        def _rotate_half(x):
            x1, x2 = (x[..., :HEAD_DIM // 2], x[..., HEAD_DIM // 2:])
            return jnp.concatenate([-x2, x1], axis=-1)

        def _apply_rope(t, cos, sin):
            c = cos[None, None]
            s = sin[None, None]
            return t * c + _rotate_half(t) * s
        key = jax.random.key(seed)
        ks = jax.random.split(key, 6)
        B, S = (1, 512)
        std = 0.02
        return {'x': jax.random.normal(ks[0], (B, S, D_MODEL), dtype=jnp.float32), 'Wq': jax.random.normal(ks[1], (D_MODEL, N_HEADS * HEAD_DIM), dtype=jnp.float32) * std, 'Wk': jax.random.normal(ks[2], (D_MODEL, N_KV * HEAD_DIM), dtype=jnp.float32) * std, 'Wv': jax.random.normal(ks[3], (D_MODEL, N_KV * HEAD_DIM), dtype=jnp.float32) * std, 'Wo': jax.random.normal(ks[4], (N_HEADS * HEAD_DIM, D_MODEL), dtype=jnp.float32) * std, 'lam': jnp.full((N_HEADS,), 0.1, dtype=jnp.float32)}
    _L1_attn_in = _L1_attn_setup()

    def _L1_ffn_setup():
        import jax, jax.numpy as jnp
        import numpy as np
        B, S, H = (1, 256, 512)
        E, K = (32, 4)
        F, FS = (352, 1408)
        CAP = 64

        def silu(x):
            return x * jax.nn.sigmoid(x)
        key = jax.random.key(seed)
        ks = jax.random.split(key, 9)
        sc = 0.02
        return {'hidden_states': jax.random.normal(ks[0], (B, S, H), jnp.float32), 'Wr': jax.random.normal(ks[1], (H, E), jnp.float32) * sc, 'Wg': jax.random.normal(ks[2], (E, H, F), jnp.float32) * sc, 'Wu': jax.random.normal(ks[3], (E, H, F), jnp.float32) * sc, 'Wd': jax.random.normal(ks[4], (E, F, H), jnp.float32) * sc, 'Wsg': jax.random.normal(ks[5], (H, FS), jnp.float32) * sc, 'Wsu': jax.random.normal(ks[6], (H, FS), jnp.float32) * sc, 'Wsd': jax.random.normal(ks[7], (FS, H), jnp.float32) * sc, 'Wse': jax.random.normal(ks[8], (H, 1), jnp.float32) * sc}
    _L1_ffn_in = _L1_ffn_setup()
    _d = {'L0_attn_x': _L0_attn_in['x'], 'L0_attn_W_q': _L0_attn_in['W_q'], 'L0_attn_W_k': _L0_attn_in['W_k'], 'L0_attn_W_v': _L0_attn_in['W_v'], 'L0_attn_W_o': _L0_attn_in['W_o'], 'L0_ffn_W1': _L0_ffn_in['W1'], 'L0_ffn_W2': _L0_ffn_in['W2'], 'L0_ffn_W3': _L0_ffn_in['W3'], 'L1_attn_Wq': _L1_attn_in['Wq'], 'L1_attn_Wk': _L1_attn_in['Wk'], 'L1_attn_Wv': _L1_attn_in['Wv'], 'L1_attn_Wo': _L1_attn_in['Wo'], 'L1_attn_lam': _L1_attn_in['lam'], 'L1_ffn_Wr': _L1_ffn_in['Wr'], 'L1_ffn_Wg': _L1_ffn_in['Wg'], 'L1_ffn_Wu': _L1_ffn_in['Wu'], 'L1_ffn_Wd': _L1_ffn_in['Wd'], 'L1_ffn_Wsg': _L1_ffn_in['Wsg'], 'L1_ffn_Wsu': _L1_ffn_in['Wsu'], 'L1_ffn_Wsd': _L1_ffn_in['Wsd'], 'L1_ffn_Wse': _L1_ffn_in['Wse']}
    _x0 = _d['L0_attn_x']
    _d['L0_attn_x'] = jax.random.normal(jax.random.fold_in(jax.random.key(seed), 1), (2, 1024, 512), dtype=_x0.dtype)
    del _x0
    return _d

def reference(L0_attn_x, L0_attn_W_q, L0_attn_W_k, L0_attn_W_v, L0_attn_W_o, L0_ffn_W1, L0_ffn_W2, L0_ffn_W3, L1_attn_Wq, L1_attn_Wk, L1_attn_Wv, L1_attn_Wo, L1_attn_lam, L1_ffn_Wr, L1_ffn_Wg, L1_ffn_Wu, L1_ffn_Wd, L1_ffn_Wsg, L1_ffn_Wsu, L1_ffn_Wsd, L1_ffn_Wse):

    def _L0_attn_ref(x, W_q, W_k, W_v, W_o):
        import jax, jax.numpy as jnp
        import numpy as np
        B, S, D = (2, 512, 512)
        N_HEADS, N_KV_HEADS = (16, 4)
        HEAD_DIM = D // N_HEADS

        def _apply_rope(xh, positions):
            Dh = xh.shape[-1]
            half = Dh // 2
            freqs = 1.0 / 10000.0 ** (jnp.arange(half, dtype=jnp.float32) / half)
            angles = positions[:, None].astype(jnp.float32) * freqs[None, :]
            cos, sin = (jnp.cos(angles), jnp.sin(angles))
            xp = xh.reshape(*xh.shape[:-1], half, 2)
            x0, x1 = (xp[..., 0], xp[..., 1])
            r0 = x0 * cos - x1 * sin
            r1 = x0 * sin + x1 * cos
            return jnp.stack([r0, r1], axis=-1).reshape(xh.shape)
        b, s, d = x.shape
        positions = jnp.arange(s)
        rep = N_HEADS // N_KV_HEADS
        Q = (x @ W_q).reshape(b, s, N_HEADS, HEAD_DIM).transpose(0, 2, 1, 3)
        K = (x @ W_k).reshape(b, s, N_KV_HEADS, HEAD_DIM).transpose(0, 2, 1, 3)
        V = (x @ W_v).reshape(b, s, N_KV_HEADS, HEAD_DIM).transpose(0, 2, 1, 3)
        Qr = _apply_rope(Q, positions)
        K_rep = jnp.tile(K, (1, rep, 1, 1))
        V_rep = jnp.tile(V, (1, rep, 1, 1))
        Kr = _apply_rope(K_rep, positions)
        scores = jnp.einsum('bhqd,bhkd->bhqk', Qr, Kr) / HEAD_DIM ** 0.5
        weights = jax.nn.softmax(scores, axis=-1)
        out = jnp.einsum('bhqk,bhkd->bhqd', weights, V_rep)
        out = out.transpose(0, 2, 1, 3).reshape(b, s, d)
        return out @ W_o

    def _L0_ffn_ref(x, W1, W2, W3):
        import jax, jax.numpy as jnp
        import numpy as np
        B, S, D, H = (4, 512, 512, 2048)

        def fwht(x):
            orig_shape = x.shape
            n = orig_shape[-1]
            x = x.reshape(-1, n)
            h = 1
            while h < n:
                xb = x.reshape(-1, n // (2 * h), 2, h)
                a = xb[:, :, 0, :]
                b = xb[:, :, 1, :]
                x = jnp.stack([a + b, a - b], axis=2).reshape(-1, n)
                h *= 2
            scale = jnp.asarray(1.0 / np.sqrt(n), dtype=x.dtype)
            return (x * scale).reshape(orig_shape)
        up_gate = jnp.einsum('bsd,hd->bsh', x, W1)
        up_lin = jnp.einsum('bsd,hd->bsh', x, W3)
        hidden = jax.nn.silu(up_gate) * up_lin
        hidden = fwht(hidden)
        out = jnp.einsum('bsh,dh->bsd', hidden, W2)
        return out

    def _L1_attn_ref(x, Wq, Wk, Wv, Wo, lam):
        import jax, jax.numpy as jnp
        import numpy as np
        D_MODEL = 512
        N_HEADS = 16
        N_KV = 4
        HEAD_DIM = 128
        SUB = 64
        WINDOW = 128
        THETA = 10000.0
        NEG = jnp.float32(-1e+30)

        def _rope_tables(seq_len):
            inv_freq = 1.0 / THETA ** (jnp.arange(0, HEAD_DIM, 2, dtype=jnp.float32) / HEAD_DIM)
            freqs = jnp.arange(seq_len, dtype=jnp.float32)[:, None] * inv_freq[None, :]
            emb = jnp.concatenate([freqs, freqs], axis=-1)
            return (jnp.cos(emb), jnp.sin(emb))

        def _rotate_half(x):
            x1, x2 = (x[..., :HEAD_DIM // 2], x[..., HEAD_DIM // 2:])
            return jnp.concatenate([-x2, x1], axis=-1)

        def _apply_rope(t, cos, sin):
            c = cos[None, None]
            s = sin[None, None]
            return t * c + _rotate_half(t) * s
        B, S, _ = x.shape
        n_rep = N_HEADS // N_KV
        q = (x @ Wq).reshape(B, S, N_HEADS, HEAD_DIM).transpose(0, 2, 1, 3)
        k = (x @ Wk).reshape(B, S, N_KV, HEAD_DIM).transpose(0, 2, 1, 3)
        v = (x @ Wv).reshape(B, S, N_KV, HEAD_DIM).transpose(0, 2, 1, 3)
        cos, sin = _rope_tables(S)
        q = _apply_rope(q, cos, sin)
        k = _apply_rope(k, cos, sin)
        k = jnp.repeat(k, n_rep, axis=1)
        v = jnp.repeat(v, n_rep, axis=1)
        q1, q2 = (q[..., :SUB], q[..., SUB:])
        k1, k2 = (k[..., :SUB], k[..., SUB:])
        scale = 1.0 / jnp.sqrt(jnp.float32(SUB))
        s1 = jnp.einsum('bhqd,bhkd->bhqk', q1, k1) * scale
        s2 = jnp.einsum('bhqd,bhkd->bhqk', q2, k2) * scale
        i = jnp.arange(S)[:, None]
        j = jnp.arange(S)[None, :]
        allowed = (j <= i) & (j >= i - WINDOW + 1)
        s1 = jnp.where(allowed[None, None], s1, NEG)
        s2 = jnp.where(allowed[None, None], s2, NEG)
        a1 = jax.nn.softmax(s1.astype(jnp.float32), axis=-1).astype(x.dtype)
        a2 = jax.nn.softmax(s2.astype(jnp.float32), axis=-1).astype(x.dtype)
        diff = jax.nn.relu(a1 - lam[None, :, None, None] * a2)
        diff = diff / (jnp.sum(diff, axis=-1, keepdims=True) + 1e-06)
        out = jnp.einsum('bhqk,bhkd->bhqd', diff, v)
        out = out.transpose(0, 2, 1, 3).reshape(B, S, N_HEADS * HEAD_DIM)
        return out @ Wo

    def _L1_ffn_ref(hidden_states, Wr, Wg, Wu, Wd, Wsg, Wsu, Wsd, Wse):
        import jax, jax.numpy as jnp
        import numpy as np
        B, S, H = (1, 256, 512)
        E, K = (32, 4)
        F, FS = (352, 1408)
        CAP = 64

        def silu(x):
            return x * jax.nn.sigmoid(x)
        b, s_len, h = hidden_states.shape
        x = hidden_states.reshape(-1, h)
        T = x.shape[0]
        probs = jax.nn.softmax(x @ Wr, axis=-1)
        topw, topi = jax.lax.top_k(probs, K)
        topw = topw / jnp.sum(topw, axis=-1, keepdims=True)
        shared = silu(x @ Wsg) * (x @ Wsu) @ Wsd
        shared = shared * jax.nn.sigmoid(x @ Wse)
        sel = topi.reshape(-1)
        w = topw.reshape(-1)
        tok = jnp.repeat(jnp.arange(T), K)
        oh = jax.nn.one_hot(sel, E, dtype=jnp.int32)
        pos = (jnp.cumsum(oh, axis=0) * oh).sum(-1) - 1
        valid = (pos < CAP).astype(x.dtype)
        posc = jnp.clip(pos, 0, CAP - 1)
        xe = jnp.zeros((E, CAP, h), x.dtype).at[sel, posc].add(x[tok] * valid[:, None])
        g = silu(jnp.einsum('ech,ehf->ecf', xe, Wg))
        u = jnp.einsum('ech,ehf->ecf', xe, Wu)
        ye = jnp.einsum('ecf,efh->ech', g * u, Wd)
        y_pair = ye[sel, posc] * (w * valid)[:, None]
        out = shared.at[tok].add(y_pair)
        return out.reshape(b, s_len, h)
    x = L0_attn_x
    xn = _layernorm(x, axis=-1)
    x = x + _L0_attn_ref(xn, L0_attn_W_q, L0_attn_W_k, L0_attn_W_v, L0_attn_W_o) + _L0_ffn_ref(xn, L0_ffn_W1, L0_ffn_W2, L0_ffn_W3)
    xn = _layernorm(x, axis=-1)
    x = x + _L1_attn_ref(xn, L1_attn_Wq, L1_attn_Wk, L1_attn_Wv, L1_attn_Wo, L1_attn_lam) + _L1_ffn_ref(xn, L1_ffn_Wr, L1_ffn_Wg, L1_ffn_Wu, L1_ffn_Wd, L1_ffn_Wsg, L1_ffn_Wsu, L1_ffn_Wsd, L1_ffn_Wse)
    return x

_drawn_inputs = setup_inputs


def setup_inputs(seed=0):
    import zlib

    import numpy as np

    out = dict(_drawn_inputs(seed))
    spreads = {'L1_attn_lam': (0.10000000149011612, 0.6)}
    factors = {'L0_attn_W_q': 8.0,
     'L0_attn_W_k': 8.0,
     'L0_attn_W_v': 8.0,
     'L0_attn_W_o': 8.0,
     'L1_attn_Wq': 44.762,
     'L1_attn_Wk': 44.623,
     'L1_ffn_Wr': 7.339,
     'L1_ffn_Wg': 7.051,
     'L1_ffn_Wu': 6.929,
     'L1_ffn_Wd': 6.903,
     'L1_ffn_Wse': 64.0,
     'L1_ffn_Wsg': 8.0,
     'L1_ffn_Wsu': 8.0,
     'L1_ffn_Wsd': 8.0,
     'L1_attn_Wv': 6.246,
     'L1_attn_Wo': 6.247}
    for name, (base, spread) in spreads.items():
        noise = np.random.default_rng([zlib.crc32(name.encode()), seed]).standard_normal(out[name].shape)
        drawn = base * np.exp(spread * noise) if base else spread * noise
        out[name] = jnp.asarray(drawn.astype(out[name].dtype))
    for name, factor in factors.items():
        out[name] = (out[name] * factor).astype(out[name].dtype)
    return out
```

```python
from contextlib import ExitStack

import numpy as np

import concourse.bass as bass
from concourse import mybir

F32 = mybir.dt.float32
U32 = mybir.dt.uint32
ALU = mybir.AluOpType
ACT = mybir.ActivationFunctionType
AX = mybir.AxisListType

P = 128
BATCH, SEQ, D = 2, 1024, 512
T = BATCH * SEQ
NT = T // P
KD = D // P
CH = 512
NC = T // CH
EPS = 1e-5

H0, KV0, HD0 = 16, 4, 32
QT0 = H0 * HD0 // P
HPT = P // HD0
QB = SEQ // P
UN0 = QT0 * HPT
F0 = 2048
H1, KV1, HD1, SUB = 16, 4, 128, 64
WINDOW = 128
NEG = -1e30
E, TOPK, CAP, F1, FS = 32, 4, 64, 352, 1408
SLOTS = E * CAP
FT1 = (F1 + P - 1) // P
F1R = F1 - (FT1 - 1) * P
OOB = 1 << 20


def ds(start, n):
    return bass.ds(start, n)


def shape_constants():
    pos = np.arange(SEQ, dtype=np.float32)
    half = HD0 // 2
    freq = np.float32(1.0) / np.power(np.float32(10000.0), np.arange(half, dtype=np.float32) / np.float32(half))
    ang = pos[:, None] * freq[None, :].astype(np.float32)
    c, s = np.cos(ang).astype(np.float32), np.sin(ang).astype(np.float32)
    cos0 = np.tile(np.repeat(c.T, 2, axis=0), (HPT, 1))
    sgn = np.tile(np.array([-1.0, 1.0], np.float32), P // 2)[:, None]
    sin0 = np.tile(np.repeat(s.T, 2, axis=0), (HPT, 1)) * sgn
    inv = np.float32(1.0) / np.power(np.float32(10000.0), np.arange(0, HD1, 2, dtype=np.float32) / np.float32(HD1))
    ang1 = pos[:, None] * inv[None, :].astype(np.float32)
    cos1 = np.tile(np.cos(ang1).astype(np.float32).T, (2, 1))
    sin1 = np.tile(np.sin(ang1).astype(np.float32).T, (2, 1))
    h = np.array([[1.0]], np.float32)
    while h.shape[0] < P:
        h = np.block([[h, h], [h, -h]])
    q, k = np.arange(P)[:, None], np.arange(P)[None, :]
    band = np.concatenate([np.where(k > q, 0.0, NEG), np.where(k <= q, 0.0, NEG)], axis=1)
    before = (q < k).astype(np.float32)
    misc = np.concatenate([np.eye(P), h, band, before, np.ones((P, P))], axis=1)
    expert = np.tile(np.arange(E, dtype=np.float32), (P, NT, 1)).reshape(P, NT * E)
    f = np.float32
    return {"rope0": np.ascontiguousarray(np.concatenate([cos0, sin0], axis=1), f),
            "rope1": np.ascontiguousarray(np.concatenate([cos1, sin1], axis=1), f),
            "misc": np.ascontiguousarray(misc, f), "expert": np.ascontiguousarray(expert, f)}


def build(nc, ins, out):
    consts = {k: nc.inline_tensor(v, name="c_" + k) for k, v in shape_constants().items()}
    consts = {k: (v if isinstance(v, bass.AP) else v.ap()) for k, v in consts.items()}
    xe_dram = nc.dram_tensor("xe_dram", [SLOTS, D], F32).ap()
    ye_dram = nc.dram_tensor("ye_dram", [SLOTS, D], F32).ap()

    with ExitStack() as top:
        def sb(ctx, name, shape, dt=F32):
            return ctx.enter_context(nc.sbuf_tensor(name, shape, dt))

        def sem(name):
            return top.enter_context(nc.semaphore(name))

        bank = top.enter_context(nc.psum_tensor("bank", [P, 8, 512], F32))
        X = sb(top, "X", [P, NT, D])
        xnT = sb(top, "xnT", [P, KD, T])
        misc = sb(top, "misc", [P, 6 * P])
        ident, had, band = misc[:, 0:P], misc[:, P:2 * P], misc[:, 2 * P:4 * P]
        before, ones = misc[:, 4 * P:5 * P], misc[:, 5 * P:6 * P]
        env = dict(nc=nc, ins=ins, out=out, sb=sb, sem=sem, bank=bank, X=X, xnT=xnT, ident=ident, had=had,
                   band=band, before=before, ones=ones, consts=consts, misc=misc, xe=xe_dram, ye=ye_dram)
        layer_norm(env, "0", first=True)
        attention0(env)
        feed_forward0(env)
        with ExitStack() as moe:
            r = dict(slot=sb(moe, "slot", [P, NT, TOPK], U32), wk=sb(moe, "wk", [P, NT, TOPK]),
                     gshared=sb(moe, "gshared", [P, NT]), xn=sb(moe, "xn_rows", [P, NT, D]))
            layer_norm(env, "1", rows=r["xn"])
            route(env, r)
            dispatch(env, r)
            attention1(env)
            feed_forward1(env, r)
            experts(env)
            combine(env, r)


def layer_norm(env, tag, first=False, rows=None):
    nc, X, xnT, bank, ident = env["nc"], env["X"], env["xnT"], env["bank"], env["ident"]
    sem = env["sem"]
    x_loaded = sem("ln_x" + tag)
    stats_done, aggr_done, var_done, sd_done, rstd_done = (sem(f"ln_{n}{tag}") for n in
                                                           ("stats", "aggr", "var", "sd", "rstd"))
    xn_ready, xt_ready, xt_taken = (sem(f"ln_{n}{tag}") for n in ("xn", "xt", "taken"))
    QL = 4
    with ExitStack() as ctx:
        stats = env["sb"](ctx, "ln_stats" + tag, [P, NT, 6])
        mv = env["sb"](ctx, "ln_mv" + tag, [P, NT, 2])
        sd = env["sb"](ctx, "ln_sd" + tag, [P, 2, NT])
        xn = rows if rows is not None else env["sb"](ctx, "ln_xn" + tag, [P, 2, D])
        slots = NT if rows is not None else 2
        block = ctx.enter_context(nc.Block())

        if first:
            @block.sync
            def _(sp):
                src = env["ins"]["L0_attn_x"].rearrange("b (n p) d -> p (b n) d", p=P)
                sp.dma_start(env["misc"][:, :], env["consts"]["misc"]).then_inc(x_loaded, 16)
                for c in range(QL):
                    n = NT // QL
                    sp.dma_start(X[:, c * n:(c + 1) * n, :], src[:, c * n:(c + 1) * n, :]).then_inc(x_loaded, 16)
                sp.wait_ge(x_loaded, 16 * (QL + 1))

        @block.vector
        def _(dve):
            if first:
                dve.wait_ge(x_loaded, 16 * (QL + 1))
            for n in range(NT):
                dve.bn_stats(stats[:, n, :], X[:, n, :]).then_inc(stats_done, 1)
            for n in range(NT):
                dve.wait_ge(stats_done, n + 1)
                dve.bn_aggr(mv[:, n, :], stats[:, n, :]).then_inc(aggr_done, 1)
            dve.wait_ge(aggr_done, NT)
            dve.tensor_scalar(sd[:, 0, :], mv[:, :, 1], EPS, None, ALU.add).then_inc(var_done, 1)
            dve.wait_ge(sd_done, 1)
            dve.reciprocal(sd[:, 0, :], sd[:, 1, :]).then_inc(rstd_done, 1)
            dve.wait_ge(rstd_done, 1)
            for n in range(NT):
                if n >= slots:
                    dve.wait_ge(xt_ready, n - slots + 1)
                dve.tensor_scalar(xn[:, n % slots, :], X[:, n, :], mv[:, n, 0:1], sd[:, 0, n:n + 1],
                                  ALU.subtract, ALU.mult).then_inc(xn_ready, 1)

        @block.tensor
        def _(pe):
            if first:
                pe.wait_ge(x_loaded, 16 * (QL + 1))
            for n in range(NT):
                pe.wait_ge(xn_ready, n + 1)
                if n >= 4:
                    pe.wait_ge(xt_taken, n - 3)
                for k in range(KD):
                    mm = pe.transpose(bank[:, n % 4, k * P:(k + 1) * P], xn[:, n % slots, k * P:(k + 1) * P], ident)
                mm.then_inc(xt_ready, 1)

        @block.scalar
        def _(act):
            act.wait_ge(var_done, 1)
            act.activation(sd[:, 1, :], sd[:, 0, :], ACT.Sqrt).then_inc(sd_done, 1)
            for n in range(NT):
                act.wait_ge(xt_ready, n + 1)
                act.activation(xnT[:, :, n * P:(n + 1) * P], bank[:, n % 4, :].rearrange("p (k t) -> p k t", k=KD),
                               ACT.Copy).then_inc(xt_taken, 1)


def attention0(env):
    nc, X, xnT, bank, ident, sem, sb, ins = (env[k] for k in ("nc", "X", "xnT", "bank", "ident", "sem", "sb", "ins"))
    NF = QT0 + 2
    with ExitStack() as ctx:
        qT = sb(ctx, "qT", [P, QT0, T])
        kT = sb(ctx, "kT", [P, T])
        v = sb(ctx, "v", [P, NT, P])
        wo = sb(ctx, "wo", [P, KD, D])
        a0_w = sem("a0_w")
        with ExitStack() as c2:
            w = sb(c2, "wqkv", [P, KD, NF * P])
            rope = sb(c2, "rope0", [P, 2, SEQ])
            swapped = sb(c2, "swapped", [P, 2, CH])
            direct = sb(c2, "direct", [P, 2, CH])
            vT = sb(c2, "vT", [P, CH])
            proj, swap_done, cos_done, sin_done, roped, v_rows, v_taken = (
                sem("a0_" + n) for n in ("proj", "swap", "cos", "sin", "roped", "vrows", "vtaken"))
            PER = 2 * NF
            RO = 2 * (NF - 1)
            block = c2.enter_context(nc.Block())

            @block.sync
            def _(sp):
                kd = dict(p=P)
                sp.dma_start(w[:, :, 0:D], ins["L0_attn_W_q"].rearrange("(k p) n -> p k n", **kd)).then_inc(a0_w, 16)
                sp.dma_start(w[:, :, D:D + P], ins["L0_attn_W_k"].rearrange("(k p) n -> p k n", **kd)).then_inc(a0_w, 16)
                sp.dma_start(w[:, :, D + P:], ins["L0_attn_W_v"].rearrange("(k p) n -> p k n", **kd)).then_inc(a0_w, 16)
                sp.dma_start(rope[:, :, :], env["consts"]["rope0"].rearrange("p (a s) -> p a s", a=2)).then_inc(a0_w, 16)
                sp.dma_start(wo[:, :, :], ins["L0_attn_W_o"].rearrange("(k p) n -> p k n", **kd)).then_inc(a0_w, 16)
                sp.wait_ge(a0_w, 80)

            @block.tensor
            def _(pe):
                pe.wait_ge(a0_w, 80)
                with pe.Fori(0, BATCH) as b:
                    for h in range(2):
                        for f in range(NF):
                            u = h * NF + f
                            pe.wait_ge(cos_done, b * PER + max(u - 3, 0))
                            for k in range(KD):
                                mm = pe.matmul(bank[:, u % 4, :], w[:, k, f * P:(f + 1) * P],
                                               xnT[:, k, ds(b * SEQ + h * CH, CH)], start=(k == 0), stop=(k == KD - 1))
                            mm.then_inc(proj, 1)
                        pe.wait_ge(cos_done, b * PER + (h + 1) * NF)
                        pe.wait_ge(v_taken, b * 2 + h)
                        for s in range(CH // P):
                            mm = pe.transpose(bank[:, 4, s * P:(s + 1) * P], vT[:, s * P:(s + 1) * P], ident)
                        mm.then_inc(v_rows, 1)

            @block.vector
            def _(dve):
                dve.wait_ge(a0_w, 80)
                mask = [i ^ 1 for i in range(32)]
                with dve.Fori(0, BATCH) as b:
                    for h in range(2):
                        for f in range(NF):
                            u, r = h * NF + f, h * (NF - 1) + f
                            dve.wait_ge(proj, b * PER + u + 1)
                            if f == NF - 1:
                                dve.wait_ge(v_rows, b * 2 + h)
                                dve.tensor_copy(vT[:, :], bank[:, u % 4, :]).then_inc(cos_done, 1)
                                continue
                            dst = qT[:, f, ds(b * SEQ + h * CH, CH)] if f < QT0 else kT[:, ds(b * SEQ + h * CH, CH)]
                            dve.tensor_tensor(direct[:, u % 2, :], bank[:, u % 4, :],
                                              rope[:, 0, h * CH:(h + 1) * CH], ALU.mult).then_inc(swap_done, 1)
                            dve.stream_shuffle(swapped[:, u % 2, :], bank[:, u % 4, :], mask).then_inc(cos_done, 1)
                            dve.wait_ge(cos_done, b * PER + u + 1)
                            dve.wait_ge(swap_done, b * RO + r + 1)
                            dve.tensor_tensor(swapped[:, u % 2, :], swapped[:, u % 2, :],
                                              rope[:, 1, h * CH:(h + 1) * CH], ALU.mult).then_inc(sin_done, 1)
                            dve.wait_ge(sin_done, b * RO + r + 1)
                            dve.tensor_tensor(dst, direct[:, u % 2, :], swapped[:, u % 2, :],
                                              ALU.add).then_inc(roped, 1)

            @block.scalar
            def _(act):
                with act.Fori(0, BATCH) as b:
                    for h in range(2):
                        act.wait_ge(v_rows, b * 2 + h + 1)
                        act.activation(v[:, ds(b * QB + h * (CH // P), CH // P), :],
                                       bank[:, 4, :].rearrange("p (s d) -> p s d", d=P), ACT.Copy).then_inc(v_taken, 1)

        attention0_heads(env, ctx, qT, kT, v, wo)


def attention0_heads(env, outer, qT, kT, v, wo):
    nc, X, bank, ident, sem, sb = (env[k] for k in ("nc", "X", "bank", "ident", "sem", "sb"))
    scale = float(HD0) ** -0.5
    names = ("q_staged", "kv_staged", "scores", "max_done", "negmax", "probs", "turned", "pt_a", "pt_b", "pv",
             "recip", "normed", "o_turned", "o_taken", "y", "added")
    S = {n: sem("h0_" + n) for n in names}
    with ExitStack() as ctx:
        qs = sb(ctx, "qs", [P, QT0, P])
        ks = sb(ctx, "ks", [P, SEQ])
        vs = sb(ctx, "vs", [P, QB, P])
        pr = sb(ctx, "pr", [P, 2, SEQ])
        pt = sb(ctx, "pt", [P, 2, QB, P])
        small = sb(ctx, "small0", [P, 4, UN0])
        on = sb(ctx, "on", [P, D])
        oT = sb(ctx, "oT", [P, KD, P])
        for b in range(BATCH):
            with nc.Block() as block:
                def base(i, per):
                    return i * per + b * QB * per

                @block.gpsimd
                def _(pool):
                    pool.tensor_copy(ks[:, :], kT[:, b * SEQ:(b + 1) * SEQ]).then_inc(S["kv_staged"], 1)
                    pool.tensor_copy(vs[:, :, :], v[:, b * QB:(b + 1) * QB, :]).then_inc(S["kv_staged"], 1)
                    with pool.Fori(0, QB) as i:
                        pool.wait_ge(S["scores"], base(i, UN0))
                        pool.tensor_copy(qs[:, :, :], qT[:, :, ds(i * P + b * SEQ, P)]).then_inc(S["q_staged"], 1)

                @block.tensor
                def _(pe):
                    pe.wait_ge(S["kv_staged"], 2 * (b + 1))
                    with pe.Fori(0, QB) as i:
                        pe.wait_ge(S["q_staged"], base(i, 1) + 1)

                        def scores(u):
                            t, j = u // HPT, u % HPT
                            rows = slice(HD0 * j, HD0 * (j + 1))
                            pe.wait_ge(S["probs"], base(i, UN0) + max(u - 1, 0))
                            for h in range(2):
                                mm = pe.matmul(bank[:, 2 * (u % 2) + h, :], qs[rows, t, :],
                                               ks[rows, h * CH:(h + 1) * CH], start=True, stop=True)
                            mm.then_inc(S["scores"], 1)

                        def turn(u):
                            pe.wait_ge(S["probs"], base(i, UN0) + u + 1)
                            for h, s in ((0, "pt_a"), (1, "pt_b")):
                                pe.wait_ge(S[s], base(i, UN0) + u)
                                if u == 0:
                                    pe.wait_ge(S["o_taken" if h == 0 else "added"], base(i, 1))
                                for m in range(4):
                                    kt = 4 * h + m
                                    mm = pe.transpose(bank[:, 4 + h, m * P:(m + 1) * P],
                                                      pr[:, u % 2, kt * P:(kt + 1) * P], ident)
                                mm.then_inc(S["turned"], 1)

                        def weigh(u):
                            j = u % HPT
                            pe.wait_ge(S["normed"], base(i, UN0) + max(u - 1, 0))
                            pe.wait_ge(S["pt_a"], base(i, UN0) + u + 1)
                            pe.wait_ge(S["pt_b"], base(i, UN0) + u + 1)
                            for kt in range(QB):
                                mm = pe.matmul(bank[:, 6 + u % 2, 0:HD0], pt[:, u % 2, kt, :],
                                               vs[:, kt, HD0 * j:HD0 * (j + 1)], start=(kt == 0), stop=(kt == QB - 1))
                            mm.then_inc(S["pv"], 1)

                        for s in range(UN0 + 2):
                            if s < UN0:
                                scores(s)
                            if 1 <= s <= UN0:
                                turn(s - 1)
                            if s >= 2:
                                weigh(s - 2)
                        pe.wait_ge(S["normed"], base(i, UN0) + UN0)
                        for t in range(KD):
                            mm = pe.transpose(bank[:, 4, t * P:(t + 1) * P], on[:, t * P:(t + 1) * P], ident)
                        mm.then_inc(S["o_turned"], 1)
                        pe.wait_ge(S["o_taken"], base(i, 1) + 1)
                        for t in range(KD):
                            mm = pe.matmul(bank[:, 5, :], oT[:, t, :], wo[:, t, :], start=(t == 0), stop=(t == KD - 1))
                        mm.then_inc(S["y"], 1)

                @block.vector
                def _(dve):
                    with dve.Fori(0, QB) as i:
                        def maximum(u):
                            dve.wait_ge(S["scores"], base(i, UN0) + u + 1)
                            if u == 0:
                                dve.wait_ge(S["normed"], base(i, UN0))
                            dve.reduce_max(small[:, 0, u:u + 1],
                                           bank[:, 2 * (u % 2):2 * (u % 2) + 2, :].rearrange("p a s -> p (a s)"),
                                           AX.X).then_inc(S["max_done"], 1)
                            dve.wait_ge(S["max_done"], base(i, UN0) + u + 1)
                            dve.tensor_scalar(small[:, 1, u:u + 1], small[:, 0, u:u + 1], -scale, None,
                                              ALU.mult).then_inc(S["negmax"], 1)

                        def take(u):
                            dve.wait_ge(S["turned"], base(i, 2 * UN0) + 2 * u + 2)
                            dve.wait_ge(S["pv"], base(i, UN0) + max(u - 1, 0))
                            dve.tensor_copy(pt[:, u % 2, 4:8, :],
                                            bank[:, 5, :].rearrange("p (m q) -> p m q", m=4)).then_inc(S["pt_b"], 1)

                        def norm(u):
                            dve.reciprocal(small[:, 3, u:u + 1], small[:, 2, u:u + 1]).then_inc(S["recip"], 1)
                            dve.wait_ge(S["recip"], base(i, UN0) + u + 1)
                            dve.wait_ge(S["pv"], base(i, UN0) + u + 1)
                            if u == 0:
                                dve.wait_ge(S["o_turned"], base(i, 1))
                            dve.tensor_scalar(on[:, HD0 * u:HD0 * (u + 1)], bank[:, 6 + u % 2, 0:HD0],
                                              small[:, 3, u:u + 1], None, ALU.mult).then_inc(S["normed"], 1)

                        for s in range(UN0 + 2):
                            if s < UN0:
                                maximum(s)
                            if 1 <= s <= UN0:
                                take(s - 1)
                            if s >= 2:
                                norm(s - 2)
                        dve.wait_ge(S["y"], base(i, 1) + 1)
                        row = X[:, ds(i + b * QB, 1), :].rearrange("p a d -> p (a d)")
                        dve.tensor_tensor(row, row, bank[:, 5, :], ALU.add).then_inc(S["added"], 1)

                @block.scalar
                def _(act):
                    with act.Fori(0, QB) as i:
                        for s in range(UN0 + 1):
                            if s < UN0:
                                u = s
                                act.wait_ge(S["negmax"], base(i, UN0) + u + 1)
                                act.wait_ge(S["turned"], base(i, 2 * UN0) + 2 * max(u - 1, 0))
                                act.activation(pr[:, u % 2, :],
                                               bank[:, 2 * (u % 2):2 * (u % 2) + 2, :].rearrange("p a s -> p (a s)"),
                                               ACT.Exp, bias=small[:, 1, u:u + 1], scale=scale,
                                               accum_out=small[:, 2, u:u + 1]).then_inc(S["probs"], 1)
                            if s >= 1:
                                u = s - 1
                                act.wait_ge(S["turned"], base(i, 2 * UN0) + 2 * u + 1)
                                act.wait_ge(S["pv"], base(i, UN0) + max(u - 1, 0))
                                act.activation(pt[:, u % 2, 0:4, :], bank[:, 4, :].rearrange("p (m q) -> p m q", m=4),
                                               ACT.Copy).then_inc(S["pt_a"], 1)
                        act.wait_ge(S["o_turned"], base(i, 1) + 1)
                        act.wait_ge(S["y"], base(i, 1))
                        act.activation(oT[:, :, :], bank[:, 4, :].rearrange("p (t q) -> p t q", t=KD),
                                       ACT.Copy).then_inc(S["o_taken"], 1)


def swiglu_chunks(env, tag, block, tiles, wg, wu, wd, hid, sg, ready, ready_value, scale=None, gate=None):
    nc, X, xnT, bank, sem = (env[k] for k in ("nc", "X", "xnT", "bank", "sem"))
    up, sig, gated, hidden, y, added = (sem(f"ff{tag}_{n}") for n in ("up", "sig", "gated", "hidden", "y", "added"))
    SUBS = CH // P

    @block.tensor
    def _(pe):
        pe.wait_ge(ready, ready_value)
        with pe.Fori(0, NC) as c:
            def down(h):
                pe.wait_ge(hidden, c * tiles + h + 1)
                if h == 0:
                    pe.wait_ge(added, c * SUBS)
                for s in range(SUBS):
                    mm = pe.matmul(bank[:, 4 + s, :], hid[:, h % 2, s * P:(s + 1) * P], wd[:, h, :],
                                   start=(h == 0), stop=(h == tiles - 1))
                mm.then_inc(y, 1)
            for h in range(tiles):
                pe.wait_ge(hidden, c * tiles + max(h - 1, 0))
                for a, w in ((0, wg), (1, wu)):
                    for k in range(KD):
                        mm = pe.matmul(bank[:, 2 * (h % 2) + a, :], w[:, k, h * P:(h + 1) * P],
                                       xnT[:, k, ds(c * CH, CH)], start=(k == 0), stop=(k == KD - 1))
                mm.then_inc(up, 1)
                if h >= 1:
                    down(h - 1)
            down(tiles - 1)

    @block.scalar
    def _(act):
        with act.Fori(0, NC) as c:
            for h in range(tiles):
                act.wait_ge(up, c * tiles + h + 1)
                act.wait_ge(gated, c * tiles + max(h - 1, 0))
                act.activation(sg[:, h % 2, :], bank[:, 2 * (h % 2), :], ACT.Sigmoid).then_inc(sig, 1)

    @block.vector
    def _(dve):
        with dve.Fori(0, NC) as c:
            for h in range(tiles):
                dve.wait_ge(sig, c * tiles + h + 1)
                dve.wait_ge(y, c * tiles + max(h - 1, 0))
                dve.tensor_tensor(hid[:, h % 2, :], bank[:, 2 * (h % 2), :], sg[:, h % 2, :],
                                  ALU.mult).then_inc(gated, 1)
                dve.wait_ge(gated, c * tiles + h + 1)
                dve.tensor_tensor(hid[:, h % 2, :], bank[:, 2 * (h % 2) + 1, :], hid[:, h % 2, :],
                                  ALU.mult).then_inc(hidden, 1)
            dve.wait_ge(y, c * tiles + tiles)
            for s in range(SUBS):
                row = X[:, ds(c * SUBS + s, 1), :].rearrange("p a d -> p (a d)")
                factor = scale if gate is None else gate[:, ds(c * SUBS + s, 1)]
                dve.scalar_tensor_tensor(out=row, in0=bank[:, 4 + s, :], scalar=factor, in1=row,
                                         op0=ALU.mult, op1=ALU.add).then_inc(added, 1)


def feed_forward0(env):
    nc, bank, had, sem, sb, ins = (env[k] for k in ("nc", "bank", "had", "sem", "sb", "ins"))
    HT = F0 // P
    CW = 128
    with ExitStack() as ctx:
        w1 = sb(ctx, "w1", [P, KD, F0])
        w3 = sb(ctx, "w3", [P, KD, F0])
        w2 = sb(ctx, "w2", [P, HT, D])
        loaded, raw, flat, bf = (sem("f0_" + n) for n in ("loaded", "raw", "flat", "bf"))
        with ExitStack() as c2:
            ping = sb(c2, "ping", [P, HT, CW])
            pong = sb(c2, "pong", [P, HT, CW])
            with nc.Block() as block:
                @block.sync
                def _(sp):
                    sp.dma_start(w2[:, :, :], ins["L0_ffn_W2"].rearrange("(h p) d -> p h d", p=P)).then_inc(loaded, 16)
                    sp.dma_start(w1[:, :, :], ins["L0_ffn_W1"].rearrange("(k p) h -> p k h", p=P)).then_inc(loaded, 16)
                    sp.dma_start(w3[:, :, :], ins["L0_ffn_W3"].rearrange("(k p) h -> p k h", p=P)).then_inc(loaded, 16)
                    sp.wait_ge(loaded, 48)

                @block.tensor
                def _(pe):
                    pe.wait_ge(loaded, 48)
                    for c in range(D // CW):
                        if c:
                            pe.wait_ge(flat, 4 * c)
                        for q in range(4):
                            mm = pe.matmul(bank[:, q, :], had, w2[:, 4 * q:4 * q + 4, c * CW:(c + 1) * CW],
                                           start=True, stop=True)
                            mm.then_inc(raw, 1)

                @block.scalar
                def _(act):
                    for c in range(D // CW):
                        if c:
                            act.wait_ge(bf, 8 * c)
                        for q in range(4):
                            act.wait_ge(raw, 4 * c + q + 1)
                            act.activation(ping[:, 4 * q:4 * q + 4, :],
                                           bank[:, q, :].rearrange("p (a n) -> p a n", n=CW),
                                           ACT.Copy).then_inc(flat, 1)

                @block.vector
                def _(dve):
                    for c in range(D // CW):
                        dve.wait_ge(flat, 4 * (c + 1))
                        bufs = [ping[:, :, :], pong[:, :, :], ping[:, :, :], pong[:, :, :],
                                w2[:, :, c * CW:(c + 1) * CW]]
                        for st in range(4):
                            h = 1 << st
                            src = bufs[st].rearrange("p (g two h) n -> p g two h n", two=2, h=h)
                            dst = bufs[st + 1].rearrange("p (g two h) n -> p g two h n", two=2, h=h)
                            if st:
                                dve.wait_ge(bf, 8 * c + 2 * st)
                            for j, op in ((0, ALU.add), (1, ALU.subtract)):
                                if h in (1, 8):
                                    a = 0 if h == 8 else slice(None)
                                    z = slice(None) if h == 8 else 0
                                    i0, i1, o = src[:, a, 0, z, :], src[:, a, 1, z, :], dst[:, a, j, z, :]
                                else:
                                    i0, i1, o = src[:, :, 0], src[:, :, 1], dst[:, :, j]
                                dve.tensor_tensor(o, i0, i1, op).then_inc(bf, 1)
        with ExitStack() as c3:
            hid = sb(c3, "hid0", [P, 2, CH])
            sg = sb(c3, "sg0", [P, 2, CH])
            with nc.Block() as block:
                swiglu_chunks(env, "0", block, HT, w1, w3, w2, hid, sg, loaded, 48, scale=float(F0) ** -0.5)


def route(env, r):
    nc, xnT, bank, ident, sem, sb, ins = (env[k] for k in ("nc", "xnT", "bank", "ident", "sem", "sb", "ins"))
    W = E + 1
    loaded, lgT, lgT_s, lg, lg_s, cnt, chain, ex = (sem("r_" + n) for n in
                                                    ("loaded", "lgT", "lgTs", "lg", "lgs", "cnt", "chain", "exp"))
    with ExitStack() as ctx:
        wr = sb(ctx, "wr", [P, KD, W])
        logT = sb(ctx, "logT", [W, T])
        log = sb(ctx, "log", [P, NT, W])
        iota = sb(ctx, "iota", [P, NT, E])
        top = sb(ctx, "top", [P, NT, 8])
        topi = sb(ctx, "topi", [P, NT, 8], U32)
        topf = sb(ctx, "topf", [P, NT, 8])
        hot = sb(ctx, "hot", [P, TOPK, NT, E])
        mask = sb(ctx, "mask", [P, NT, E])
        slotv = sb(ctx, "slotv", [P, NT, E])
        base = sb(ctx, "base", [P, NT, E])
        tmp = sb(ctx, "tmp", [P, NT, E])
        exps = sb(ctx, "exps", [P, NT, TOPK])
        sums = sb(ctx, "sums", [P, 2, NT])
        slotf = sb(ctx, "slotf", [P, NT, TOPK])
        ok = sb(ctx, "ok", [P, NT, TOPK])
        with nc.Block() as block:
            @block.sync
            def _(sp):
                sp.dma_start(wr[:, :, 0:E], ins["L1_ffn_Wr"].rearrange("(k p) n -> p k n", p=P)).then_inc(loaded, 16)
                sp.dma_start(wr[:, :, E:W], ins["L1_ffn_Wse"].rearrange("(k p) n -> p k n", p=P),
                             allow_slow_non_contiguous=True).then_inc(loaded, 16)
                sp.dma_start(iota[:, :, :], env["consts"]["expert"].rearrange("p (n e) -> p n e", e=E)).then_inc(loaded, 16)
                sp.wait_ge(loaded, 48)

            @block.tensor
            def _(pe):
                pe.wait_ge(loaded, 48)
                for c in range(NC):
                    for k in range(KD):
                        mm = pe.matmul(bank[0:W, c, :], wr[:, k, :], xnT[:, k, c * CH:(c + 1) * CH],
                                       start=(k == 0), stop=(k == KD - 1))
                    mm.then_inc(lgT, 1)
                for c in range(NC):
                    pe.wait_ge(lgT_s, c + 1)
                    for s in range(CH // P):
                        n = c * (CH // P) + s
                        mm = pe.transpose(bank[:, 4 + c // 2, (n % 8) * W:(n % 8 + 1) * W],
                                          logT[:, n * P:(n + 1) * P], ident[0:W, 0:W])
                    mm.then_inc(lg, 1)
                pe.wait_ge(cnt, 1)
                pe.matmul(bank[:, 6, :], env["before"], mask[:, :, :], start=True, stop=True).then_inc(lg, 1)
                pe.matmul(bank[:, 7, :], env["ones"], mask[:, :, :], start=True, stop=True).then_inc(lg, 1)

            @block.scalar
            def _(act):
                for c in range(NC):
                    act.wait_ge(lgT, c + 1)
                    act.activation(logT[:, c * CH:(c + 1) * CH], bank[0:W, c, :], ACT.Copy).then_inc(lgT_s, 1)
                for g in range(2):
                    act.wait_ge(lg, 2 * (g + 1))
                    act.activation(log[:, 8 * g:8 * g + 8, :],
                                   bank[:, 4 + g, 0:8 * W].rearrange("p (n e) -> p n e", e=W),
                                   ACT.Copy).then_inc(lg_s, 1)
                act.wait_ge(ex, 1)
                act.activation(exps[:, :, :], slotf[:, :, :], ACT.Exp).then_inc(lg_s, 1)
                act.wait_ge(lg_s, 3)
                act.activation(r["gshared"][:, :], log[:, :, E], ACT.Sigmoid).then_inc(lg_s, 1)

            @block.vector
            def _(dve):
                steps = [0]

                def step(instruction):
                    steps[0] += 1
                    instruction.then_inc(chain, 1)
                    dve.wait_ge(chain, steps[0])
                dve.wait_ge(loaded, 48)
                dve.wait_ge(lg_s, 2)
                for n in range(NT):
                    ins_ = dve.max(top[:, n, :], log[:, n, 0:E])
                step(ins_)
                for n in range(NT):
                    ins_ = dve.max_index(topi[:, n, :], top[:, n, :], log[:, n, 0:E])
                step(ins_)
                step(dve.tensor_copy(topf[:, :, :], topi[:, :, :]))
                step(dve.tensor_tensor(slotf[:, :, :], top[:, :, 0:TOPK],
                                       top[:, :, 0:1].to_broadcast([P, NT, TOPK]), ALU.subtract))
                dve.sem_inc(ex, 1)
                for k in range(TOPK):
                    step(dve.tensor_tensor(hot[:, k], iota[:, :, :], topf[:, :, k:k + 1].to_broadcast([P, NT, E]),
                                           ALU.is_equal))
                step(dve.tensor_tensor(mask[:, :, :], hot[:, 0], hot[:, 1], ALU.add))
                step(dve.tensor_tensor(mask[:, :, :], mask[:, :, :], hot[:, 2], ALU.add))
                step(dve.tensor_tensor(mask[:, :, :], mask[:, :, :], hot[:, 3], ALU.add))
                dve.sem_inc(cnt, 1)
                dve.wait_ge(lg, NC + 2)
                step(dve.memset(base[:, 0, :], 0.0))
                for n in range(1, NT):
                    step(dve.tensor_tensor(base[:, n, :], bank[:, 7, (n - 1) * E:n * E], base[:, n - 1, :], ALU.add))
                step(dve.tensor_tensor(base[:, :, :], bank[:, 6, :].rearrange("p (n e) -> p n e", e=E),
                                       base[:, :, :], ALU.add))
                step(dve.tensor_scalar(tmp[:, :, :], base[:, :, :], float(CAP), float(OOB), ALU.is_ge, ALU.mult))
                step(dve.tensor_tensor(tmp[:, :, :], tmp[:, :, :], base[:, :, :], ALU.add))
                step(dve.scalar_tensor_tensor(out=slotv[:, :, :], in0=iota[:, :, :], scalar=float(CAP),
                                              in1=tmp[:, :, :], op0=ALU.mult, op1=ALU.add))
                dve.wait_ge(lg_s, 3)
                for k in range(TOPK):
                    step(dve.tensor_tensor(tmp[:, :, :], hot[:, k], slotv[:, :, :], ALU.mult))
                    step(dve.tensor_reduce(slotf[:, :, k], tmp[:, :, :], AX.X, ALU.add))
                step(dve.tensor_copy(r["slot"][:, :, :], slotf[:, :, :]))
                step(dve.tensor_scalar(ok[:, :, :], slotf[:, :, :], float(SLOTS), None, ALU.is_lt))
                step(dve.tensor_reduce(sums[:, 0, :], exps[:, :, :], AX.X, ALU.add))
                step(dve.reciprocal(sums[:, 1, :], sums[:, 0, :]))
                step(dve.tensor_tensor(ok[:, :, :], ok[:, :, :], exps[:, :, :], ALU.mult))
                for k in range(TOPK):
                    step(dve.tensor_tensor(r["wk"][:, :, k], ok[:, :, k], sums[:, 1, :], ALU.mult))


def dispatch(env, r):
    nc, sem, sb = (env[k] for k in ("nc", "sem", "sb"))
    zeroed, sent, z = sem("d_zeroed"), sem("d_sent"), sem("d_z")
    env["sent"] = sent
    with ExitStack() as ctx:
        zero = sb(ctx, "zero", [P, D])
        with nc.Block() as block:
            @block.gpsimd
            def _(pool):
                pool.memset(zero[:, :], 0.0).then_inc(z, 1)
                pool.wait_ge(zeroed, 16 * SLOTS // P)
                for n in range(NT):
                    for k in range(TOPK):
                        pool.indirect_dma_start(env["xe"], bass.IndirectOffsetOnAxis(ap=r["slot"][:, n, k:k + 1], axis=0),
                                                r["xn"][:, n, :], None, bounds_check=SLOTS - 1,
                                                oob_is_err=False).then_inc(sent, 16)
                pool.wait_ge(sent, 16 * NT * TOPK)

            @block.sync
            def _(sp):
                sp.wait_ge(z, 1)
                for m in range(SLOTS // P):
                    sp.dma_start(env["xe"][m * P:(m + 1) * P, :], zero[:, :]).then_inc(zeroed, 16)
                sp.wait_ge(zeroed, 16 * SLOTS // P)


def attention1(env):
    nc, X, xnT, bank, ident, band, sem, sb, ins = (env[k] for k in ("nc", "X", "xnT", "bank", "ident", "band", "sem",
                                                                    "sb", "ins"))
    PAIRS = H1 // 4
    scale = float(SUB) ** -0.5
    UN = 2 * NT
    names = ("w", "kvw", "proj", "cos", "sin", "roped", "qproj", "scores", "masked", "negmax", "exps", "recip2", "coef", "cleared",
             "mixed", "den", "recipd", "relu", "probs", "turned", "pt", "pv", "ot", "y", "added", "vrows", "vtaken", "lam", "qdone")
    S = {n: sem("h1_" + n) for n in names}
    with ExitStack() as ctx:
        wq = sb(ctx, "wq1", [P, KD, 2 * P])
        wo = sb(ctx, "wo1", [P, 2, D])
        wk = sb(ctx, "wk1", [P, KD, 2 * P])
        q = sb(ctx, "q1", [P, 2, T])
        k_ = sb(ctx, "k1", [P, 2, T])
        v = sb(ctx, "v1", [P, NT, 2 * P])
        rope = sb(ctx, "rope1", [P, 2, SEQ])
        lam = sb(ctx, "lam", [P, H1])
        tr = sb(ctx, "tr", [P, 4, CH])
        ms = sb(ctx, "ms", [P, 4, 2, 2 * P])
        mix = sb(ctx, "mix", [P, 4, 2 * P])
        pt = sb(ctx, "pt1", [P, 2, 2 * P])
        oT = sb(ctx, "oT1", [P, 2, 2, P])
        sm = sb(ctx, "sm1", [P, 4, 12])
        wv = wk

        with nc.Block() as block:
            @block.sync
            def _(sp):
                sp.dma_start(rope[:, :, :], env["consts"]["rope1"].rearrange("p (a s) -> p a s", a=2)).then_inc(S["lam"], 16)
                sp.dma_start(lam[:, :], ins["L1_attn_lam"].partition_broadcast(P)).then_inc(S["lam"], 16)
                sp.wait_ge(S["lam"], 32)

            @block.vector
            def _(dve):
                dve.wait_ge(S["lam"], 32)
                dve.tensor_scalar(lam[:, :], lam[:, :], -1.0, None, ALU.mult).then_inc(S["lam"], 1)
                dve.wait_ge(S["lam"], 33)

        for g in range(2):
            for part in range(2):
                src = ins["L1_attn_Wk" if part == 0 else "L1_attn_Wv"]
                with nc.Block() as block:
                    n0 = (2 * g + part)
                    project_rope(env, block, S, "k" if part == 0 else "v", n0, g,
                                 src.rearrange("(k p) n -> p k n", p=P)[:, :, 2 * P * g:2 * P * (g + 1)],
                                 wk, k_, v, rope, tr)
            with nc.Block() as block:
                attention1_pairs(env, block, S, g, PAIRS, UN, scale, wq, wo, q, k_, v, rope, lam, tr, ms, mix, pt,
                                 oT, sm)


def project_rope(env, block, S, kind, n0, g, src, wk, k_, v, rope, tr):
    nc, xnT, bank, ident = (env[k] for k in ("nc", "xnT", "bank", "ident"))
    rounds = NC * g

    @block.sync
    def _(sp):
        sp.dma_start(wk[:, :, :], src).then_inc(S["kvw"], 16)
        sp.wait_ge(S["kvw"], 16 * (n0 + 1))

    @block.tensor
    def _(pe):
        pe.wait_ge(S["kvw"], 16 * (n0 + 1))
        for c in range(NC):
            if c >= 2 or n0:
                pe.wait_ge(S["qdone"], n0 * NC + max(c - 1, 0))
            for a in range(2):
                for k in range(KD):
                    mm = pe.matmul(bank[:, 2 * (c % 2) + a, :], wk[:, k, a * P:(a + 1) * P],
                                   xnT[:, k, c * CH:(c + 1) * CH], start=(k == 0), stop=(k == KD - 1))
            mm.then_inc(S["proj"], 1)
            if kind == "v":
                pe.wait_ge(S["qdone"], n0 * NC + c + 1)
                if c or g:
                    pe.wait_ge(S["vtaken"], rounds + c)
                for s in range(CH // P):
                    for a in range(2):
                        mm = pe.transpose(bank[:, 4 + s // 2, (s % 2) * 2 * P + a * P:(s % 2) * 2 * P + (a + 1) * P],
                                          tr[:, a, s * P:(s + 1) * P], ident)
                mm.then_inc(S["vrows"], 1)

    @block.vector
    def _(dve):
        for c in range(NC):
            dve.wait_ge(S["proj"], n0 * NC + c + 1)
            if c or n0:
                dve.wait_ge(S["qdone"], n0 * NC + c)
            if kind == "v":
                if c or g:
                    dve.wait_ge(S["vrows"], rounds + c)
                dve.tensor_copy(tr[:, 0:2, :], bank[:, 2 * (c % 2):2 * (c % 2) + 2, :]).then_inc(S["qdone"], 1)
            else:
                rotate(dve, S, bank[:, 2 * (c % 2), :], bank[:, 2 * (c % 2) + 1, :],
                       k_[:, 0, c * CH:(c + 1) * CH], k_[:, 1, c * CH:(c + 1) * CH],
                       rope[:, 0, (c % 2) * CH:(c % 2 + 1) * CH], rope[:, 1, (c % 2) * CH:(c % 2 + 1) * CH], tr,
                       (rounds + c) * 2, lambda n: n)

    if kind == "v":
        @block.scalar
        def _(act):
            for c in range(NC):
                act.wait_ge(S["vrows"], rounds + c + 1)
                act.activation(v[:, c * 4:(c + 1) * 4, :],
                               bank[:, 4:6, :].rearrange("p a (s n) -> p (a s) n", n=2 * P),
                               ACT.Copy).then_inc(S["vtaken"], 1)


def rotate(dve, S, first, second, out1, out2, cos, sin, tr, done, at, names=("cos", "qdone")):
    pa, pc = names
    dve.tensor_tensor(tr[:, 0, :], first, cos, ALU.mult)
    dve.tensor_tensor(tr[:, 1, :], second, sin, ALU.mult).then_inc(S[pa], 1)
    dve.tensor_tensor(tr[:, 2, :], second, cos, ALU.mult)
    dve.tensor_tensor(tr[:, 3, :], first, sin, ALU.mult).then_inc(S[pa], 1)
    dve.wait_ge(S[pa], at(done + 1))
    dve.tensor_tensor(out1, tr[:, 0, :], tr[:, 1, :], ALU.subtract)
    dve.wait_ge(S[pa], at(done + 2))
    dve.tensor_tensor(out2, tr[:, 2, :], tr[:, 3, :], ALU.add).then_inc(S[pc], 1)


def attention1_pairs(env, block, S, g, PAIRS, UN, scale, wq, wo, q, k_, v, rope, lam, tr, ms, mix, pt, oT, sm):
    nc, X, xnT, bank, ident, band, sem, ins = (env[k] for k in ("nc", "X", "xnT", "bank", "ident", "band", "sem",
                                                                "ins"))

    def base(i, per):
        return i * per + g * PAIRS * per

    def keys(n):
        return (n, 1) if n % QB == 0 else (n - 1, 2)

    @block.sync
    def _(sp):
        wq_v = ins["L1_attn_Wq"].rearrange("(k p) n -> p k n", p=P)
        wo_v = ins["L1_attn_Wo"].rearrange("(h p) n -> p h n", p=P)
        with sp.Fori(0, PAIRS) as i:
            col = sp.snap(i * 2 * P + g * PAIRS * 2 * P)
            head = sp.snap(i * 2 + g * PAIRS * 2)
            sp.wait_ge(S["y"], base(i, NT))
            sp.dma_start(wq[:, :, :], wq_v[:, :, ds(col, 2 * P)]).then_inc(S["w"], 16)
            sp.dma_start(wo[:, :, :], wo_v[:, ds(head, 2), :]).then_inc(S["w"], 16)
        sp.wait_ge(S["w"], 32 * PAIRS * (g + 1))

    @block.tensor
    def _(pe):
        with pe.Fori(0, PAIRS) as i:
            pe.wait_ge(S["w"], base(i, 32) + 32)
            for c in range(NC):
                pe.wait_ge(S["roped"], base(i, NC) + max(c - 1, 0))
                for a in range(2):
                    for k in range(KD):
                        mm = pe.matmul(bank[:, 2 * (c % 2) + a, :], wq[:, k, a * P:(a + 1) * P],
                                       xnT[:, k, c * CH:(c + 1) * CH], start=(k == 0), stop=(k == KD - 1))
                mm.then_inc(S["qproj"], 1)

            def scores(u):
                n, h = u // 2, u % 2
                k0, kn = keys(n)
                rows = slice(SUB * h, SUB * (h + 1))
                if u % 8 == 0:
                    pe.wait_ge(S["roped"], base(i, NC) + n // 4 + 1)
                if u < 2:
                    pe.wait_ge(S["roped"], base(i, NC) + NC)
                pe.wait_ge(S["masked"], base(i, UN) + max(u - 1, 0))
                for a in range(2):
                    mm = pe.matmul(bank[:, u % 2, a * 2 * P:a * 2 * P + kn * P], q[rows, a, n * P:(n + 1) * P],
                                   k_[rows, a, k0 * P:(k0 + kn) * P], start=True, stop=True)
                mm.then_inc(S["scores"], 1)

            def turn(u):
                kn = keys(u // 2)[1]
                pe.wait_ge(S["probs"], base(i, UN) + u + 1)
                pe.wait_ge(S["pt"], base(i, UN) + max(u - 1, 0))
                for m in range(kn):
                    mm = pe.transpose(bank[:, 2 + u % 2, m * P:(m + 1) * P], mix[:, u % 4, m * P:(m + 1) * P], ident)
                mm.then_inc(S["turned"], 1)

            def weigh(u):
                n, h = u // 2, u % 2
                k0, kn = keys(n)
                pe.wait_ge(S["pt"], base(i, UN) + u + 1)
                pe.wait_ge(S["ot"], base(i, UN) + max(u - 1, 0))
                for m in range(kn):
                    mm = pe.matmul(bank[:, 4 + u % 2, 0:P], v[:, k0 + m, h * P:(h + 1) * P],
                                   pt[:, u % 2, m * P:(m + 1) * P], start=(m == 0), stop=(m == kn - 1))
                mm.then_inc(S["pv"], 1)

            def project(n):
                pe.wait_ge(S["ot"], base(i, UN) + 2 * n + 2)
                pe.wait_ge(S["added"], base(i, NT) + max(n - 1, 0))
                for h in range(2):
                    mm = pe.matmul(bank[:, 6 + n % 2, :], oT[:, n % 2, h, :], wo[:, h, :], start=(h == 0), stop=(h == 1))
                mm.then_inc(S["y"], 1)

            for s in range(UN + 6):
                if s < UN:
                    scores(s)
                if 3 <= s < UN + 3:
                    turn(s - 3)
                if 4 <= s < UN + 4:
                    weigh(s - 4)
                if s >= 7 and s % 2 == 1:
                    project((s - 7) // 2)

    @block.vector
    def _(dve):
        with dve.Fori(0, PAIRS) as i:
            for c in range(NC):
                dve.wait_ge(S["qproj"], base(i, NC) + c + 1)
                if c == 0:
                    dve.wait_ge(S["scores"], base(i, UN))
                dve.wait_ge(S["roped"], base(i, NC) + c)
                rotate(dve, S, bank[:, 2 * (c % 2), :], bank[:, 2 * (c % 2) + 1, :],
                       q[:, 0, c * CH:(c + 1) * CH], q[:, 1, c * CH:(c + 1) * CH],
                       rope[:, 0, (c % 2) * CH:(c % 2 + 1) * CH], rope[:, 1, (c % 2) * CH:(c % 2 + 1) * CH], tr,
                       2 * c, lambda n: base(i, 2 * NC) + n, names=("sin", "roped"))

            def mask(u):
                kn = keys(u // 2)[1]
                w = kn * P
                dve.wait_ge(S["mixed"], base(i, UN) + max(u - 3, 0))
                dve.wait_ge(S["scores"], base(i, UN) + u + 1)
                dve.memset(sm[:, u % 4, 11:12], 0.0).then_inc(S["cleared"], 1)
                for a in range(2):
                    m = dve.tensor_tensor_reduce(ms[:, u % 4, a, 0:w], bank[:, u % 2, a * 2 * P:a * 2 * P + w],
                                                 band[:, 2 * P - w:2 * P], scale, -3e38, ALU.add, ALU.max,
                                                 sm[:, u % 4, a:a + 1])
                m.then_inc(S["masked"], 1)
                dve.wait_ge(S["masked"], base(i, UN) + u + 1)
                dve.tensor_scalar(sm[:, u % 4, 2:4], sm[:, u % 4, 0:2], -1.0, None, ALU.mult).then_inc(S["negmax"], 1)

            def combine(u):
                n, h = u // 2, u % 2
                w = keys(n)[1] * P
                b = sm[:, u % 4, :]
                dve.wait_ge(S["exps"], base(i, UN) + u + 1)
                dve.reciprocal(b[:, 6:7], b[:, 5:6]).then_inc(S["recip2"], 1)
                dve.wait_ge(S["recip2"], base(i, UN) + u + 1)
                dve.scalar_tensor_tensor(out=b[:, 7:8], in0=b[:, 4:5], scalar=b[:, 6:7],
                                         in1=nlam(i, h), op0=ALU.mult, op1=ALU.mult).then_inc(S["coef"], 1)
                dve.wait_ge(S["coef"], base(i, UN) + u + 1)
                dve.wait_ge(S["turned"], base(i, UN) + max(u - 3, 0))
                dve.scalar_tensor_tensor(out=mix[:, u % 4, 0:w], in0=ms[:, u % 4, 1, 0:w], scalar=b[:, 7:8],
                                         in1=ms[:, u % 4, 0, 0:w], op0=ALU.mult, op1=ALU.add).then_inc(S["mixed"], 1)

            def normalise(u):
                w = keys(u // 2)[1] * P
                b = sm[:, u % 4, :]
                dve.wait_ge(S["relu"], base(i, UN) + u + 1)
                dve.scalar_tensor_tensor(out=b[:, 9:10], in0=b[:, 4:5], scalar=1e-6, in1=b[:, 8:9],
                                         op0=ALU.mult, op1=ALU.add).then_inc(S["den"], 1)
                dve.wait_ge(S["den"], base(i, UN) + u + 1)
                dve.reciprocal(b[:, 10:11], b[:, 9:10]).then_inc(S["recipd"], 1)
                dve.wait_ge(S["recipd"], base(i, UN) + u + 1)
                dve.tensor_scalar(mix[:, u % 4, 0:w], mix[:, u % 4, 0:w], b[:, 10:11], None,
                                  ALU.mult).then_inc(S["probs"], 1)

            def take(u):
                w = keys(u // 2)[1] * P
                dve.wait_ge(S["turned"], base(i, UN) + u + 1)
                dve.wait_ge(S["pv"], base(i, UN) + max(u - 1, 0))
                dve.tensor_copy(pt[:, u % 2, 0:w], bank[:, 2 + u % 2, 0:w]).then_inc(S["pt"], 1)

            def add(n):
                dve.wait_ge(S["y"], base(i, NT) + n + 1)
                dve.tensor_tensor(X[:, n, :], X[:, n, :], bank[:, 6 + n % 2, :], ALU.add).then_inc(S["added"], 1)

            def nlam(i, h):
                return lam[:, ds(i + (2 * g * PAIRS + h * PAIRS), 1)]

            for s in range(UN + 7):
                if s < UN:
                    mask(s)
                if 1 <= s <= UN:
                    combine(s - 1)
                if 2 <= s < UN + 2:
                    normalise(s - 2)
                if 3 <= s < UN + 3:
                    take(s - 3)
                if s >= 8 and s % 2 == 0:
                    add((s - 8) // 2)

    @block.scalar
    def _(act):
        with act.Fori(0, PAIRS) as i:
            for s in range(UN + 5):
                if s < UN:
                    u = s
                    w = keys(u // 2)[1] * P
                    act.wait_ge(S["negmax"], base(i, UN) + u + 1)
                    for a in range(2):
                        ex = act.activation(ms[:, u % 4, a, 0:w], ms[:, u % 4, a, 0:w], ACT.Exp,
                                            bias=sm[:, u % 4, 2 + a:3 + a], accum_out=sm[:, u % 4, 4 + a:5 + a])
                    ex.then_inc(S["exps"], 1)
                if 1 <= s <= UN:
                    u = s - 1
                    w = keys(u // 2)[1] * P
                    act.wait_ge(S["mixed"], base(i, UN) + u + 1)
                    act.activation(mix[:, u % 4, 0:w], mix[:, u % 4, 0:w], ACT.Relu,
                                   accum_out=sm[:, u % 4, 8:9]).then_inc(S["relu"], 1)
                if s >= 5:
                    u = s - 5
                    n, h = u // 2, u % 2
                    act.wait_ge(S["pv"], base(i, UN) + u + 1)
                    act.wait_ge(S["y"], base(i, NT) + max(n - 1, 0))
                    act.activation(oT[:, n % 2, h, :], bank[:, 4 + u % 2, 0:P], ACT.Copy).then_inc(S["ot"], 1)


def feed_forward1(env, r):
    nc, sem, sb, ins = (env[k] for k in ("nc", "sem", "sb", "ins"))
    HT = FS // P
    with ExitStack() as ctx:
        loaded = sem("f1_loaded")
        wg = sb(ctx, "wsg", [P, KD, FS])
        wu = sb(ctx, "wsu", [P, KD, FS])
        wd = sb(ctx, "wsd", [P, HT, D])
        hid = sb(ctx, "hid1", [P, 2, CH])
        sg = sb(ctx, "sg1", [P, 2, CH])
        with nc.Block() as block:
            @block.sync
            def _(sp):
                sp.dma_start(wg[:, :, :], ins["L1_ffn_Wsg"].rearrange("(k p) h -> p k h", p=P)).then_inc(loaded, 16)
                sp.dma_start(wu[:, :, :], ins["L1_ffn_Wsu"].rearrange("(k p) h -> p k h", p=P)).then_inc(loaded, 16)
                sp.dma_start(wd[:, :, :], ins["L1_ffn_Wsd"].rearrange("(h p) d -> p h d", p=P)).then_inc(loaded, 16)
                sp.wait_ge(loaded, 48)
            swiglu_chunks(env, "1", block, HT, wg, wu, wd, hid, sg, loaded, 48, gate=r["gshared"])


def experts(env):
    nc, bank, ident, sem, sb, ins = (env[k] for k in ("nc", "bank", "ident", "sem", "sb", "ins"))
    FP = FT1 * P
    names = ("wloaded0", "wloaded1", "xloaded", "xt", "xt_s", "up", "sig", "gated", "hidden", "y", "y_s", "stored",
             "zeroed")
    S = {n: sem("e_" + n) for n in names}
    with ExitStack() as ctx:
        wg = sb(ctx, "ewg", [P, 2, KD, FP])
        wu = sb(ctx, "ewu", [P, 2, KD, FP])
        wd = sb(ctx, "ewd", [P, 2, FT1, D])
        xr = sb(ctx, "exr", [P, D])
        xT = sb(ctx, "exT", [P, KD, P])
        sg = sb(ctx, "esg", [P, 2, FT1, CAP])
        hT = sb(ctx, "ehT", [P, 2, FT1, CAP])
        ys = sb(ctx, "eys", [CAP, 2, D])
        with nc.Block() as block:
            @block.gpsimd
            def _(pool):
                pool.memset(wg[:, :, :, F1:], 0.0).then_inc(S["zeroed"], 1)
                pool.memset(wu[:, :, :, F1:], 0.0).then_inc(S["zeroed"], 1)
                pool.wait_ge(S["zeroed"], 2)
                pool.memset(wd[F1R:, :, FT1 - 1, :], 0.0).then_inc(S["zeroed"], 1)

            @block.sync
            def _(sp):
                with sp.Fori(0, E // 2) as i:
                    sp.wait_ge(S["xt"], i)
                    sp.wait_ge(env["sent"], 16 * NT * TOPK)
                    sp.dma_start(xr[:, :], env["xe"][ds(i * P, P), :]).then_inc(S["xloaded"], 16)
                    for j in range(2):
                        s = S[f"wloaded{j}"]
                        sp.wait_ge(S["y"], i * 2)
                        sp.wait_ge(env["sent"], 16 * NT * TOPK)
                        for dst, src in ((wg, ins["L1_ffn_Wg"]), (wu, ins["L1_ffn_Wu"])):
                            sp.dma_start(dst[:, j, :, 0:F1], src[ds(i * 2 + j, 1), :, :].rearrange(
                                "a (k p) f -> p (a k) f", p=P)).then_inc(s, 16)
                        down = ins["L1_ffn_Wd"][ds(i * 2 + j, 1), :, :]
                        full = (FT1 - 1) * P
                        sp.dma_start(wd[:, j, 0:FT1 - 1, :], down[:, 0:full, :].rearrange(
                            "a (t p) d -> p (a t) d", p=P)).then_inc(s, 16)
                        sp.dma_start(wd[0:F1R, j, FT1 - 1, :], down[:, full:F1, :].rearrange(
                            "a p d -> p (a d)")).then_inc(s, 16)

            @block.tensor
            def _(pe):
                pe.wait_ge(S["zeroed"], 3)
                with pe.Fori(0, E // 2) as i:
                    pe.wait_ge(S["xloaded"], i * 16 + 16)
                    for k in range(KD):
                        mm = pe.transpose(bank[:, 0, k * P:(k + 1) * P], xr[:, k * P:(k + 1) * P], ident)
                    mm.then_inc(S["xt"], 1)
                    pe.wait_ge(S["xt_s"], i + 1)
                    for j in range(2):
                        pe.wait_ge(S[f"wloaded{j}"], i * 64 + 64)
                        pe.wait_ge(S["hidden"], i * 2)
                        for a, w in ((0, wg), (1, wu)):
                            for t in range(FT1):
                                for k in range(KD):
                                    mm = pe.matmul(bank[:, 1 + 2 * j + a, t * CAP:(t + 1) * CAP],
                                                   w[:, j, k, t * P:(t + 1) * P], xT[:, k, j * CAP:(j + 1) * CAP],
                                                   start=(k == 0), stop=(k == KD - 1))
                        mm.then_inc(S["up"], 1)
                    for j in range(2):
                        pe.wait_ge(S["hidden"], i * 2 + j + 1)
                        pe.wait_ge(S["y_s"], i * 2)
                        for t in range(FT1):
                            mm = pe.matmul(bank[0:CAP, 5 + j, :], hT[:, j, t, :], wd[:, j, t, :], start=(t == 0),
                                           stop=(t == FT1 - 1))
                        mm.then_inc(S["y"], 1)

            @block.scalar
            def _(act):
                with act.Fori(0, E // 2) as i:
                    for j in range(2):
                        act.wait_ge(S["up"], i * 2 + j + 1)
                        act.wait_ge(S["gated"], i * 2)
                        act.activation(sg[:, j], bank[:, 1 + 2 * j, 0:FT1 * CAP].rearrange("p (t c) -> p t c", c=CAP),
                                       ACT.Sigmoid).then_inc(S["sig"], 1)
                    for j in range(2):
                        act.wait_ge(S["y"], i * 2 + j + 1)
                        act.wait_ge(S["stored"], i * 32)
                        act.activation(ys[:, j, :], bank[0:CAP, 5 + j, :], ACT.Copy).then_inc(S["y_s"], 1)
                        act.wait_ge(S["y_s"], i * 2 + j + 1)
                        act.dma_start(env["ye"][ds(i * P + j * CAP, CAP), :], ys[:, j, :]).then_inc(S["stored"], 16)
                act.wait_ge(S["stored"], 16 * E)

            @block.vector
            def _(dve):
                with dve.Fori(0, E // 2) as i:
                    dve.wait_ge(S["xt"], i + 1)
                    dve.wait_ge(S["up"], i * 2)
                    dve.tensor_copy(xT[:, :, :], bank[:, 0, :].rearrange("p (k c) -> p k c", k=KD)).then_inc(S["xt_s"], 1)
                    for j in range(2):
                        dve.wait_ge(S["sig"], i * 2 + j + 1)
                        dve.wait_ge(S["y"], i * 2)
                        g = bank[:, 1 + 2 * j, 0:FT1 * CAP].rearrange("p (t c) -> p t c", c=CAP)
                        u = bank[:, 2 + 2 * j, 0:FT1 * CAP].rearrange("p (t c) -> p t c", c=CAP)
                        dve.tensor_tensor(hT[:, j], g, sg[:, j], ALU.mult).then_inc(S["gated"], 1)
                        dve.wait_ge(S["gated"], i * 2 + j + 1)
                        dve.tensor_tensor(hT[:, j], u, hT[:, j], ALU.mult).then_inc(S["hidden"], 1)


def combine(env, r):
    nc, X, sem, sb = (env[k] for k in ("nc", "X", "sem", "sb"))
    G = 4
    cleared, got, used, stored = sem("c_clear"), [sem(f"c_got{s}") for s in range(G)], sem("c_used"), sem("c_stored")
    out_v = env["out"].rearrange("b (n p) d -> p (b n) d", p=P)
    with ExitStack() as ctx:
        y = sb(ctx, "cy", [P, G, TOPK, D])
        with nc.Block() as block:
            @block.scalar
            def _(act):
                pass

            @block.gpsimd
            def _(pool):
                for n in range(NT):
                    if n >= G:
                        pool.wait_ge(used, TOPK * (n - G + 1))
                    pool.memset(y[:, n % G], 0.0).then_inc(cleared, 1)
                    pool.wait_ge(cleared, n + 1)
                    for k in range(TOPK):
                        pool.indirect_dma_start(y[:, n % G, k, :], None, env["ye"],
                                                bass.IndirectOffsetOnAxis(ap=r["slot"][:, n, k:k + 1], axis=0),
                                                bounds_check=SLOTS - 1, oob_is_err=False).then_inc(got[n % G], 16)

            @block.vector
            def _(dve):
                for n in range(NT):
                    dve.wait_ge(got[n % G], 16 * TOPK * (n // G + 1))
                    for k in range(TOPK):
                        if k:
                            dve.wait_ge(used, TOPK * n + k)
                        dve.scalar_tensor_tensor(out=X[:, n, :], in0=y[:, n % G, k, :], scalar=r["wk"][:, n, k:k + 1],
                                                 in1=X[:, n, :], op0=ALU.mult, op1=ALU.add).then_inc(used, 1)

            @block.sync
            def _(sp):
                for n in range(NT):
                    sp.wait_ge(used, TOPK * (n + 1))
                    sp.dma_start(out_v[:, n, :], X[:, n, :]).then_inc(stored, 16)
                sp.wait_ge(stored, 16 * NT)


_INS = ['L0_attn_x', 'L0_attn_W_q', 'L0_attn_W_k', 'L0_attn_W_v', 'L0_attn_W_o', 'L0_ffn_W1', 'L0_ffn_W2',
        'L0_ffn_W3', 'L1_attn_Wq', 'L1_attn_Wk', 'L1_attn_Wv', 'L1_attn_Wo', 'L1_attn_lam', 'L1_ffn_Wr', 'L1_ffn_Wg',
        'L1_ffn_Wu', 'L1_ffn_Wd', 'L1_ffn_Wsg', 'L1_ffn_Wsu', 'L1_ffn_Wsd', 'L1_ffn_Wse']


def _lay_out(name, a):
    import numpy as _np
    if name in ("L0_ffn_W1", "L0_ffn_W2", "L0_ffn_W3"):
        a = a.T
    if name == "L1_attn_Wq":
        a = a.reshape(512, 2, 2, 4, 2, 64).transpose(0, 1, 3, 4, 2, 5).reshape(512, 2048)
    if name == "L1_attn_Wk":
        a = a.reshape(512, 2, 2, 2, 64).transpose(0, 1, 3, 2, 4).reshape(512, 512)
    if name == "L1_attn_Wo":
        a = a.reshape(2, 2, 4, 128, 512).transpose(0, 2, 1, 3, 4).reshape(2048, 512)
    return _np.ascontiguousarray(a)


def kernel(**inputs):
    import numpy as _np
    import concourse.bacc as _bacc
    from concourse import mybir as _mybir
    from concourse.bass_utils import run_bass_kernel_spmd as _run

    nc = _bacc.Bacc("TRN2", target_bir_lowering=False, num_devices=1)
    arrays, args = {}, {}
    for name in _INS:
        a = _lay_out(name, _np.asarray(inputs[name]))
        arrays[f"in_{name}_dram"] = a
        args[name] = nc.dram_tensor(f"in_{name}_dram", a.shape, _mybir.dt.from_np(a.dtype), kind="ExternalInput").ap()
    out = nc.dram_tensor("out_0_dram", (BATCH, SEQ, D), F32, kind="ExternalOutput").ap()
    build(nc, args, out)
    r = _run(nc, [arrays], core_ids=[0])
    return r.results[0]["out_0_dram"]
```

```python
from contextlib import ExitStack

import numpy as np

import concourse.bass as bass
from concourse import mybir

F32 = mybir.dt.float32
F32R = mybir.dt.float32r
U32 = mybir.dt.uint32
ALU = mybir.AluOpType
ACT = mybir.ActivationFunctionType
AX = mybir.AxisListType

P = 128
BATCH, SEQ, D = 2, 1024, 512
T = BATCH * SEQ
NT = T // P
KD = D // P
CH = 512
NC = T // CH
EPS = 1e-5

H0, KV0, HD0 = 16, 4, 32
QT0 = H0 * HD0 // P
HPT = P // HD0
QB = SEQ // P
UN0 = QT0 * HPT
F0 = 2048
H1, KV1, HD1, SUB = 16, 4, 128, 64
WINDOW = 128
NEG = -1e30
E, TOPK, CAP, F1, FS = 32, 4, 64, 352, 1408
SLOTS = E * CAP
FT1 = (F1 + P - 1) // P
F1R = F1 - (FT1 - 1) * P
CREDIT = 64
OOB = 1 << 20


SIGNALS = {
    "p0": "w proj read cos sin rotated hi lo v_rows v_taken",
    "h0": "k_loaded q_loaded0 q_loaded1 const peaks max neg neg_rows shift scored exps weighed rec normed "
          "o_taken y added",
    "f0": "up sig gated hidden y added",
    "h1": "w kvw proj cos sin roped scores masked negmax exps recip2 coef cleared mixed den recipd qproj relu probs "
          "turned pt pv ot y added vrows vtaken lam qdone",
    "f1": "up sig gated hidden y added",
    "e": "wloaded0 wloaded1 wloaded2 wloaded3 xloaded0 xloaded1 xt xt_s up sig gated hidden y y_s stored0 stored1 "
         "zeroed",
}


def ds(start, n):
    return bass.ds(start, n)


def shape_constants():
    pos = np.arange(SEQ, dtype=np.float32)
    half = HD0 // 2
    freq = np.float32(1.0) / np.power(np.float32(10000.0), np.arange(half, dtype=np.float32) / np.float32(half))
    ang = pos[:, None] * freq[None, :].astype(np.float32)
    c, s = np.cos(ang).astype(np.float32), np.sin(ang).astype(np.float32)
    cos0 = np.tile(np.repeat(c.T, 2, axis=0), (HPT, 1))
    sgn = np.tile(np.array([-1.0, 1.0], np.float32), P // 2)[:, None]
    sin0 = np.tile(np.repeat(s.T, 2, axis=0), (HPT, 1)) * sgn
    inv = np.float32(1.0) / np.power(np.float32(10000.0), np.arange(0, HD1, 2, dtype=np.float32) / np.float32(HD1))
    ang1 = pos[:, None] * inv[None, :].astype(np.float32)
    cos1 = np.tile(np.cos(ang1).astype(np.float32).T, (2, 1))
    sin1 = np.tile(np.sin(ang1).astype(np.float32).T, (2, 1))
    h = np.array([[1.0]], np.float32)
    while h.shape[0] < P:
        h = np.block([[h, h], [h, -h]])
    q, k = np.arange(P)[:, None], np.arange(P)[None, :]
    band = np.concatenate([np.where(k > q, 0.0, NEG), np.where(k <= q, 0.0, NEG)], axis=1)
    before = (q < k).astype(np.float32)
    misc = np.concatenate([np.eye(P), h, band, before, np.ones((P, P))], axis=1)
    expert = np.tile(np.arange(E, dtype=np.float32), (P, NT, 1)).reshape(P, NT * E)
    f = np.float32
    return {"rope0": np.ascontiguousarray(np.concatenate([cos0, sin0], axis=1), f),
            "rope1": np.ascontiguousarray(np.concatenate([cos1, sin1], axis=1), f),
            "misc": np.ascontiguousarray(misc, f),
            "blocks": np.ascontiguousarray(np.eye(P // 4, CH // P).repeat(P, axis=1), f), "expert": np.ascontiguousarray(expert, f)}


def build(nc, ins, out):
    consts = {k: nc.inline_tensor(v, name="c_" + k) for k, v in shape_constants().items()}
    consts = {k: (v if isinstance(v, bass.AP) else v.ap()) for k, v in consts.items()}
    xe_dram = nc.dram_tensor("xe_dram", [SLOTS, D], F32).ap()
    ye_dram = nc.dram_tensor("ye_dram", [SLOTS, D], F32).ap()

    with ExitStack() as top:
        used = {}

        def sb(ctx, name, shape, dt=F32):
            used[name] = used.get(name, 0) + 1
            return ctx.enter_context(nc.sbuf_tensor(name if used[name] == 1 else f"{name}_{used[name]}", shape, dt))

        def sem(name):
            return top.enter_context(nc.semaphore(name))

        bank = top.enter_context(nc.psum_tensor("bank", [P, 8, 512], F32))
        X = sb(top, "X", [P, NT, D])
        xnT = sb(top, "xnT", [P, KD, T])
        misc = sb(top, "misc", [P, 6 * P])
        ident, had, band = misc[:, 0:P], misc[:, P:2 * P], misc[:, 2 * P:4 * P]
        before, ones = misc[:, 4 * P:5 * P], misc[:, 5 * P:6 * P]
        env = dict(nc=nc, ins=ins, out=out, sb=sb, sem=sem, bank=bank, X=X, xnT=xnT, ident=ident, had=had,
                   band=band, before=before, ones=ones, consts=consts, misc=misc, xe=xe_dram, ye=ye_dram)
        env.update({kind: {n: sem(f"{kind}_{n}") for n in names.split()} for kind, names in SIGNALS.items()})
        layer_norm(env, "0", first=True)
        attention0(env)
        feed_forward0(env)
        with ExitStack() as moe:
            r = dict(slot=sb(moe, "slot", [P, NT, TOPK], U32), wk=sb(moe, "wk", [P, NT, TOPK]),
                     gshared=sb(moe, "gshared", [P, NT]), xn=sb(moe, "xn_rows", [P, NT, D]))
            layer_norm(env, "1", rows=r["xn"])
            route(env, r)
            dispatch(env, r)
            attention1(env)
            feed_forward1(env, r)
            experts(env)
            combine(env, r)


def layer_norm(env, tag, first=False, rows=None):
    nc, X, xnT, bank, ident = env["nc"], env["X"], env["xnT"], env["bank"], env["ident"]
    sem = env["sem"]
    x_loaded = sem("ln_x" + tag)
    stats_done, aggr_done, var_done, sd_done, rstd_done = (sem(f"ln_{n}{tag}") for n in
                                                           ("stats", "aggr", "var", "sd", "rstd"))
    xn_ready, xt_ready, xt_taken = (sem(f"ln_{n}{tag}") for n in ("xn", "xt", "taken"))
    QL = 4
    with ExitStack() as ctx:
        stats = env["sb"](ctx, "ln_stats" + tag, [P, NT, 6])
        mv = env["sb"](ctx, "ln_mv" + tag, [P, NT, 2])
        sd = env["sb"](ctx, "ln_sd" + tag, [P, 2, NT])
        xn = rows if rows is not None else env["sb"](ctx, "ln_xn" + tag, [P, 2, D])
        slots = NT if rows is not None else 2
        block = ctx.enter_context(nc.Block())

        if first:
            @block.gpsimd
            def _(pool):
                for kind in SIGNALS:
                    for s in env[kind].values():
                        pool.sem_inc(s, CREDIT)

            @block.sync
            def _(sp):
                src = env["ins"]["L0_attn_x"].rearrange("b (n p) d -> p (b n) d", p=P)
                sp.dma_start(env["misc"][:, :], env["consts"]["misc"]).then_inc(x_loaded, 16)
                for c in range(QL):
                    n = NT // QL
                    sp.dma_start(X[:, c * n:(c + 1) * n, :], src[:, c * n:(c + 1) * n, :]).then_inc(x_loaded, 16)
                sp.wait_ge(x_loaded, 16 * (QL + 1))

        @block.vector
        def _(dve):
            if first:
                dve.wait_ge(x_loaded, 16 * (QL + 1))
            for n in range(NT):
                dve.bn_stats(stats[:, n, :], X[:, n, :]).then_inc(stats_done, 1)
            for n in range(NT):
                dve.wait_ge(stats_done, n + 1)
                dve.bn_aggr(mv[:, n, :], stats[:, n, :]).then_inc(aggr_done, 1)
            dve.wait_ge(aggr_done, NT)
            dve.tensor_scalar(sd[:, 0, :], mv[:, :, 1], EPS, None, ALU.add).then_inc(var_done, 1)
            dve.wait_ge(sd_done, 1)
            dve.reciprocal(sd[:, 0, :], sd[:, 1, :]).then_inc(rstd_done, 1)
            dve.wait_ge(rstd_done, 1)
            for n in range(NT):
                if n >= slots:
                    dve.wait_ge(xt_ready, n - slots + 1)
                dve.tensor_scalar(xn[:, n % slots, :], X[:, n, :], mv[:, n, 0:1], sd[:, 0, n:n + 1],
                                  ALU.subtract, ALU.mult).then_inc(xn_ready, 1)

        @block.tensor
        def _(pe):
            if first:
                pe.wait_ge(x_loaded, 16 * (QL + 1))
            for n in range(NT):
                pe.wait_ge(xn_ready, n + 1)
                if n >= 4:
                    pe.wait_ge(xt_taken, n - 3)
                for k in range(KD):
                    mm = pe.transpose(bank[:, n % 4, k * P:(k + 1) * P], xn[:, n % slots, k * P:(k + 1) * P], ident)
                mm.then_inc(xt_ready, 1)

        @block.scalar
        def _(act):
            act.wait_ge(var_done, 1)
            act.activation(sd[:, 1, :], sd[:, 0, :], ACT.Sqrt).then_inc(sd_done, 1)
            for n in range(NT):
                act.wait_ge(xt_ready, n + 1)
                act.activation(xnT[:, :, n * P:(n + 1) * P], bank[:, n % 4, :].rearrange("p (k t) -> p k t", k=KD),
                               ACT.Copy).then_inc(xt_taken, 1)


def wait(engine, signal, count):
    engine.wait_ge(signal, count + CREDIT)


def attention0(env):
    nc, sb, ins = (env[k] for k in ("nc", "sb", "ins"))
    NF = QT0 + 2
    with ExitStack() as ctx:
        t = dict(q_hi=sb(ctx, "q_hi", [P, QT0, SEQ], F32R), q_lo=sb(ctx, "q_lo", [P, QT0, SEQ], F32R),
                 k_hi=sb(ctx, "k_hi", [P, SEQ], F32R), k_lo=sb(ctx, "k_lo", [P, SEQ], F32R),
                 v=sb(ctx, "v0", [P, QB, KV0, HD0]), wo=sb(ctx, "wo0", [P, KD, D]))
        for b in range(BATCH):
            with ExitStack() as c2:
                w = sb(c2, "wqkv", [P, KD, NF * P])
                rope = sb(c2, "rope0", [P, 2, SEQ])
                project0(env, c2, b, t, w, rope, NF)
            heads0(env, b, t)


def project0(env, ctx, b, t, w, rope, NF):
    nc, xnT, bank, ident, sb, ins, S = (env[k] for k in ("nc", "xnT", "bank", "ident", "sb", "ins", "p0"))
    swapped = sb(ctx, "swapped", [P, 2, CH])
    direct = sb(ctx, "direct", [P, 2, CH])
    rot = sb(ctx, "rot", [P, 2, CH])
    vT = sb(ctx, "vT", [P, CH])
    HALVES, NR = SEQ // CH, NF - 1
    loads = 4 + (b == 0)
    loaded = 16 * (loads + (5 if b else 0))

    def turn(i, per):
        return (i + b * HALVES) * per

    with nc.Block() as block:
        @block.sync
        def _(sp):
            for c0, c1, name in ((0, D, "W_q"), (D, D + P, "W_k"), (D + P, D + 2 * P, "W_v")):
                sp.dma_start(w[:, :, c0:c1], ins["L0_attn_" + name].rearrange("(k p) n -> p k n", p=P)).then_inc(S["w"], 16)
            sp.dma_start(rope[:, :, :], env["consts"]["rope0"].rearrange("p (a s) -> p a s", a=2)).then_inc(S["w"], 16)
            if b == 0:
                sp.dma_start(t["wo"][:, :, :], ins["L0_attn_W_o"].rearrange("(k p) n -> p k n", p=P)).then_inc(S["w"], 16)
            wait(sp, S["w"], loaded)

        @block.tensor
        def _(pe):
            wait(pe, S["w"], loaded)
            with pe.Fori(0, HALVES) as h:
                for f in range(NF):
                    wait(pe, S["read"], turn(h, NF) + f - (1 if f < NF - 4 else 3))
                    for k in range(KD):
                        mm = pe.matmul(bank[:, f % 4, :], w[:, k, f * P:(f + 1) * P],
                                       xnT[:, k, ds(h * CH + b * SEQ, CH)], start=(k == 0), stop=(k == KD - 1))
                    mm.then_inc(S["proj"], 1)
                wait(pe, S["read"], turn(h, NF) + NF)
                wait(pe, S["v_taken"], turn(h, 1))
                for s in range(CH // P):
                    mm = pe.transpose(bank[:, 6, s * P:(s + 1) * P], vT[:, s * P:(s + 1) * P], ident)
                mm.then_inc(S["v_rows"], 1)

        @block.vector
        def _(dve):
            wait(dve, S["w"], loaded)
            with dve.Fori(0, HALVES) as h:
                for f in range(NF):
                    wait(dve, S["proj"], turn(h, NF) + f + 1)
                    if f == NR:
                        wait(dve, S["v_rows"], turn(h, 1))
                        dve.tensor_copy(vT[:, :], bank[:, f % 4, :]).then_inc(S["read"], 1)
                        continue
                    n = turn(h, NR) + f
                    wait(dve, S["rotated"], n)
                    dve.tensor_tensor(direct[:, f % 2, :], bank[:, f % 4, :], rope[:, 0, ds(h * CH, CH)],
                                      ALU.mult).then_inc(S["cos"], 1)
                    dve.stream_shuffle(swapped[:, f % 2, :], bank[:, f % 4, :],
                                       [i ^ 1 for i in range(32)]).then_inc(S["read"], 1)
                    wait(dve, S["read"], turn(h, NF) + f + 1)
                    dve.tensor_tensor(swapped[:, f % 2, :], swapped[:, f % 2, :], rope[:, 1, ds(h * CH, CH)],
                                      ALU.mult).then_inc(S["sin"], 1)
                    wait(dve, S["sin"], n + 1)
                    wait(dve, S["lo"], n - 1 if f else n)
                    dve.tensor_tensor(rot[:, f % 2, :], direct[:, f % 2, :], swapped[:, f % 2, :],
                                      ALU.add).then_inc(S["rotated"], 1)

        def parts(f, h):
            at = ds(h * CH, CH)
            if f < QT0:
                return t["q_hi"][:, f, at], t["q_lo"][:, f, at]
            return t["k_hi"][:, at], t["k_lo"][:, at]

        @block.scalar
        def _(act):
            with act.Fori(0, HALVES) as h:
                for f in range(NR):
                    wait(act, S["rotated"], turn(h, NR) + f + 1)
                    act.activation(parts(f, h)[0], rot[:, f % 2, :], ACT.Copy).then_inc(S["hi"], 1)
                wait(act, S["v_rows"], turn(h, 1) + 1)
                act.activation(t["v"][:, ds(h * (CH // P), CH // P), :, :],
                               bank[:, 6, :].rearrange("p (s j d) -> p s j d", j=KV0, d=HD0),
                               ACT.Copy).then_inc(S["v_taken"], 1)

        @block.gpsimd
        def _(pool):
            with pool.Fori(0, HALVES) as h:
                for f in range(NR):
                    wait(pool, S["hi"], turn(h, NR) + f + 1)
                    hi, lo = parts(f, h)
                    pool.tensor_tensor(lo, rot[:, f % 2, :], hi.bitcast(F32), ALU.subtract).then_inc(S["lo"], 1)


def heads0(env, b, t):
    nc, X, bank, ident, ones, sb, S = (env[k] for k in ("nc", "X", "bank", "ident", "ones", "sb", "h0"))
    scale = float(HD0) ** -0.5
    CHUNKS, SUBS, STEPS = SEQ // CH, CH // P, QB // 2
    R = 3 * HD0
    GROUP = HPT
    LOADS = 3 * GROUP
    PAIRS = UN0 // 2
    with ExitStack() as ctx:
        qp = sb(ctx, "q_parts", [P, 2 * GROUP, CH], F32R)
        kp = sb(ctx, "k_parts", [P, KV0, SEQ], F32R)
        probs = sb(ctx, "probs", [P, 2, 2, 2, CH])
        mx = sb(ctx, "mx", [P, 2, SUBS, 2])
        neg = sb(ctx, "neg", [P, 2, P])
        o = sb(ctx, "o", [P, CH])
        rec = sb(ctx, "rec", [P, CH])
        oT = sb(ctx, "oT", [P, KD, CH])
        blocks = sb(ctx, "blocks", [P, SUBS, P])

        def at(c, per):
            return (c + b * CHUNKS) * per

        with nc.Block() as block:
            @block.sync
            def _(sp):
                sp.dma_start(blocks[R:, :, :], env["consts"]["blocks"].rearrange("p (s q) -> p s q", s=SUBS)).then_inc(
                    S["k_loaded"], 16)
                for j in range(KV0):
                    for r, part in enumerate(("k_hi", "k_hi", "k_lo")):
                        sp.dma_start(kp[HD0 * r:HD0 * (r + 1), j, :].bitcast(F32),
                                     t[part][HD0 * j:HD0 * (j + 1), :].bitcast(F32)).then_inc(S["k_loaded"], 16)
                with sp.Fori(0, CHUNKS) as c:
                    for g in range(QT0):
                        wait(sp, S["scored"], at(c, UN0 * STEPS) + (g - 1) * GROUP * STEPS)
                        for j in range(GROUP):
                            for r, part in enumerate(("q_hi", "q_lo", "q_hi")):
                                sp.dma_start(qp[HD0 * r:HD0 * (r + 1), g % 2 * GROUP + j, :].bitcast(F32),
                                             t[part][HD0 * j:HD0 * (j + 1), g, ds(c * CH, CH)].bitcast(F32)).then_inc(
                                    S[f"q_loaded{g % 2}"], 16)

            @block.gpsimd
            def _(pool):
                pool.memset(kp[R:, :, :].bitcast(F32), 1.0).then_inc(S["const"], 1)
                wait(pool, S["const"], 2 * b + 1)
                pool.memset(neg[:, :, :], 0.0).then_inc(S["const"], 1)

            def loaded(engine, c, u):
                g = u // GROUP
                wait(engine, S[f"q_loaded{g % 2}"], at(c, QT0 // 2 * 16 * LOADS) + (g // 2 + 1) * 16 * LOADS)

            @block.tensor
            def _(pe):
                wait(pe, S["k_loaded"], 16 * (1 + LOADS) * (b + 1))
                wait(pe, S["const"], 2 * (b + 1))
                with pe.Fori(0, CHUNKS) as c:
                    def peak(u, q, h):
                        if u >= UN0:
                            return
                        n = at(c, 2 * UN0 * SUBS) + 2 * (u * SUBS + q) + h
                        if q == 0 and h == 0 and u % GROUP == 0:
                            loaded(pe, c, u)
                        if u == 0 and q == 0:
                            wait(pe, S["added"], at(c, SUBS))
                        wait(pe, S["max"], n - 1)
                        pe.matmul(bank[:, h, :], qp[0:R, u % (2 * GROUP), q * P:(q + 1) * P],
                                  kp[0:R, u % KV0, h * CH:(h + 1) * CH], start=True, stop=True).then_inc(S["peaks"], 1)

                    def turn_max(u):
                        if u >= UN0:
                            return
                        wait(pe, S["neg"], at(c, UN0) + u + 1)
                        pe.transpose(bank[:, 7, 0:P], neg[:, u % 2, :], ident).then_inc(S["neg_rows"], 1)

                    def score(w, s, x):
                        n, u = at(c, UN0 * STEPS) + 2 * (w * STEPS + s) + x, 2 * w + x
                        if s == 0:
                            wait(pe, S["shift"], at(c, UN0) + u + 1)
                        wait(pe, S["exps"], n - 1)
                        for m in range(2):
                            kt = 2 * s + m
                            mm = pe.matmul(bank[:, 2 + 2 * x + m, :], kp[:, u % KV0, kt * P:(kt + 1) * P],
                                           qp[:, u % (2 * GROUP), :], start=True, stop=True)
                        mm.then_inc(S["scored"], 1)

                    def weigh(w, s):
                        wait(pe, S["exps"], at(c, UN0 * STEPS) + 2 * (w * STEPS + s) + 2)
                        if s == 0:
                            wait(pe, S["o_taken"], at(c, PAIRS) + w)
                        for m in range(2):
                            for x in range(2):
                                for row, left in ((64 * x, t["v"][:, 2 * s + m, (2 * w + x) % KV0, :]),
                                                  (64 * x + HD0, ones[:, 0:HD0])):
                                    mm = pe.matmul(bank[row:row + HD0, 6, :], left, probs[:, x, s % 2, m, :],
                                                   start=(s == 0 and m == 0), stop=(s == STEPS - 1 and m == 1),
                                                   skip_group_check=True)
                        mm.then_inc(S["weighed"], 1)

                    for x in range(2):
                        for q in range(SUBS):
                            peak(x, q, 0)
                            peak(x, q, 1)
                        if x == 0:
                            turn_max(0)
                    for w in range(PAIRS):
                        for s in range(STEPS):
                            u, q = 2 * w + 2 + s // 2, s % 2 * 2
                            peak(u, q, 0)
                            score(w, s, 0)
                            peak(u, q, 1)
                            if s == 0:
                                turn_max(2 * w + 1)
                            if s or w:
                                weigh(*((w, s - 1) if s else (w - 1, STEPS - 1)))
                            peak(u, q + 1, 0)
                            score(w, s, 1)
                            peak(u, q + 1, 1)
                            if s == 2:
                                turn_max(2 * w + 2)
                    weigh(PAIRS - 1, STEPS - 1)
                    wait(pe, S["normed"], at(c, UN0) + UN0)
                    for q in range(SUBS):
                        for k in range(KD):
                            mm = pe.matmul(bank[:, q, :], oT[:, k, q * P:(q + 1) * P], t["wo"][:, k, :],
                                           start=(k == 0), stop=(k == KD - 1))
                        mm.then_inc(S["y"], 1)

            @block.vector
            def _(dve):
                wait(dve, S["k_loaded"], 16 * (1 + LOADS) * (b + 1))
                wait(dve, S["const"], 2 * (b + 1))
                with dve.Fori(0, CHUNKS) as c:
                    def maximum(u, q, h):
                        if u >= UN0:
                            return
                        wait(dve, S["peaks"], at(c, 2 * UN0 * SUBS) + 2 * (u * SUBS + q) + h + 1)
                        dve.reduce_max(mx[:, u % 2, q, h:h + 1], bank[:, h, :], AX.X).then_inc(S["max"], 1)

                    def negate(u):
                        if u >= UN0:
                            return
                        wait(dve, S["max"], at(c, 2 * UN0 * SUBS) + 2 * (u + 1) * SUBS)
                        wait(dve, S["neg_rows"], at(c, UN0) + u)
                        dve.tensor_reduce(neg[:, u % 2, R:R + SUBS], mx[:, u % 2, :, :], AX.X, ALU.max,
                                          negate=True).then_inc(S["neg"], 1)

                    def shift(u):
                        if u >= UN0:
                            return
                        wait(dve, S["neg_rows"], at(c, UN0) + u + 1)
                        dve.tensor_tensor(qp[R:, u % (2 * GROUP), :].rearrange("p (s q) -> p s q", s=SUBS),
                                          bank[R:, 7:8, 0:P].to_broadcast([P - R, SUBS, P]), blocks[R:, :, :],
                                          ALU.mult).then_inc(S["shift"], 1)

                    def norm(w):
                        wait(dve, S["o_taken"], at(c, PAIRS) + w + 1)
                        wait(dve, S["normed"], at(c, UN0) + 2 * w)
                        for x in range(2):
                            dve.reciprocal(rec[64 * x:64 * x + HD0, :], o[64 * x + HD0:64 * x + 2 * HD0, :]).then_inc(
                                S["rec"], 1)
                        if w == 0:
                            wait(dve, S["y"], at(c, SUBS))
                        for x in range(2):
                            j, k = (2 * w + x) % HPT, 2 * w // HPT
                            wait(dve, S["rec"], at(c, UN0) + 2 * w + x + 1)
                            dve.tensor_tensor(oT[HD0 * j:HD0 * (j + 1), k, :], o[64 * x:64 * x + HD0, :],
                                              rec[64 * x:64 * x + HD0, :], ALU.mult).then_inc(S["normed"], 1)

                    for x in range(2):
                        for q in range(SUBS):
                            maximum(x, q, 0)
                            maximum(x, q, 1)
                        negate(x)
                        if x == 0:
                            shift(0)
                    for w in range(PAIRS):
                        for s in range(STEPS):
                            u, q = 2 * w + 2 + s // 2, s % 2 * 2
                            maximum(u, q, 0)
                            maximum(u, q, 1)
                            if s == 0:
                                shift(2 * w + 1)
                            maximum(u, q + 1, 0)
                            maximum(u, q + 1, 1)
                            if s % 2 == 1:
                                negate(u)
                            if s == 1 and w:
                                norm(w - 1)
                            if s == 2:
                                shift(2 * w + 2)
                    norm(PAIRS - 1)
                    for q in range(SUBS):
                        wait(dve, S["y"], at(c, SUBS) + q + 1)
                        row = X[:, ds(c * SUBS + (b * QB + q), 1), :].rearrange("p a d -> p (a d)")
                        dve.tensor_tensor(row, row, bank[:, q, :], ALU.add).then_inc(S["added"], 1)

            @block.scalar
            def _(act):
                with act.Fori(0, CHUNKS) as c:
                    def take(w):
                        wait(act, S["weighed"], at(c, PAIRS * STEPS) + (w + 1) * STEPS)
                        wait(act, S["normed"], at(c, UN0) + 2 * w)
                        act.activation(o[:, :], bank[:, 6, :], ACT.Copy).then_inc(S["o_taken"], 1)

                    for w in range(PAIRS):
                        for s in range(STEPS):
                            for x in range(2):
                                n = at(c, UN0 * STEPS) + 2 * (w * STEPS + s) + x
                                wait(act, S["scored"], n + 1)
                                wait(act, S["weighed"], at(c, PAIRS * STEPS) + w * STEPS + s - 1)
                                act.activation(probs[:, x, s % 2, :, :], bank[:, 2 + 2 * x:4 + 2 * x, :], ACT.Exp,
                                               scale=scale).then_inc(S["exps"], 1)
                            if s == 0 and w:
                                take(w - 1)
                    take(PAIRS - 1)


def swiglu_chunks(env, tag, block, tiles, wg, wu, wd, hid, sg, ready, ready_value, scale=None, gate=None):
    nc, X, xnT, bank, S = (env[k] for k in ("nc", "X", "xnT", "bank", "f" + tag))
    up, sig, gated, hidden, y, added = (S[n] for n in ("up", "sig", "gated", "hidden", "y", "added"))
    SUBS = CH // P

    @block.tensor
    def _(pe):
        pe.wait_ge(ready, ready_value)
        with pe.Fori(0, NC) as c:
            def down(h):
                wait(pe, hidden, c * tiles + h + 1)
                if h == 0:
                    wait(pe, added, c * SUBS)
                for s in range(SUBS):
                    mm = pe.matmul(bank[:, 4 + s, :], hid[:, h % 2, s * P:(s + 1) * P], wd[:, h, :],
                                   start=(h == 0), stop=(h == tiles - 1))
                mm.then_inc(y, 1)
            for h in range(tiles):
                wait(pe, hidden, c * tiles + h - 1)
                for a, w in ((0, wg), (1, wu)):
                    for k in range(KD):
                        mm = pe.matmul(bank[:, 2 * (h % 2) + a, :], w[:, k, h * P:(h + 1) * P],
                                       xnT[:, k, ds(c * CH, CH)], start=(k == 0), stop=(k == KD - 1))
                mm.then_inc(up, 1)
                if h >= 1:
                    down(h - 1)
            down(tiles - 1)

    @block.scalar
    def _(act):
        with act.Fori(0, NC) as c:
            for h in range(tiles):
                wait(act, up, c * tiles + h + 1)
                wait(act, gated, c * tiles + h - 1)
                act.activation(sg[:, h % 2, :], bank[:, 2 * (h % 2), :], ACT.Sigmoid).then_inc(sig, 1)

    @block.vector
    def _(dve):
        with dve.Fori(0, NC) as c:
            for h in range(tiles):
                wait(dve, sig, c * tiles + h + 1)
                wait(dve, y, c * tiles + h - 1)
                dve.tensor_tensor(hid[:, h % 2, :], bank[:, 2 * (h % 2), :], sg[:, h % 2, :],
                                  ALU.mult).then_inc(gated, 1)
                wait(dve, gated, c * tiles + h + 1)
                dve.tensor_tensor(hid[:, h % 2, :], bank[:, 2 * (h % 2) + 1, :], hid[:, h % 2, :],
                                  ALU.mult).then_inc(hidden, 1)
            wait(dve, y, c * tiles + tiles)
            for s in range(SUBS):
                row = X[:, ds(c * SUBS + s, 1), :].rearrange("p a d -> p (a d)")
                factor = scale if gate is None else gate[:, ds(c * SUBS + s, 1)]
                dve.scalar_tensor_tensor(out=row, in0=bank[:, 4 + s, :], scalar=factor, in1=row,
                                         op0=ALU.mult, op1=ALU.add).then_inc(added, 1)


def feed_forward0(env):
    nc, bank, had, sem, sb, ins = (env[k] for k in ("nc", "bank", "had", "sem", "sb", "ins"))
    HT = F0 // P
    CW = 128
    with ExitStack() as ctx:
        w1 = sb(ctx, "w1", [P, KD, F0])
        w3 = sb(ctx, "w3", [P, KD, F0])
        w2 = sb(ctx, "w2", [P, HT, D])
        loaded, raw, flat, bf = (sem("f0_" + n) for n in ("loaded", "raw", "flat", "bf"))
        with ExitStack() as c2:
            ping = sb(c2, "ping", [P, HT, CW])
            pong = sb(c2, "pong", [P, HT, CW])
            with nc.Block() as block:
                @block.sync
                def _(sp):
                    sp.dma_start(w2[:, :, :], ins["L0_ffn_W2"].rearrange("(h p) d -> p h d", p=P)).then_inc(loaded, 16)
                    sp.dma_start(w1[:, :, :], ins["L0_ffn_W1"].rearrange("(k p) h -> p k h", p=P)).then_inc(loaded, 16)
                    sp.dma_start(w3[:, :, :], ins["L0_ffn_W3"].rearrange("(k p) h -> p k h", p=P)).then_inc(loaded, 16)
                    sp.wait_ge(loaded, 48)

                @block.tensor
                def _(pe):
                    pe.wait_ge(loaded, 48)
                    for c in range(D // CW):
                        if c:
                            pe.wait_ge(flat, 4 * c)
                        for q in range(4):
                            mm = pe.matmul(bank[:, q, :], had, w2[:, 4 * q:4 * q + 4, c * CW:(c + 1) * CW],
                                           start=True, stop=True)
                            mm.then_inc(raw, 1)

                @block.scalar
                def _(act):
                    for c in range(D // CW):
                        if c:
                            act.wait_ge(bf, 8 * c)
                        for q in range(4):
                            act.wait_ge(raw, 4 * c + q + 1)
                            act.activation(ping[:, 4 * q:4 * q + 4, :],
                                           bank[:, q, :].rearrange("p (a n) -> p a n", n=CW),
                                           ACT.Copy).then_inc(flat, 1)

                @block.vector
                def _(dve):
                    for c in range(D // CW):
                        dve.wait_ge(flat, 4 * (c + 1))
                        bufs = [ping[:, :, :], pong[:, :, :], ping[:, :, :], pong[:, :, :],
                                w2[:, :, c * CW:(c + 1) * CW]]
                        for st in range(4):
                            h = 1 << st
                            src = bufs[st].rearrange("p (g two h) n -> p g two h n", two=2, h=h)
                            dst = bufs[st + 1].rearrange("p (g two h) n -> p g two h n", two=2, h=h)
                            if st:
                                dve.wait_ge(bf, 8 * c + 2 * st)
                            for j, op in ((0, ALU.add), (1, ALU.subtract)):
                                if h in (1, 8):
                                    a = 0 if h == 8 else slice(None)
                                    z = slice(None) if h == 8 else 0
                                    i0, i1, o = src[:, a, 0, z, :], src[:, a, 1, z, :], dst[:, a, j, z, :]
                                else:
                                    i0, i1, o = src[:, :, 0], src[:, :, 1], dst[:, :, j]
                                dve.tensor_tensor(o, i0, i1, op).then_inc(bf, 1)
        with ExitStack() as c3:
            hid = sb(c3, "hid0", [P, 2, CH])
            sg = sb(c3, "sg0", [P, 2, CH])
            with nc.Block() as block:
                swiglu_chunks(env, "0", block, HT, w1, w3, w2, hid, sg, loaded, 48, scale=float(F0) ** -0.5)


def route(env, r):
    nc, xnT, bank, ident, sem, sb, ins = (env[k] for k in ("nc", "xnT", "bank", "ident", "sem", "sb", "ins"))
    W = E + 1
    loaded, lgT, lgT_s, lg, lg_s, cnt, chain, ex = (sem("r_" + n) for n in
                                                    ("loaded", "lgT", "lgTs", "lg", "lgs", "cnt", "chain", "exp"))
    with ExitStack() as ctx:
        wr = sb(ctx, "wr", [P, KD, W])
        logT = sb(ctx, "logT", [W, T])
        log = sb(ctx, "log", [P, NT, W])
        iota = sb(ctx, "iota", [P, NT, E])
        top = sb(ctx, "top", [P, NT, 8])
        topi = sb(ctx, "topi", [P, NT, 8], U32)
        topf = sb(ctx, "topf", [P, NT, 8])
        hot = sb(ctx, "hot", [P, TOPK, NT, E])
        mask = sb(ctx, "mask", [P, NT, E])
        slotv = sb(ctx, "slotv", [P, NT, E])
        base = sb(ctx, "base", [P, NT, E])
        tmp = sb(ctx, "tmp", [P, NT, E])
        exps = sb(ctx, "exps", [P, NT, TOPK])
        sums = sb(ctx, "sums", [P, 2, NT])
        slotf = sb(ctx, "slotf", [P, NT, TOPK])
        ok = sb(ctx, "ok", [P, NT, TOPK])
        with nc.Block() as block:
            @block.sync
            def _(sp):
                sp.dma_start(wr[:, :, 0:E], ins["L1_ffn_Wr"].rearrange("(k p) n -> p k n", p=P)).then_inc(loaded, 16)
                sp.dma_start(wr[:, :, E:W], ins["L1_ffn_Wse"].rearrange("(k p) n -> p k n", p=P),
                             allow_slow_non_contiguous=True).then_inc(loaded, 16)
                sp.dma_start(iota[:, :, :], env["consts"]["expert"].rearrange("p (n e) -> p n e", e=E)).then_inc(loaded, 16)
                sp.wait_ge(loaded, 48)

            @block.tensor
            def _(pe):
                pe.wait_ge(loaded, 48)
                for c in range(NC):
                    for k in range(KD):
                        mm = pe.matmul(bank[0:W, c, :], wr[:, k, :], xnT[:, k, c * CH:(c + 1) * CH],
                                       start=(k == 0), stop=(k == KD - 1))
                    mm.then_inc(lgT, 1)
                for c in range(NC):
                    pe.wait_ge(lgT_s, c + 1)
                    for s in range(CH // P):
                        n = c * (CH // P) + s
                        mm = pe.transpose(bank[:, 4 + c // 2, (n % 8) * W:(n % 8 + 1) * W],
                                          logT[:, n * P:(n + 1) * P], ident[0:W, 0:W])
                    mm.then_inc(lg, 1)
                pe.wait_ge(cnt, 1)
                pe.matmul(bank[:, 6, :], env["before"], mask[:, :, :], start=True, stop=True).then_inc(lg, 1)
                pe.matmul(bank[:, 7, :], env["ones"], mask[:, :, :], start=True, stop=True).then_inc(lg, 1)

            @block.scalar
            def _(act):
                for c in range(NC):
                    act.wait_ge(lgT, c + 1)
                    act.activation(logT[:, c * CH:(c + 1) * CH], bank[0:W, c, :], ACT.Copy).then_inc(lgT_s, 1)
                for g in range(2):
                    act.wait_ge(lg, 2 * (g + 1))
                    act.activation(log[:, 8 * g:8 * g + 8, :],
                                   bank[:, 4 + g, 0:8 * W].rearrange("p (n e) -> p n e", e=W),
                                   ACT.Copy).then_inc(lg_s, 1)
                act.wait_ge(ex, 1)
                act.activation(exps[:, :, :], slotf[:, :, :], ACT.Exp).then_inc(lg_s, 1)
                act.wait_ge(lg_s, 3)
                act.activation(r["gshared"][:, :], log[:, :, E], ACT.Sigmoid).then_inc(lg_s, 1)

            @block.vector
            def _(dve):
                steps = [0]

                def step(instruction):
                    steps[0] += 1
                    instruction.then_inc(chain, 1)
                    dve.wait_ge(chain, steps[0])
                dve.wait_ge(loaded, 48)
                dve.wait_ge(lg_s, 2)
                for n in range(NT):
                    ins_ = dve.max(top[:, n, :], log[:, n, 0:E])
                step(ins_)
                for n in range(NT):
                    ins_ = dve.max_index(topi[:, n, :], top[:, n, :], log[:, n, 0:E])
                step(ins_)
                step(dve.tensor_copy(topf[:, :, :], topi[:, :, :]))
                step(dve.tensor_tensor(slotf[:, :, :], top[:, :, 0:TOPK],
                                       top[:, :, 0:1].to_broadcast([P, NT, TOPK]), ALU.subtract))
                dve.sem_inc(ex, 1)
                for k in range(TOPK):
                    step(dve.tensor_tensor(hot[:, k], iota[:, :, :], topf[:, :, k:k + 1].to_broadcast([P, NT, E]),
                                           ALU.is_equal))
                step(dve.tensor_tensor(mask[:, :, :], hot[:, 0], hot[:, 1], ALU.add))
                step(dve.tensor_tensor(mask[:, :, :], mask[:, :, :], hot[:, 2], ALU.add))
                step(dve.tensor_tensor(mask[:, :, :], mask[:, :, :], hot[:, 3], ALU.add))
                dve.sem_inc(cnt, 1)
                dve.wait_ge(lg, NC + 2)
                step(dve.memset(base[:, 0, :], 0.0))
                for n in range(1, NT):
                    step(dve.tensor_tensor(base[:, n, :], bank[:, 7, (n - 1) * E:n * E], base[:, n - 1, :], ALU.add))
                step(dve.tensor_tensor(base[:, :, :], bank[:, 6, :].rearrange("p (n e) -> p n e", e=E),
                                       base[:, :, :], ALU.add))
                step(dve.tensor_scalar(tmp[:, :, :], base[:, :, :], float(CAP), float(OOB), ALU.is_ge, ALU.mult))
                step(dve.tensor_tensor(tmp[:, :, :], tmp[:, :, :], base[:, :, :], ALU.add))
                step(dve.scalar_tensor_tensor(out=slotv[:, :, :], in0=iota[:, :, :], scalar=float(CAP),
                                              in1=tmp[:, :, :], op0=ALU.mult, op1=ALU.add))
                dve.wait_ge(lg_s, 3)
                for k in range(TOPK):
                    step(dve.tensor_tensor(tmp[:, :, :], hot[:, k], slotv[:, :, :], ALU.mult))
                    step(dve.tensor_reduce(slotf[:, :, k], tmp[:, :, :], AX.X, ALU.add))
                step(dve.tensor_copy(r["slot"][:, :, :], slotf[:, :, :]))
                step(dve.tensor_scalar(ok[:, :, :], slotf[:, :, :], float(SLOTS), None, ALU.is_lt))
                step(dve.tensor_reduce(sums[:, 0, :], exps[:, :, :], AX.X, ALU.add))
                step(dve.reciprocal(sums[:, 1, :], sums[:, 0, :]))
                step(dve.tensor_tensor(ok[:, :, :], ok[:, :, :], exps[:, :, :], ALU.mult))
                for k in range(TOPK):
                    step(dve.tensor_tensor(r["wk"][:, :, k], ok[:, :, k], sums[:, 1, :], ALU.mult))


def dispatch(env, r):
    nc, sem, sb = (env[k] for k in ("nc", "sem", "sb"))
    zeroed, sent, z = sem("d_zeroed"), sem("d_sent"), sem("d_z")
    env["sent"] = sent
    with ExitStack() as ctx:
        zero = sb(ctx, "zero", [P, D])
        with nc.Block() as block:
            @block.gpsimd
            def _(pool):
                pool.memset(zero[:, :], 0.0).then_inc(z, 1)
                pool.wait_ge(zeroed, 16 * SLOTS // P)
                for n in range(NT):
                    for k in range(TOPK):
                        pool.indirect_dma_start(env["xe"], bass.IndirectOffsetOnAxis(ap=r["slot"][:, n, k:k + 1], axis=0),
                                                r["xn"][:, n, :], None, bounds_check=SLOTS - 1,
                                                oob_is_err=False).then_inc(sent, 16)
                pool.wait_ge(sent, 16 * NT * TOPK)

            @block.sync
            def _(sp):
                sp.wait_ge(z, 1)
                for m in range(SLOTS // P):
                    sp.dma_start(env["xe"][m * P:(m + 1) * P, :], zero[:, :]).then_inc(zeroed, 16)
                sp.wait_ge(zeroed, 16 * SLOTS // P)


def attention1(env):
    nc, X, xnT, bank, ident, band, sem, sb, ins = (env[k] for k in ("nc", "X", "xnT", "bank", "ident", "band", "sem",
                                                                    "sb", "ins"))
    PAIRS = H1 // 4
    scale = float(SUB) ** -0.5
    UN = 2 * NT
    S = env["h1"]
    with ExitStack() as ctx:
        wq = sb(ctx, "wq1", [P, KD, 2 * P])
        wo = sb(ctx, "wo1", [P, 2, D])
        wk = sb(ctx, "wk1", [P, KD, 2 * P])
        q = sb(ctx, "q1", [P, 2, T])
        k_ = sb(ctx, "k1", [P, 2, T])
        v = sb(ctx, "v1", [P, NT, 2 * P])
        rope = sb(ctx, "rope1", [P, 2, SEQ])
        lam = sb(ctx, "lam", [P, H1])
        tr = sb(ctx, "tr", [P, 4, CH])
        ms = sb(ctx, "ms", [P, 4, 2, 2 * P])
        mix = sb(ctx, "mix", [P, 4, 2 * P])
        pt = sb(ctx, "pt1", [P, 2, 2 * P])
        oT = sb(ctx, "oT1", [P, 2, 2, P])
        sm = sb(ctx, "sm1", [P, 4, 12])
        wv = wk

        with nc.Block() as block:
            @block.sync
            def _(sp):
                sp.dma_start(rope[:, :, :], env["consts"]["rope1"].rearrange("p (a s) -> p a s", a=2)).then_inc(S["lam"], 16)
                sp.dma_start(lam[:, :], ins["L1_attn_lam"].partition_broadcast(P)).then_inc(S["lam"], 16)
                wait(sp, S["lam"], 32)

            @block.vector
            def _(dve):
                wait(dve, S["lam"], 32)
                dve.tensor_scalar(lam[:, :], lam[:, :], -1.0, None, ALU.mult).then_inc(S["lam"], 1)
                wait(dve, S["lam"], 33)

        for g in range(2):
            for part in range(2):
                src = ins["L1_attn_Wk" if part == 0 else "L1_attn_Wv"]
                with nc.Block() as block:
                    n0 = (2 * g + part)
                    project_rope(env, block, S, "k" if part == 0 else "v", n0, g,
                                 src.rearrange("(k p) n -> p k n", p=P)[:, :, 2 * P * g:2 * P * (g + 1)],
                                 wk, k_, v, rope, tr)
            with nc.Block() as block:
                attention1_pairs(env, block, S, g, PAIRS, UN, scale, wq, wo, q, k_, v, rope, lam, tr, ms, mix, pt,
                                 oT, sm)


def project_rope(env, block, S, kind, n0, g, src, wk, k_, v, rope, tr):
    nc, xnT, bank, ident = (env[k] for k in ("nc", "xnT", "bank", "ident"))
    rounds = NC * g

    @block.sync
    def _(sp):
        sp.dma_start(wk[:, :, :], src).then_inc(S["kvw"], 16)
        wait(sp, S["kvw"], 16 * (n0 + 1))

    @block.tensor
    def _(pe):
        wait(pe, S["kvw"], 16 * (n0 + 1))
        for c in range(NC):
            if c >= 2 or n0:
                wait(pe, S["qdone"], n0 * NC + c - 1)
            for a in range(2):
                for k in range(KD):
                    mm = pe.matmul(bank[:, 2 * (c % 2) + a, :], wk[:, k, a * P:(a + 1) * P],
                                   xnT[:, k, c * CH:(c + 1) * CH], start=(k == 0), stop=(k == KD - 1))
            mm.then_inc(S["proj"], 1)
            if kind == "v":
                wait(pe, S["qdone"], n0 * NC + c + 1)
                if c or g:
                    wait(pe, S["vtaken"], rounds + c)
                for s in range(CH // P):
                    for a in range(2):
                        mm = pe.transpose(bank[:, 4 + s // 2, (s % 2) * 2 * P + a * P:(s % 2) * 2 * P + (a + 1) * P],
                                          tr[:, a, s * P:(s + 1) * P], ident)
                mm.then_inc(S["vrows"], 1)

    @block.vector
    def _(dve):
        for c in range(NC):
            wait(dve, S["proj"], n0 * NC + c + 1)
            if c or n0:
                wait(dve, S["qdone"], n0 * NC + c)
            if kind == "v":
                if c or g:
                    wait(dve, S["vrows"], rounds + c)
                dve.tensor_copy(tr[:, 0:2, :], bank[:, 2 * (c % 2):2 * (c % 2) + 2, :]).then_inc(S["qdone"], 1)
            else:
                rotate(dve, S, bank[:, 2 * (c % 2), :], bank[:, 2 * (c % 2) + 1, :],
                       k_[:, 0, c * CH:(c + 1) * CH], k_[:, 1, c * CH:(c + 1) * CH],
                       rope[:, 0, (c % 2) * CH:(c % 2 + 1) * CH], rope[:, 1, (c % 2) * CH:(c % 2 + 1) * CH], tr,
                       (rounds + c) * 2, lambda n: n)

    if kind == "v":
        @block.scalar
        def _(act):
            for c in range(NC):
                wait(act, S["vrows"], rounds + c + 1)
                act.activation(v[:, c * 4:(c + 1) * 4, :],
                               bank[:, 4:6, :].rearrange("p a (s n) -> p (a s) n", n=2 * P),
                               ACT.Copy).then_inc(S["vtaken"], 1)


def rotate(dve, S, first, second, out1, out2, cos, sin, tr, done, at, names=("cos", "qdone")):
    pa, pc = names
    dve.tensor_tensor(tr[:, 0, :], first, cos, ALU.mult)
    dve.tensor_tensor(tr[:, 1, :], second, sin, ALU.mult).then_inc(S[pa], 1)
    dve.tensor_tensor(tr[:, 2, :], second, cos, ALU.mult)
    dve.tensor_tensor(tr[:, 3, :], first, sin, ALU.mult).then_inc(S[pa], 1)
    wait(dve, S[pa], at(done + 1))
    dve.tensor_tensor(out1, tr[:, 0, :], tr[:, 1, :], ALU.subtract)
    wait(dve, S[pa], at(done + 2))
    dve.tensor_tensor(out2, tr[:, 2, :], tr[:, 3, :], ALU.add).then_inc(S[pc], 1)


def attention1_pairs(env, block, S, g, PAIRS, UN, scale, wq, wo, q, k_, v, rope, lam, tr, ms, mix, pt, oT, sm):
    nc, X, xnT, bank, ident, band, sem, ins = (env[k] for k in ("nc", "X", "xnT", "bank", "ident", "band", "sem",
                                                                "ins"))

    def base(i, per):
        return i * per + g * PAIRS * per

    def keys(n):
        return (n, 1) if n % QB == 0 else (n - 1, 2)

    @block.sync
    def _(sp):
        wq_v = ins["L1_attn_Wq"].rearrange("(k p) n -> p k n", p=P)
        wo_v = ins["L1_attn_Wo"].rearrange("(h p) n -> p h n", p=P)
        with sp.Fori(0, PAIRS) as i:
            col = sp.snap(i * 2 * P + g * PAIRS * 2 * P)
            head = sp.snap(i * 2 + g * PAIRS * 2)
            wait(sp, S["y"], base(i, NT))
            sp.dma_start(wq[:, :, :], wq_v[:, :, ds(col, 2 * P)]).then_inc(S["w"], 16)
            sp.dma_start(wo[:, :, :], wo_v[:, ds(head, 2), :]).then_inc(S["w"], 16)
        wait(sp, S["w"], 32 * PAIRS * (g + 1))

    @block.tensor
    def _(pe):
        with pe.Fori(0, PAIRS) as i:
            wait(pe, S["w"], base(i, 32) + 32)
            for c in range(NC):
                wait(pe, S["roped"], base(i, NC) + c - 1)
                for a in range(2):
                    for k in range(KD):
                        mm = pe.matmul(bank[:, 2 * (c % 2) + a, :], wq[:, k, a * P:(a + 1) * P],
                                       xnT[:, k, c * CH:(c + 1) * CH], start=(k == 0), stop=(k == KD - 1))
                mm.then_inc(S["qproj"], 1)

            def scores(u):
                n, h = u // 2, u % 2
                k0, kn = keys(n)
                rows = slice(SUB * h, SUB * (h + 1))
                if u % 8 == 0:
                    wait(pe, S["roped"], base(i, NC) + n // 4 + 1)
                if u < 2:
                    wait(pe, S["roped"], base(i, NC) + NC)
                wait(pe, S["masked"], base(i, UN) + u - 1)
                for a in range(2):
                    mm = pe.matmul(bank[:, u % 2, a * 2 * P:a * 2 * P + kn * P], q[rows, a, n * P:(n + 1) * P],
                                   k_[rows, a, k0 * P:(k0 + kn) * P], start=True, stop=True)
                mm.then_inc(S["scores"], 1)

            def turn(u):
                kn = keys(u // 2)[1]
                wait(pe, S["probs"], base(i, UN) + u + 1)
                wait(pe, S["pt"], base(i, UN) + u - 1)
                for m in range(kn):
                    mm = pe.transpose(bank[:, 2 + u % 2, m * P:(m + 1) * P], mix[:, u % 4, m * P:(m + 1) * P], ident)
                mm.then_inc(S["turned"], 1)

            def weigh(u):
                n, h = u // 2, u % 2
                k0, kn = keys(n)
                wait(pe, S["pt"], base(i, UN) + u + 1)
                wait(pe, S["ot"], base(i, UN) + u - 1)
                for m in range(kn):
                    mm = pe.matmul(bank[:, 4 + u % 2, 0:P], v[:, k0 + m, h * P:(h + 1) * P],
                                   pt[:, u % 2, m * P:(m + 1) * P], start=(m == 0), stop=(m == kn - 1))
                mm.then_inc(S["pv"], 1)

            def project(n):
                wait(pe, S["ot"], base(i, UN) + 2 * n + 2)
                wait(pe, S["added"], base(i, NT) + n - 1)
                for h in range(2):
                    mm = pe.matmul(bank[:, 6 + n % 2, :], oT[:, n % 2, h, :], wo[:, h, :], start=(h == 0), stop=(h == 1))
                mm.then_inc(S["y"], 1)

            for s in range(UN + 6):
                if s < UN:
                    scores(s)
                if 3 <= s < UN + 3:
                    turn(s - 3)
                if 4 <= s < UN + 4:
                    weigh(s - 4)
                if s >= 7 and s % 2 == 1:
                    project((s - 7) // 2)

    @block.vector
    def _(dve):
        with dve.Fori(0, PAIRS) as i:
            for c in range(NC):
                wait(dve, S["qproj"], base(i, NC) + c + 1)
                if c == 0:
                    wait(dve, S["scores"], base(i, UN))
                wait(dve, S["roped"], base(i, NC) + c)
                rotate(dve, S, bank[:, 2 * (c % 2), :], bank[:, 2 * (c % 2) + 1, :],
                       q[:, 0, c * CH:(c + 1) * CH], q[:, 1, c * CH:(c + 1) * CH],
                       rope[:, 0, (c % 2) * CH:(c % 2 + 1) * CH], rope[:, 1, (c % 2) * CH:(c % 2 + 1) * CH], tr,
                       2 * c, lambda n: base(i, 2 * NC) + n, names=("sin", "roped"))

            def mask(u):
                kn = keys(u // 2)[1]
                w = kn * P
                wait(dve, S["mixed"], base(i, UN) + u - 3)
                wait(dve, S["scores"], base(i, UN) + u + 1)
                dve.memset(sm[:, u % 4, 11:12], 0.0).then_inc(S["cleared"], 1)
                for a in range(2):
                    m = dve.tensor_tensor_reduce(ms[:, u % 4, a, 0:w], bank[:, u % 2, a * 2 * P:a * 2 * P + w],
                                                 band[:, 2 * P - w:2 * P], scale, -3e38, ALU.add, ALU.max,
                                                 sm[:, u % 4, a:a + 1])
                m.then_inc(S["masked"], 1)
                wait(dve, S["masked"], base(i, UN) + u + 1)
                dve.tensor_scalar(sm[:, u % 4, 2:4], sm[:, u % 4, 0:2], -1.0, None, ALU.mult).then_inc(S["negmax"], 1)

            def combine(u):
                n, h = u // 2, u % 2
                w = keys(n)[1] * P
                b = sm[:, u % 4, :]
                wait(dve, S["exps"], base(i, UN) + u + 1)
                dve.reciprocal(b[:, 6:7], b[:, 5:6]).then_inc(S["recip2"], 1)
                wait(dve, S["recip2"], base(i, UN) + u + 1)
                dve.scalar_tensor_tensor(out=b[:, 7:8], in0=b[:, 4:5], scalar=b[:, 6:7],
                                         in1=nlam(i, h), op0=ALU.mult, op1=ALU.mult).then_inc(S["coef"], 1)
                wait(dve, S["coef"], base(i, UN) + u + 1)
                wait(dve, S["turned"], base(i, UN) + u - 3)
                dve.scalar_tensor_tensor(out=mix[:, u % 4, 0:w], in0=ms[:, u % 4, 1, 0:w], scalar=b[:, 7:8],
                                         in1=ms[:, u % 4, 0, 0:w], op0=ALU.mult, op1=ALU.add).then_inc(S["mixed"], 1)

            def normalise(u):
                w = keys(u // 2)[1] * P
                b = sm[:, u % 4, :]
                wait(dve, S["relu"], base(i, UN) + u + 1)
                dve.scalar_tensor_tensor(out=b[:, 9:10], in0=b[:, 4:5], scalar=1e-6, in1=b[:, 8:9],
                                         op0=ALU.mult, op1=ALU.add).then_inc(S["den"], 1)
                wait(dve, S["den"], base(i, UN) + u + 1)
                dve.reciprocal(b[:, 10:11], b[:, 9:10]).then_inc(S["recipd"], 1)
                wait(dve, S["recipd"], base(i, UN) + u + 1)
                dve.tensor_scalar(mix[:, u % 4, 0:w], mix[:, u % 4, 0:w], b[:, 10:11], None,
                                  ALU.mult).then_inc(S["probs"], 1)

            def take(u):
                w = keys(u // 2)[1] * P
                wait(dve, S["turned"], base(i, UN) + u + 1)
                wait(dve, S["pv"], base(i, UN) + u - 1)
                dve.tensor_copy(pt[:, u % 2, 0:w], bank[:, 2 + u % 2, 0:w]).then_inc(S["pt"], 1)

            def add(n):
                wait(dve, S["y"], base(i, NT) + n + 1)
                dve.tensor_tensor(X[:, n, :], X[:, n, :], bank[:, 6 + n % 2, :], ALU.add).then_inc(S["added"], 1)

            def nlam(i, h):
                return lam[:, ds(i + (2 * g * PAIRS + h * PAIRS), 1)]

            for s in range(UN + 7):
                if s < UN:
                    mask(s)
                if 1 <= s <= UN:
                    combine(s - 1)
                if 2 <= s < UN + 2:
                    normalise(s - 2)
                if 3 <= s < UN + 3:
                    take(s - 3)
                if s >= 8 and s % 2 == 0:
                    add((s - 8) // 2)

    @block.scalar
    def _(act):
        with act.Fori(0, PAIRS) as i:
            for s in range(UN + 5):
                if s < UN:
                    u = s
                    w = keys(u // 2)[1] * P
                    wait(act, S["negmax"], base(i, UN) + u + 1)
                    for a in range(2):
                        ex = act.activation(ms[:, u % 4, a, 0:w], ms[:, u % 4, a, 0:w], ACT.Exp,
                                            bias=sm[:, u % 4, 2 + a:3 + a], accum_out=sm[:, u % 4, 4 + a:5 + a])
                    ex.then_inc(S["exps"], 1)
                if 1 <= s <= UN:
                    u = s - 1
                    w = keys(u // 2)[1] * P
                    wait(act, S["mixed"], base(i, UN) + u + 1)
                    act.activation(mix[:, u % 4, 0:w], mix[:, u % 4, 0:w], ACT.Relu,
                                   accum_out=sm[:, u % 4, 8:9]).then_inc(S["relu"], 1)
                if s >= 5:
                    u = s - 5
                    n, h = u // 2, u % 2
                    wait(act, S["pv"], base(i, UN) + u + 1)
                    wait(act, S["y"], base(i, NT) + n - 1)
                    act.activation(oT[:, n % 2, h, :], bank[:, 4 + u % 2, 0:P], ACT.Copy).then_inc(S["ot"], 1)


def feed_forward1(env, r):
    nc, sem, sb, ins = (env[k] for k in ("nc", "sem", "sb", "ins"))
    HT = FS // P
    with ExitStack() as ctx:
        loaded = sem("f1_loaded")
        wg = sb(ctx, "wsg", [P, KD, FS])
        wu = sb(ctx, "wsu", [P, KD, FS])
        wd = sb(ctx, "wsd", [P, HT, D])
        hid = sb(ctx, "hid1", [P, 2, CH])
        sg = sb(ctx, "sg1", [P, 2, CH])
        with nc.Block() as block:
            @block.sync
            def _(sp):
                sp.dma_start(wg[:, :, :], ins["L1_ffn_Wsg"].rearrange("(k p) h -> p k h", p=P)).then_inc(loaded, 16)
                sp.dma_start(wu[:, :, :], ins["L1_ffn_Wsu"].rearrange("(k p) h -> p k h", p=P)).then_inc(loaded, 16)
                sp.dma_start(wd[:, :, :], ins["L1_ffn_Wsd"].rearrange("(h p) d -> p h d", p=P)).then_inc(loaded, 16)
                sp.wait_ge(loaded, 48)
            swiglu_chunks(env, "1", block, HT, wg, wu, wd, hid, sg, loaded, 48, gate=r["gshared"])


def experts(env):
    nc, bank, ident, sb, ins, S = (env[k] for k in ("nc", "bank", "ident", "sb", "ins", "e"))
    FP = FT1 * P
    NB = 4
    FULL = (FT1 - 1) * P
    with ExitStack() as ctx:
        wg = sb(ctx, "ewg", [P, NB, KD, FP])
        wu = sb(ctx, "ewu", [P, NB, KD, FP])
        wd = sb(ctx, "ewd", [P, NB, FT1, D])
        xr = sb(ctx, "exr", [P, 2, D])
        xT = sb(ctx, "exT", [P, 2, KD, P])
        sg = sb(ctx, "esg", [P, 2, FT1, CAP])
        hT = sb(ctx, "ehT", [P, 2, FT1, CAP])
        ys = sb(ctx, "eys", [CAP, 2, D])
        with nc.Block() as block:
            @block.gpsimd
            def _(pool):
                pool.memset(wg[:, :, :, F1:], 0.0).then_inc(S["zeroed"], 1)
                pool.memset(wu[:, :, :, F1:], 0.0).then_inc(S["zeroed"], 1)
                wait(pool, S["zeroed"], 2)
                pool.memset(wd[F1R:, :, FT1 - 1, :], 0.0).then_inc(S["zeroed"], 1)

            @block.sync
            def _(sp):
                with sp.Fori(0, E // NB) as i:
                    pair = [sp.snap(i * NB * CAP + p * P) for p in range(NB // 2)]
                    expert = [sp.snap(i * NB + j) for j in range(NB)]
                    for j in range(NB):
                        if j % 2 == 0:
                            wait(sp, S["xt"], i * (NB // 2) + j // 2 - 1)
                            sp.dma_start(xr[:, j // 2, :], env["xe"][ds(pair[j // 2], P), :]).then_inc(
                                S[f"xloaded{j // 2}"], 16)
                        wait(sp, S["y"], i * NB + j - (NB - 1))
                        s = S[f"wloaded{j}"]
                        for dst, name in ((wg, "Wg"), (wu, "Wu")):
                            sp.dma_start(dst[:, j, :, 0:F1], ins["L1_ffn_" + name][ds(expert[j], 1), :, :].rearrange(
                                "a (k p) f -> p (a k) f", p=P)).then_inc(s, 16)
                        down = ins["L1_ffn_Wd"][ds(expert[j], 1), :, :]
                        sp.dma_start(wd[:, j, 0:FT1 - 1, :], down[:, 0:FULL, :].rearrange(
                            "a (t p) d -> p (a t) d", p=P)).then_inc(s, 16)
                        sp.dma_start(wd[0:F1R, j, FT1 - 1, :], down[:, FULL:F1, :].rearrange(
                            "a p d -> p (a d)")).then_inc(s, 16)

            @block.tensor
            def _(pe):
                wait(pe, S["zeroed"], 3)
                with pe.Fori(0, E // NB) as i:
                    def turn(p):
                        wait(pe, S[f"xloaded{p}"], i * 16 + 16)
                        wait(pe, S["xt_s"], i * (NB // 2) + p - 1)
                        for k in range(KD):
                            mm = pe.transpose(bank[:, p, k * P:(k + 1) * P], xr[:, p, k * P:(k + 1) * P], ident)
                        mm.then_inc(S["xt"], 1)

                    def up(j):
                        if j % 2 == 0:
                            wait(pe, S["xt_s"], i * (NB // 2) + j // 2 + 1)
                        wait(pe, S[f"wloaded{j}"], i * 64 + 64)
                        wait(pe, S["hidden"], i * NB + j - 1)
                        for a, w in ((0, wg), (1, wu)):
                            for t in range(FT1):
                                for k in range(KD):
                                    mm = pe.matmul(bank[:, 2 + j % 2, (a * FT1 + t) * CAP:(a * FT1 + t + 1) * CAP],
                                                   w[:, j, k, t * P:(t + 1) * P],
                                                   xT[:, j // 2, k, (j % 2) * CAP:(j % 2 + 1) * CAP],
                                                   start=(k == 0), stop=(k == KD - 1))
                        mm.then_inc(S["up"], 1)

                    def down(j):
                        wait(pe, S["hidden"], i * NB + j + 1)
                        wait(pe, S["y_s"], i * NB + j - 1)
                        for t in range(FT1):
                            mm = pe.matmul(bank[0:CAP, 4 + j % 2, :], hT[:, j % 2, t, :], wd[:, j, t, :],
                                           start=(t == 0), stop=(t == FT1 - 1))
                        mm.then_inc(S["y"], 1)

                    turn(0)
                    for j in range(NB):
                        up(j)
                        if j == 0:
                            turn(1)
                        if j:
                            down(j - 1)
                    down(NB - 1)

            @block.scalar
            def _(act):
                with act.Fori(0, E // NB) as i:
                    rows = [act.snap(i * NB * CAP + j * CAP) for j in range(NB)]

                    def sigmoid(j):
                        wait(act, S["up"], i * NB + j + 1)
                        wait(act, S["gated"], i * NB + j - 1)
                        act.activation(sg[:, j % 2], bank[:, 2 + j % 2, 0:FT1 * CAP].rearrange("p (t c) -> p t c", c=CAP),
                                       ACT.Sigmoid).then_inc(S["sig"], 1)

                    def store(j):
                        wait(act, S["y"], i * NB + j + 1)
                        wait(act, S[f"stored{j % 2}"], i * (NB // 2) * 16 + (j // 2) * 16)
                        act.activation(ys[:, j % 2, :], bank[0:CAP, 4 + j % 2, :], ACT.Copy).then_inc(S["y_s"], 1)
                        wait(act, S["y_s"], i * NB + j + 1)
                        act.dma_start(env["ye"][ds(rows[j], CAP), :], ys[:, j % 2, :]).then_inc(S[f"stored{j % 2}"], 16)

                    for j in range(NB):
                        sigmoid(j)
                        if j:
                            store(j - 1)
                    store(NB - 1)
                for p in range(2):
                    wait(act, S[f"stored{p}"], 16 * E // 2)

            @block.vector
            def _(dve):
                with dve.Fori(0, E // NB) as i:
                    def rows(p):
                        wait(dve, S["xt"], i * (NB // 2) + p + 1)
                        wait(dve, S["up"], i * NB + 2 * p - 2)
                        dve.tensor_copy(xT[:, p], bank[:, p, :].rearrange("p (k c) -> p k c", k=KD)).then_inc(S["xt_s"], 1)

                    rows(0)
                    for j in range(NB):
                        wait(dve, S["sig"], i * NB + j + 1)
                        wait(dve, S["y"], i * NB + j - 1)
                        g = bank[:, 2 + j % 2, 0:FT1 * CAP].rearrange("p (t c) -> p t c", c=CAP)
                        u = bank[:, 2 + j % 2, FT1 * CAP:2 * FT1 * CAP].rearrange("p (t c) -> p t c", c=CAP)
                        dve.tensor_tensor(hT[:, j % 2], g, sg[:, j % 2], ALU.mult).then_inc(S["gated"], 1)
                        wait(dve, S["gated"], i * NB + j + 1)
                        dve.tensor_tensor(hT[:, j % 2], u, hT[:, j % 2], ALU.mult).then_inc(S["hidden"], 1)
                        if j == 0:
                            rows(1)


def combine(env, r):
    nc, X, sem, sb = (env[k] for k in ("nc", "X", "sem", "sb"))
    G = 4
    cleared, got, used, stored = sem("c_clear"), [sem(f"c_got{s}") for s in range(G)], sem("c_used"), sem("c_stored")
    out_v = env["out"].rearrange("b (n p) d -> p (b n) d", p=P)
    with ExitStack() as ctx:
        y = sb(ctx, "cy", [P, G, TOPK, D])
        with nc.Block() as block:
            @block.scalar
            def _(act):
                pass

            @block.gpsimd
            def _(pool):
                for n in range(NT):
                    if n >= G:
                        pool.wait_ge(used, TOPK * (n - G + 1))
                    pool.memset(y[:, n % G], 0.0).then_inc(cleared, 1)
                    pool.wait_ge(cleared, n + 1)
                    for k in range(TOPK):
                        pool.indirect_dma_start(y[:, n % G, k, :], None, env["ye"],
                                                bass.IndirectOffsetOnAxis(ap=r["slot"][:, n, k:k + 1], axis=0),
                                                bounds_check=SLOTS - 1, oob_is_err=False).then_inc(got[n % G], 16)

            @block.vector
            def _(dve):
                for n in range(NT):
                    dve.wait_ge(got[n % G], 16 * TOPK * (n // G + 1))
                    for k in range(TOPK):
                        if k:
                            dve.wait_ge(used, TOPK * n + k)
                        dve.scalar_tensor_tensor(out=X[:, n, :], in0=y[:, n % G, k, :], scalar=r["wk"][:, n, k:k + 1],
                                                 in1=X[:, n, :], op0=ALU.mult, op1=ALU.add).then_inc(used, 1)

            @block.sync
            def _(sp):
                for n in range(NT):
                    sp.wait_ge(used, TOPK * (n + 1))
                    sp.dma_start(out_v[:, n, :], X[:, n, :]).then_inc(stored, 16)
                sp.wait_ge(stored, 16 * NT)


_INS = ['L0_attn_x', 'L0_attn_W_q', 'L0_attn_W_k', 'L0_attn_W_v', 'L0_attn_W_o', 'L0_ffn_W1', 'L0_ffn_W2',
        'L0_ffn_W3', 'L1_attn_Wq', 'L1_attn_Wk', 'L1_attn_Wv', 'L1_attn_Wo', 'L1_attn_lam', 'L1_ffn_Wr', 'L1_ffn_Wg',
        'L1_ffn_Wu', 'L1_ffn_Wd', 'L1_ffn_Wsg', 'L1_ffn_Wsu', 'L1_ffn_Wsd', 'L1_ffn_Wse']


def _lay_out(name, a):
    import numpy as _np
    if name in ("L0_ffn_W1", "L0_ffn_W2", "L0_ffn_W3"):
        a = a.T
    if name == "L1_attn_Wq":
        a = a.reshape(512, 2, 2, 4, 2, 64).transpose(0, 1, 3, 4, 2, 5).reshape(512, 2048)
    if name == "L1_attn_Wk":
        a = a.reshape(512, 2, 2, 2, 64).transpose(0, 1, 3, 2, 4).reshape(512, 512)
    if name == "L1_attn_Wo":
        a = a.reshape(2, 2, 4, 128, 512).transpose(0, 2, 1, 3, 4).reshape(2048, 512)
    return _np.ascontiguousarray(a)


def kernel(**inputs):
    import numpy as _np
    import concourse.bacc as _bacc
    from concourse import mybir as _mybir
    from concourse.bass_utils import run_bass_kernel_spmd as _run

    nc = _bacc.Bacc("TRN2", target_bir_lowering=False, num_devices=1)
    arrays, args = {}, {}
    for name in _INS:
        a = _lay_out(name, _np.asarray(inputs[name]))
        arrays[f"in_{name}_dram"] = a
        args[name] = nc.dram_tensor(f"in_{name}_dram", a.shape, _mybir.dt.from_np(a.dtype), kind="ExternalInput").ap()
    out = nc.dram_tensor("out_0_dram", (BATCH, SEQ, D), F32, kind="ExternalOutput").ap()
    build(nc, args, out)
    r = _run(nc, [arrays], core_ids=[0])
    return r.results[0]["out_0_dram"]
```

```python
from contextlib import ExitStack

import numpy as np

import concourse.bass as bass
from concourse import mybir

F32 = mybir.dt.float32
F32R = mybir.dt.float32r
U32 = mybir.dt.uint32
ALU = mybir.AluOpType
ACT = mybir.ActivationFunctionType
AX = mybir.AxisListType

P = 128
BATCH, SEQ, D = 2, 1024, 512
T = BATCH * SEQ
NT = T // P
KD = D // P
CH = 512
NC = T // CH
EPS = 1e-5

H0, KV0, HD0 = 16, 4, 32
QT0 = H0 * HD0 // P
HPT = P // HD0
QB = SEQ // P
UN0 = QT0 * HPT
F0 = 2048
H1, KV1, HD1, SUB = 16, 4, 128, 64
WINDOW = 128
NEG = -1e30
E, TOPK, CAP, F1, FS = 32, 4, 64, 352, 1408
SLOTS = E * CAP
FT1 = (F1 + P - 1) // P
F1R = F1 - (FT1 - 1) * P
CREDIT = 64
OOB = 1 << 20


SIGNALS = {
    "p0": "w proj read cos sin rotated hi lo v_rows v_taken",
    "h0": "k_loaded q_loaded0 q_loaded1 const peaks max neg neg_rows shift scored exps weighed rec normed "
          "o_taken y added",
    "f0": "raw hi split up sig gated hidden hid_hi parts y added x_hi x_lo",
    "h1": "w wo kw vw proj cos sin roped scores masked exps recip2 coef cleared mixed den recipd qproj relu probs "
          "turned pt pv ot y added vrows vtaken lam qdone",
    "f1": "raw hi split up sig gated hidden hid_hi parts y added x_hi x_lo",
    "e": "wloaded0 wloaded1 wloaded2 wloaded3 dloaded0 dloaded1 dloaded2 dloaded3 "
         "xloaded0 xloaded1 xt xt_s up sig gated hidden y y_s stored0 stored1 "
         "zeroed",
}


def ds(start, n):
    return bass.ds(start, n)


def shape_constants():
    pos = np.arange(SEQ, dtype=np.float32)
    half = HD0 // 2
    freq = np.float32(1.0) / np.power(np.float32(10000.0), np.arange(half, dtype=np.float32) / np.float32(half))
    ang = pos[:, None] * freq[None, :].astype(np.float32)
    c, s = np.cos(ang).astype(np.float32), np.sin(ang).astype(np.float32)
    cos0 = np.tile(np.repeat(c.T, 2, axis=0), (HPT, 1))
    sgn = np.tile(np.array([-1.0, 1.0], np.float32), P // 2)[:, None]
    sin0 = np.tile(np.repeat(s.T, 2, axis=0), (HPT, 1)) * sgn
    inv = np.float32(1.0) / np.power(np.float32(10000.0), np.arange(0, HD1, 2, dtype=np.float32) / np.float32(HD1))
    ang1 = pos[:, None] * inv[None, :].astype(np.float32)
    cos1 = np.tile(np.cos(ang1).astype(np.float32).T, (2, 1))
    sin1 = np.tile(np.sin(ang1).astype(np.float32).T, (2, 1))
    h = np.array([[1.0]], np.float32)
    while h.shape[0] < P:
        h = np.block([[h, h], [h, -h]])
    q, k = np.arange(P)[:, None], np.arange(P)[None, :]
    band = np.concatenate([np.where(k > q, 0.0, NEG), np.where(k <= q, 0.0, NEG)], axis=1)
    before = (q < k).astype(np.float32)
    misc = np.concatenate([np.eye(P), h, band, before, np.ones((P, P))], axis=1)
    expert = np.tile(np.arange(E, dtype=np.float32), (P, NT, 1)).reshape(P, NT * E)
    f = np.float32
    return {"rope0": np.ascontiguousarray(np.concatenate([cos0, sin0], axis=1), f),
            "rope1": np.ascontiguousarray(np.concatenate([cos1, sin1], axis=1), f),
            "misc": np.ascontiguousarray(misc, f),
            "blocks": np.ascontiguousarray(np.eye(P // 4, CH // P).repeat(P, axis=1), f), "expert": np.ascontiguousarray(expert, f)}


def build(nc, ins, out):
    consts = {k: nc.inline_tensor(v, name="c_" + k) for k, v in shape_constants().items()}
    consts = {k: (v if isinstance(v, bass.AP) else v.ap()) for k, v in consts.items()}
    xe_dram = nc.dram_tensor("xe_dram", [SLOTS, D], F32).ap()
    ye_dram = nc.dram_tensor("ye_dram", [SLOTS, D], F32).ap()

    with ExitStack() as top:
        used = {}

        def sb(ctx, name, shape, dt=F32):
            used[name] = used.get(name, 0) + 1
            return ctx.enter_context(nc.sbuf_tensor(name if used[name] == 1 else f"{name}_{used[name]}", shape, dt))

        def sem(name):
            return top.enter_context(nc.semaphore(name))

        bank = top.enter_context(nc.psum_tensor("bank", [P, 8, 512], F32))
        X = sb(top, "X", [P, NT, D])
        xnT = sb(top, "xnT", [P, KD, T])
        misc = sb(top, "misc", [P, 6 * P])
        ident, had, band = misc[:, 0:P], misc[:, P:2 * P], misc[:, 2 * P:4 * P]
        before, ones = misc[:, 4 * P:5 * P], misc[:, 5 * P:6 * P]
        env = dict(nc=nc, ins=ins, out=out, sb=sb, sem=sem, bank=bank, X=X, xnT=xnT, ident=ident, had=had,
                   band=band, before=before, ones=ones, consts=consts, misc=misc, xe=xe_dram, ye=ye_dram)
        env.update({kind: {n: sem(f"{kind}_{n}") for n in names.split()} for kind, names in SIGNALS.items()})
        layer_norm(env, "0", first=True)
        attention0(env)
        feed_forward0(env)
        with ExitStack() as moe:
            r = dict(slot=sb(moe, "slot", [P, NT, TOPK], U32), wk=sb(moe, "wk", [P, NT, TOPK]),
                     gshared=sb(moe, "gshared", [P, NT]))
            with ExitStack() as rows:
                r["xn"] = sb(rows, "xn_rows", [P, NT, D])
                layer_norm(env, "1", rows=r["xn"])
                route(env, r)
                attention1(env, r)
            feed_forward1(env, r)
            experts(env)
            combine(env, r)


def layer_norm(env, tag, first=False, rows=None):
    nc, X, xnT, bank, ident = env["nc"], env["X"], env["xnT"], env["bank"], env["ident"]
    sem = env["sem"]
    consts_loaded, x_loaded = sem("ln_consts" + tag), [sem(f"ln_x{tag}_{c}") for c in range(4)]
    stats_done, aggr_done, var_done, sd_done, rstd_done = (sem(f"ln_{n}{tag}") for n in
                                                           ("stats", "aggr", "var", "sd", "rstd"))
    xn_ready, xt_ready, xt_taken = (sem(f"ln_{n}{tag}") for n in ("xn", "xt", "taken"))
    QL = len(x_loaded)
    with ExitStack() as ctx:
        stats = env["sb"](ctx, "ln_stats" + tag, [P, NT, 6])
        mv = env["sb"](ctx, "ln_mv" + tag, [P, NT, 2])
        sd = env["sb"](ctx, "ln_sd" + tag, [P, 2, NT])
        xn = rows if rows is not None else env["sb"](ctx, "ln_xn" + tag, [P, 2, D])
        slots = NT if rows is not None else 2
        block = ctx.enter_context(nc.Block())

        if first:
            @block.gpsimd
            def _(pool):
                for kind in SIGNALS:
                    for s in env[kind].values():
                        pool.sem_inc(s, CREDIT)

            @block.sync
            def _(sp):
                src = env["ins"]["L0_attn_x"].rearrange("b (n p) d -> p (b n) d", p=P)
                sp.dma_start(env["misc"][:, :], env["consts"]["misc"]).then_inc(consts_loaded, 16)
                for c in range(QL):
                    n = NT // QL
                    sp.dma_start(X[:, c * n:(c + 1) * n, :], src[:, c * n:(c + 1) * n, :]).then_inc(x_loaded[c], 16)

        @block.vector
        def _(dve):
            for n in range(NT):
                if first and n % (NT // QL) == 0:
                    dve.wait_ge(x_loaded[n // (NT // QL)], 16)
                dve.bn_stats(stats[:, n, :], X[:, n, :]).then_inc(stats_done, 1)
            for n in range(NT):
                dve.wait_ge(stats_done, n + 1)
                dve.bn_aggr(mv[:, n, :], stats[:, n, :]).then_inc(aggr_done, 1)
            dve.wait_ge(aggr_done, NT)
            dve.tensor_scalar(sd[:, 0, :], mv[:, :, 1], EPS, None, ALU.add).then_inc(var_done, 1)
            dve.wait_ge(sd_done, 1)
            dve.reciprocal(sd[:, 0, :], sd[:, 1, :]).then_inc(rstd_done, 1)
            dve.wait_ge(rstd_done, 1)
            for n in range(NT):
                if n >= slots:
                    dve.wait_ge(xt_ready, n - slots + 1)
                dve.tensor_scalar(xn[:, n % slots, :], X[:, n, :], mv[:, n, 0:1], sd[:, 0, n:n + 1],
                                  ALU.subtract, ALU.mult).then_inc(xn_ready, 1)

        @block.tensor
        def _(pe):
            if first:
                pe.wait_ge(consts_loaded, 16)
            for n in range(NT):
                pe.wait_ge(xn_ready, n + 1)
                if n >= 4:
                    pe.wait_ge(xt_taken, n - 3)
                for k in range(KD):
                    mm = pe.transpose(bank[:, n % 4, k * P:(k + 1) * P], xn[:, n % slots, k * P:(k + 1) * P], ident)
                mm.then_inc(xt_ready, 1)

        @block.scalar
        def _(act):
            act.wait_ge(var_done, 1)
            act.activation(sd[:, 1, :], sd[:, 0, :], ACT.Sqrt).then_inc(sd_done, 1)
            for n in range(NT):
                act.wait_ge(xt_ready, n + 1)
                act.activation(xnT[:, :, n * P:(n + 1) * P], bank[:, n % 4, :].rearrange("p (k t) -> p k t", k=KD),
                               ACT.Copy).then_inc(xt_taken, 1)


def wait(engine, signal, count):
    engine.wait_ge(signal, count + CREDIT)


def attention0(env):
    nc, sb, ins = (env[k] for k in ("nc", "sb", "ins"))
    NF = QT0 + 2
    with ExitStack() as ctx:
        t = dict(q_hi=sb(ctx, "q_hi", [P, QT0, SEQ], F32R), q_lo=sb(ctx, "q_lo", [P, QT0, SEQ], F32R),
                 k_hi=sb(ctx, "k_hi", [P, SEQ], F32R), k_lo=sb(ctx, "k_lo", [P, SEQ], F32R),
                 v=sb(ctx, "v0", [P, QB, KV0, HD0]), wo=sb(ctx, "wo0", [P, KD, D]))
        for b in range(BATCH):
            with ExitStack() as c2:
                w = sb(c2, "wqkv", [P, KD, NF * P])
                rope = sb(c2, "rope0", [P, 2, SEQ])
                project0(env, c2, b, t, w, rope, NF)
            heads0(env, b, t)


def project0(env, ctx, b, t, w, rope, NF):
    nc, xnT, bank, ident, sb, ins, S = (env[k] for k in ("nc", "xnT", "bank", "ident", "sb", "ins", "p0"))
    swapped = sb(ctx, "swapped", [P, 2, CH])
    direct = sb(ctx, "direct", [P, 2, CH])
    rot = sb(ctx, "rot", [P, 2, CH])
    vT = sb(ctx, "vT", [P, CH])
    HALVES, NR = SEQ // CH, NF - 1
    loads = 4 + (b == 0)
    loaded = 16 * (loads + (5 if b else 0))

    def turn(i, per):
        return (i + b * HALVES) * per

    with nc.Block() as block:
        @block.sync
        def _(sp):
            for c0, c1, name in ((0, D, "W_q"), (D, D + P, "W_k"), (D + P, D + 2 * P, "W_v")):
                sp.dma_start(w[:, :, c0:c1], ins["L0_attn_" + name].rearrange("(k p) n -> p k n", p=P)).then_inc(S["w"], 16)
            sp.dma_start(rope[:, :, :], env["consts"]["rope0"].rearrange("p (a s) -> p a s", a=2)).then_inc(S["w"], 16)
            if b == 0:
                sp.dma_start(t["wo"][:, :, :], ins["L0_attn_W_o"].rearrange("(k p) n -> p k n", p=P)).then_inc(S["w"], 16)
            wait(sp, S["w"], loaded)

        @block.tensor
        def _(pe):
            wait(pe, S["w"], loaded)
            with pe.Fori(0, HALVES) as h:
                for f in range(NF):
                    wait(pe, S["read"], turn(h, NF) + f - (1 if f < NF - 4 else 3))
                    for k in range(KD):
                        mm = pe.matmul(bank[:, f % 4, :], w[:, k, f * P:(f + 1) * P],
                                       xnT[:, k, ds(h * CH + b * SEQ, CH)], start=(k == 0), stop=(k == KD - 1))
                    mm.then_inc(S["proj"], 1)
                wait(pe, S["read"], turn(h, NF) + NF)
                wait(pe, S["v_taken"], turn(h, 1))
                for s in range(CH // P):
                    mm = pe.transpose(bank[:, 6, s * P:(s + 1) * P], vT[:, s * P:(s + 1) * P], ident)
                mm.then_inc(S["v_rows"], 1)

        @block.vector
        def _(dve):
            wait(dve, S["w"], loaded)
            with dve.Fori(0, HALVES) as h:
                for f in range(NF):
                    wait(dve, S["proj"], turn(h, NF) + f + 1)
                    if f == NR:
                        wait(dve, S["v_rows"], turn(h, 1))
                        dve.tensor_copy(vT[:, :], bank[:, f % 4, :]).then_inc(S["read"], 1)
                        continue
                    n = turn(h, NR) + f
                    wait(dve, S["rotated"], n)
                    dve.tensor_tensor(direct[:, f % 2, :], bank[:, f % 4, :], rope[:, 0, ds(h * CH, CH)],
                                      ALU.mult).then_inc(S["cos"], 1)
                    dve.stream_shuffle(swapped[:, f % 2, :], bank[:, f % 4, :],
                                       [i ^ 1 for i in range(32)]).then_inc(S["read"], 1)
                    wait(dve, S["read"], turn(h, NF) + f + 1)
                    dve.tensor_tensor(swapped[:, f % 2, :], swapped[:, f % 2, :], rope[:, 1, ds(h * CH, CH)],
                                      ALU.mult).then_inc(S["sin"], 1)
                    wait(dve, S["sin"], n + 1)
                    wait(dve, S["lo"], n - 1 if f else n)
                    dve.tensor_tensor(rot[:, f % 2, :], direct[:, f % 2, :], swapped[:, f % 2, :],
                                      ALU.add).then_inc(S["rotated"], 1)

        def parts(f, h):
            at = ds(h * CH, CH)
            if f < QT0:
                return t["q_hi"][:, f, at], t["q_lo"][:, f, at]
            return t["k_hi"][:, at], t["k_lo"][:, at]

        @block.scalar
        def _(act):
            with act.Fori(0, HALVES) as h:
                for f in range(NR):
                    wait(act, S["rotated"], turn(h, NR) + f + 1)
                    act.activation(parts(f, h)[0], rot[:, f % 2, :], ACT.Copy).then_inc(S["hi"], 1)
                wait(act, S["v_rows"], turn(h, 1) + 1)
                act.activation(t["v"][:, ds(h * (CH // P), CH // P), :, :],
                               bank[:, 6, :].rearrange("p (s j d) -> p s j d", j=KV0, d=HD0),
                               ACT.Copy).then_inc(S["v_taken"], 1)

        @block.gpsimd
        def _(pool):
            with pool.Fori(0, HALVES) as h:
                for f in range(NR):
                    wait(pool, S["hi"], turn(h, NR) + f + 1)
                    hi, lo = parts(f, h)
                    pool.tensor_tensor(lo, rot[:, f % 2, :], hi.bitcast(F32), ALU.subtract).then_inc(S["lo"], 1)


def heads0(env, b, t):
    nc, X, bank, ident, ones, sb, S = (env[k] for k in ("nc", "X", "bank", "ident", "ones", "sb", "h0"))
    scale = float(HD0) ** -0.5
    CHUNKS, SUBS, STEPS = SEQ // CH, CH // P, QB // 2
    R = 3 * HD0
    GROUP = HPT
    LOADS = 3 * GROUP
    PAIRS = UN0 // 2
    with ExitStack() as ctx:
        qp = sb(ctx, "q_parts", [P, 2 * GROUP, CH], F32R)
        kp = sb(ctx, "k_parts", [P, KV0, SEQ], F32R)
        probs = sb(ctx, "probs", [P, 2, 2, 2, CH])
        mx = sb(ctx, "mx", [P, 2, SUBS, 2])
        neg = sb(ctx, "neg", [P, 2, P])
        o = sb(ctx, "o", [P, CH])
        rec = sb(ctx, "rec", [2 * HD0, CH])
        oT = sb(ctx, "oT", [P, KD, CH])
        blocks = sb(ctx, "blocks", [P, SUBS, P])

        def at(c, per):
            return (c + b * CHUNKS) * per

        with nc.Block() as block:
            @block.sync
            def _(sp):
                sp.dma_start(blocks[R:, :, :], env["consts"]["blocks"].rearrange("p (s q) -> p s q", s=SUBS)).then_inc(
                    S["k_loaded"], 16)
                for j in range(KV0):
                    for r, part in enumerate(("k_hi", "k_hi", "k_lo")):
                        sp.dma_start(kp[HD0 * r:HD0 * (r + 1), j, :].bitcast(F32),
                                     t[part][HD0 * j:HD0 * (j + 1), :].bitcast(F32)).then_inc(S["k_loaded"], 16)
                with sp.Fori(0, CHUNKS) as c:
                    for g in range(QT0):
                        wait(sp, S["scored"], at(c, UN0 * STEPS) + (g - 1) * GROUP * STEPS)
                        for j in range(GROUP):
                            for r, part in enumerate(("q_hi", "q_lo", "q_hi")):
                                sp.dma_start(qp[HD0 * r:HD0 * (r + 1), g % 2 * GROUP + j, :].bitcast(F32),
                                             t[part][HD0 * j:HD0 * (j + 1), g, ds(c * CH, CH)].bitcast(F32)).then_inc(
                                    S[f"q_loaded{g % 2}"], 16)

            @block.gpsimd
            def _(pool):
                pool.memset(kp[R:, :, :].bitcast(F32), 1.0).then_inc(S["const"], 1)
                wait(pool, S["const"], 2 * b + 1)
                pool.memset(neg[:, :, :], 0.0).then_inc(S["const"], 1)
                with pool.Fori(0, CHUNKS) as c:
                    for w in range(PAIRS):
                        j, k = 2 * w % HPT, 2 * w // HPT
                        wait(pool, S["rec"], at(c, PAIRS) + w + 1)
                        if w == 0:
                            wait(pool, S["y"], at(c, SUBS))
                        pool.tensor_tensor(oT[HD0 * j:HD0 * (j + 2), k, :], o[0:2 * HD0, :], rec[:, :],
                                           ALU.mult).then_inc(S["normed"], 1)

            def loaded(engine, c, u):
                g = u // GROUP
                wait(engine, S[f"q_loaded{g % 2}"], at(c, QT0 // 2 * 16 * LOADS) + (g // 2 + 1) * 16 * LOADS)

            @block.tensor
            def _(pe):
                wait(pe, S["k_loaded"], 16 * (1 + LOADS) * (b + 1))
                wait(pe, S["const"], 2 * (b + 1))
                with pe.Fori(0, CHUNKS) as c:
                    def peak(u, q, h):
                        if u >= UN0:
                            return
                        n = at(c, 2 * UN0 * SUBS) + 2 * (u * SUBS + q) + h
                        if q == 0 and h == 0 and u % GROUP == 0:
                            loaded(pe, c, u)
                        if u == 0 and q == 0:
                            wait(pe, S["added"], at(c, SUBS))
                        wait(pe, S["max"], n - 1)
                        pe.matmul(bank[:, h, :], qp[0:R, u % (2 * GROUP), q * P:(q + 1) * P],
                                  kp[0:R, u % KV0, h * CH:(h + 1) * CH], start=True, stop=True).then_inc(S["peaks"], 1)

                    def turn_max(u):
                        if u >= UN0:
                            return
                        wait(pe, S["neg"], at(c, UN0) + u + 1)
                        pe.transpose(bank[:, 7, 0:P], neg[:, u % 2, :], ident).then_inc(S["neg_rows"], 1)

                    def score(w, s, x):
                        n, u = at(c, UN0 * STEPS) + 2 * (w * STEPS + s) + x, 2 * w + x
                        if s == 0:
                            wait(pe, S["shift"], at(c, UN0) + u + 1)
                        wait(pe, S["exps"], n - 1)
                        for m in range(2):
                            kt = 2 * s + m
                            mm = pe.matmul(bank[:, 2 + 2 * x + m, :], kp[:, u % KV0, kt * P:(kt + 1) * P],
                                           qp[:, u % (2 * GROUP), :], start=True, stop=True)
                        mm.then_inc(S["scored"], 1)

                    def weigh(w, s):
                        wait(pe, S["exps"], at(c, UN0 * STEPS) + 2 * (w * STEPS + s) + 2)
                        if s == 0:
                            wait(pe, S["o_taken"], at(c, PAIRS) + w)
                        for m in range(2):
                            for x in range(2):
                                for row, left in ((HD0 * x, t["v"][:, 2 * s + m, (2 * w + x) % KV0, :]),
                                                  (HD0 * (2 + x), ones[:, 0:HD0])):
                                    mm = pe.matmul(bank[row:row + HD0, 6, :], left, probs[:, x, s % 2, m, :],
                                                   start=(s == 0 and m == 0), stop=(s == STEPS - 1 and m == 1),
                                                   skip_group_check=True)
                        mm.then_inc(S["weighed"], 1)

                    for x in range(2):
                        for q in range(SUBS):
                            peak(x, q, 0)
                            peak(x, q, 1)
                        if x == 0:
                            turn_max(0)
                    for w in range(PAIRS):
                        for s in range(STEPS):
                            u, q = 2 * w + 2 + s // 2, s % 2 * 2
                            peak(u, q, 0)
                            score(w, s, 0)
                            peak(u, q, 1)
                            if s == 0:
                                turn_max(2 * w + 1)
                            if s or w:
                                weigh(*((w, s - 1) if s else (w - 1, STEPS - 1)))
                            peak(u, q + 1, 0)
                            score(w, s, 1)
                            peak(u, q + 1, 1)
                            if s == 2:
                                turn_max(2 * w + 2)
                    weigh(PAIRS - 1, STEPS - 1)
                    wait(pe, S["normed"], at(c, PAIRS) + PAIRS)
                    for q in range(SUBS):
                        for k in range(KD):
                            mm = pe.matmul(bank[:, q, :], oT[:, k, q * P:(q + 1) * P], t["wo"][:, k, :],
                                           start=(k == 0), stop=(k == KD - 1))
                        mm.then_inc(S["y"], 1)

            @block.vector
            def _(dve):
                wait(dve, S["k_loaded"], 16 * (1 + LOADS) * (b + 1))
                wait(dve, S["const"], 2 * (b + 1))
                with dve.Fori(0, CHUNKS) as c:
                    def maximum(u, q, h):
                        if u >= UN0:
                            return
                        wait(dve, S["peaks"], at(c, 2 * UN0 * SUBS) + 2 * (u * SUBS + q) + h + 1)
                        dve.reduce_max(mx[:, u % 2, q, h:h + 1], bank[:, h, :], AX.X).then_inc(S["max"], 1)

                    def negate(u):
                        if u >= UN0:
                            return
                        wait(dve, S["max"], at(c, 2 * UN0 * SUBS) + 2 * (u + 1) * SUBS)
                        wait(dve, S["neg_rows"], at(c, UN0) + u)
                        dve.tensor_reduce(neg[:, u % 2, R:R + SUBS], mx[:, u % 2, :, :], AX.X, ALU.max,
                                          negate=True).then_inc(S["neg"], 1)

                    def shift(u):
                        if u >= UN0:
                            return
                        wait(dve, S["neg_rows"], at(c, UN0) + u + 1)
                        dve.tensor_tensor(qp[R:, u % (2 * GROUP), :].rearrange("p (s q) -> p s q", s=SUBS),
                                          bank[R:, 7:8, 0:P].to_broadcast([P - R, SUBS, P]), blocks[R:, :, :],
                                          ALU.mult).then_inc(S["shift"], 1)

                    def invert(w, part):
                        if part == 0:
                            wait(dve, S["o_taken"], at(c, PAIRS) + w + 1)
                            wait(dve, S["normed"], at(c, PAIRS) + w)
                        cols = slice(part * P, (part + 1) * P)
                        inv = dve.reciprocal(rec[:, cols], o[2 * HD0:, cols])
                        if part == SUBS - 1:
                            inv.then_inc(S["rec"], 1)

                    for x in range(2):
                        for q in range(SUBS):
                            maximum(x, q, 0)
                            maximum(x, q, 1)
                        negate(x)
                        if x == 0:
                            shift(0)
                    for w in range(PAIRS):
                        for s in range(STEPS):
                            u, q = 2 * w + 2 + s // 2, s % 2 * 2
                            maximum(u, q, 0)
                            maximum(u, q, 1)
                            if s == 0:
                                shift(2 * w + 1)
                            if s == 3 and w:
                                invert(w - 1, 2)
                            maximum(u, q + 1, 0)
                            maximum(u, q + 1, 1)
                            if s % 2 == 1:
                                negate(u)
                            if s == 2:
                                shift(2 * w + 2)
                            if s and w:
                                invert(w - 1, (0, 1, 3)[s - 1])
                    for part in range(SUBS):
                        invert(PAIRS - 1, part)
                    for q in range(SUBS):
                        wait(dve, S["y"], at(c, SUBS) + q + 1)
                        row = X[:, ds(c * SUBS + (b * QB + q), 1), :].rearrange("p a d -> p (a d)")
                        dve.tensor_tensor(row, row, bank[:, q, :], ALU.add).then_inc(S["added"], 1)

            @block.scalar
            def _(act):
                with act.Fori(0, CHUNKS) as c:
                    def take(w):
                        wait(act, S["weighed"], at(c, PAIRS * STEPS) + (w + 1) * STEPS)
                        wait(act, S["normed"], at(c, PAIRS) + w)
                        act.activation(o[:, :], bank[:, 6, :], ACT.Copy).then_inc(S["o_taken"], 1)

                    for w in range(PAIRS):
                        for s in range(STEPS):
                            for x in range(2):
                                n = at(c, UN0 * STEPS) + 2 * (w * STEPS + s) + x
                                wait(act, S["scored"], n + 1)
                                wait(act, S["weighed"], at(c, PAIRS * STEPS) + w * STEPS + s - 1)
                                act.activation(probs[:, x, s % 2, :, :], bank[:, 2 + 2 * x:4 + 2 * x, :], ACT.Exp,
                                               scale=scale).then_inc(S["exps"], 1)
                            if s == 0 and w:
                                take(w - 1)
                    take(PAIRS - 1)


def swiglu(env, tag, block, ctx, tiles, gate_up, wd, ready, ready_value, scale=None, gate=None,
           down=None):
    nc, sb, X, xnT, bank, S = (env[k] for k in ("nc", "sb", "X", "xnT", "bank", "f" + tag))
    SUBS, G = CH // P, 2
    PER = 2 * G
    raw = sb(ctx, "up_raw" + tag, [P, 2, KD, G * P])
    lo = sb(ctx, "up_lo" + tag, [P, 2, 2, KD, G * P], F32R)
    hi = sb(ctx, "up_hi" + tag, [P, 2, 2, KD, G * P], F32R)
    dh = sb(ctx, "down_hi" + tag, [P, 2, G, D], F32R)
    dl = sb(ctx, "down_lo" + tag, [P, 2, G, D], F32R)
    xh = sb(ctx, "x_hi" + tag, [P, 2, KD, CH], F32R)
    xl = sb(ctx, "x_lo" + tag, [P, 2, KD, CH], F32R)
    hid = sb(ctx, "hid" + tag, [P, 2, CH])
    hh = sb(ctx, "hid_hi" + tag, [P, 2, CH], F32R)
    hl = sb(ctx, "hid_lo" + tag, [P, 2, CH], F32R)
    sg = sb(ctx, "sg" + tag, [P, 2, CH])
    PARTS = ((0, 0), (0, 1), (1, 0))

    def turns(engine, emit):
        full = (tiles - 1) // PER
        with engine.Fori(0, full) as i:
            emit(i, (G, G), False)
        rest = tiles - full * PER
        emit(full, (min(G, rest), rest - min(G, rest)), True)

    def plan(i, sizes, last):
        first = 0
        for a, size in enumerate(sizes):
            yield a, size, first, (None if last and a == 1 else (1 - a, i * 2 + a + 1, (sizes[1] if a == 0 else G)))
            first += size

    def load(sp, number, size):
        col = number * (G * P)
        col = col if isinstance(col, int) else sp.snap(col)
        if not isinstance(number, int) or number >= 1:
            wait(sp, S["split"], number * 3)
        for a in range(2):
            sp.dma_start(raw[:, a, :, 0:size * P],
                         gate_up[a].rearrange("(k p) h -> p k h", p=P)[:, :, ds(col, size * P)]).then_inc(
                             S["raw"], 16)

    @block.sync
    def _(sp):
        load(sp, 0, G)
        if down is not None:
            sp.dma_start(wd[:, :, :], down.rearrange("(h p) d -> p h d", p=P)).then_inc(ready, 16)

        def emit(i, sizes, last):
            for a, size, first, nxt in plan(i, sizes, last):
                if nxt:
                    load(sp, *nxt[1:])
        turns(sp, emit)

    @block.tensor
    def _(pe):
        def emit(i, sizes, last):
            steps = [(a, size, first, c, h) for a, size, first, _ in plan(i, sizes, last)
                     for c in range(NC) for h in range(size)]

            def up(n):
                a, size, first, c, h = steps[n]
                if c == 0 and h == 0:
                    wait(pe, S["split"], i * 6 + 3 * a + 3)
                if h == 0:
                    wait(pe, S["x_lo"], (i * 2 + a) * NC + c + 1)
                wait(pe, S["hidden"], i * (PER * NC) + n - 1)
                for m in range(2):
                    count = 0
                    for l, r in PARTS:
                        for k in range(KD):
                            w = (lo if l else hi)[:, a, m, k, h * P:(h + 1) * P]
                            x = (xl if r else xh)[:, c % 2, k, :]
                            mm = pe.matmul(bank[:, 2 * (n % 2) + m, :], w, x, start=(count == 0),
                                           stop=(count == 3 * KD - 1))
                            count += 1
                mm.then_inc(S["up"], 1)

            def down(n):
                a, size, first, c, h = steps[n]
                wait(pe, S["parts"], i * (PER * NC) + n + 1)
                if h == 0:
                    wait(pe, S["added"], (i * 2 + a) * (NC * SUBS) + c * SUBS)
                for s in range(SUBS):
                    for p, (l, r) in enumerate(PARTS):
                        left = (hl if l else hh)[:, n % 2, s * P:(s + 1) * P]
                        right = (dl if r else dh)[:, a, h, :]
                        mm = pe.matmul(bank[:, 4 + s, :], left, right, start=(h == 0 and p == 0),
                                       stop=(h == size - 1 and p == 2))
                mm.then_inc(S["y"], 1)

            for n in range(len(steps)):
                up(n)
                if n:
                    down(n - 1)
            down(len(steps) - 1)
        turns(pe, emit)

    def tokens_high(act, c):
        act.activation(xh[:, c % 2], xnT[:, :, c * CH:(c + 1) * CH], ACT.Copy).then_inc(S["x_hi"], 1)

    def tokens_low(dve, done, c):
        wait(dve, S["x_hi"], done + 1)
        dve.tensor_tensor(xl[:, c % 2], xnT[:, :, c * CH:(c + 1) * CH], xh[:, c % 2].bitcast(F32),
                          ALU.subtract).then_inc(S["x_lo"], 1)

    def high(act, number, buffer, size):
        wait(act, S["raw"], number * 32 + 32)
        wait(act, S["y"], number * (G * NC) - G * NC)
        for m in range(2):
            act.activation(hi[:, buffer, m, :, 0:size * P], raw[:, m, :, 0:size * P],
                           ACT.Copy).then_inc(S["hi"], 1)
        if isinstance(number, int) and number == 0:
            act.wait_ge(ready, ready_value)
        act.activation(dh[:, buffer, 0:size, :], wd[:, ds(number * G, size), :], ACT.Copy).then_inc(S["hi"], 1)

    def low(pool, number, buffer, size):
        for m in range(2):
            wait(pool, S["hi"], number * 3 + m + 1)
            pool.tensor_tensor(lo[:, buffer, m, :, 0:size * P], raw[:, m, :, 0:size * P], hi[:, buffer, m, :, 0:size * P].bitcast(F32),
                               ALU.subtract).then_inc(S["split"], 1)
        wait(pool, S["hi"], number * 3 + 3)
        pool.tensor_tensor(dl[:, buffer, 0:size, :], wd[:, ds(number * G, size), :], dh[:, buffer, 0:size, :].bitcast(F32), ALU.subtract).then_inc(
            S["split"], 1)

    @block.scalar
    def _(act):
        tokens_high(act, 0)
        tokens_high(act, 1)
        high(act, 0, 0, G)

        def emit(i, sizes, last):
            n = 0
            for a, size, first, nxt in plan(i, sizes, last):
                for c in range(NC):
                    for h in range(size):
                        at = i * (PER * NC) + n
                        wait(act, S["up"], at + 1)
                        wait(act, S["gated"], at - 1)
                        act.activation(sg[:, n % 2, :], bank[:, 2 * (n % 2), :], ACT.Sigmoid).then_inc(S["sig"], 1)
                        wait(act, S["hidden"], at + 1)
                        wait(act, S["y"], at - 1)
                        act.activation(hh[:, n % 2, :], hid[:, n % 2, :], ACT.Copy).then_inc(S["hid_hi"], 1)
                        n += 1
                        if h == size - 1 and (nxt or c < NC - 2):
                            tokens_high(act, (c + 2) % NC)
                    if nxt and c == 1:
                        high(act, nxt[1], nxt[0], nxt[2])
        turns(act, emit)

    @block.gpsimd
    def _(pool):
        low(pool, 0, 0, G)

        def emit(i, sizes, last):
            for a, size, first, nxt in plan(i, sizes, last):
                if nxt:
                    low(pool, nxt[1], nxt[0], nxt[2])
        turns(pool, emit)

    @block.vector
    def _(dve):
        tokens_low(dve, 0, 0)
        tokens_low(dve, 1, 1)

        def emit(i, sizes, last):
            def add(a, c, done):
                wait(dve, S["y"], i * (PER * NC) + done)
                for s in range(SUBS):
                    row = X[:, c * SUBS + s, :]
                    wait(dve, S["added"], (i * 2 + a) * (NC * SUBS) - NC * SUBS + c * SUBS + s + 1)
                    factor = scale if gate is None else gate[:, c * SUBS + s:c * SUBS + s + 1]
                    dve.scalar_tensor_tensor(out=row, in0=bank[:, 4 + s, :], scalar=factor, in1=row,
                                             op0=ALU.mult, op1=ALU.add).then_inc(S["added"], 1)

            n, pending = 0, None
            for a, size, first, nxt in plan(i, sizes, last):
                for c in range(NC):
                    for h in range(size):
                        at = i * (PER * NC) + n
                        wait(dve, S["sig"], at + 1)
                        wait(dve, S["hid_hi"], at - 1)
                        wait(dve, S["parts"], at - 1)
                        dve.tensor_tensor(hid[:, n % 2, :], bank[:, 2 * (n % 2), :], sg[:, n % 2, :],
                                          ALU.mult).then_inc(S["gated"], 1)
                        wait(dve, S["gated"], at + 1)
                        dve.tensor_tensor(hid[:, n % 2, :], bank[:, 2 * (n % 2) + 1, :], hid[:, n % 2, :],
                                          ALU.mult).then_inc(S["hidden"], 1)
                        wait(dve, S["hid_hi"], at + 1)
                        wait(dve, S["y"], at - 1)
                        dve.tensor_tensor(hl[:, n % 2, :], hid[:, n % 2, :], hh[:, n % 2, :].bitcast(F32),
                                          ALU.subtract).then_inc(S["parts"], 1)
                        n += 1
                        if pending:
                            add(*pending)
                            pending = None
                        if h == size - 1 and (nxt or c < NC - 2):
                            tokens_low(dve, (i * 2 + a) * NC + c + 2, (c + 2) % NC)
                    pending = (a, c, n)
            add(*pending)
        turns(dve, emit)


def feed_forward0(env):
    nc, bank, had, sem, sb, ins = (env[k] for k in ("nc", "bank", "had", "sem", "sb", "ins"))
    HT = F0 // P
    CW = 128
    with ExitStack() as ctx:
        w2 = sb(ctx, "w2", [P, HT, D])
        loaded = [sem(f"f0_loaded{q}") for q in range(4)]
        raw, flat, bf = (sem("w2_" + n) for n in ("raw", "flat", "bf"))
        with ExitStack() as c2:
            ping = sb(c2, "ping", [P, HT, CW])
            pong = sb(c2, "pong", [P, HT, CW])
            with nc.Block() as block:
                @block.sync
                def _(sp):
                    for q in range(4):
                        sp.dma_start(w2[:, 4 * q:4 * q + 4, :], ins["L0_ffn_W2"].rearrange(
                            "(h p) d -> p h d", p=P)[:, 4 * q:4 * q + 4, :]).then_inc(loaded[q], 16)

                @block.tensor
                def _(pe):
                    for c in range(D // CW):
                        if c:
                            pe.wait_ge(flat, 4 * c)
                        for q in range(4):
                            pe.wait_ge(loaded[q], 16)
                            mm = pe.matmul(bank[:, q, :], had, w2[:, 4 * q:4 * q + 4, c * CW:(c + 1) * CW],
                                           start=True, stop=True)
                            mm.then_inc(raw, 1)

                @block.scalar
                def _(act):
                    for c in range(D // CW):
                        if c:
                            act.wait_ge(bf, 8 * c)
                        for q in range(4):
                            act.wait_ge(raw, 4 * c + q + 1)
                            act.activation(ping[:, 4 * q:4 * q + 4, :],
                                           bank[:, q, :].rearrange("p (a n) -> p a n", n=CW),
                                           ACT.Copy).then_inc(flat, 1)

                @block.vector
                def _(dve):
                    for c in range(D // CW):
                        dve.wait_ge(flat, 4 * (c + 1))
                        bufs = [ping[:, :, :], pong[:, :, :], ping[:, :, :], pong[:, :, :],
                                w2[:, :, c * CW:(c + 1) * CW]]
                        for st in range(4):
                            h = 1 << st
                            src = bufs[st].rearrange("p (g two h) n -> p g two h n", two=2, h=h)
                            dst = bufs[st + 1].rearrange("p (g two h) n -> p g two h n", two=2, h=h)
                            if st:
                                dve.wait_ge(bf, 8 * c + 2 * st)
                            for j, op in ((0, ALU.add), (1, ALU.subtract)):
                                if h in (1, 8):
                                    a = 0 if h == 8 else slice(None)
                                    z = slice(None) if h == 8 else 0
                                    i0, i1, o = src[:, a, 0, z, :], src[:, a, 1, z, :], dst[:, a, j, z, :]
                                else:
                                    i0, i1, o = src[:, :, 0], src[:, :, 1], dst[:, :, j]
                                dve.tensor_tensor(o, i0, i1, op).then_inc(bf, 1)
        with nc.Block() as block:
            swiglu(env, "0", block, ctx, HT, (ins["L0_ffn_W1"], ins["L0_ffn_W3"]), w2, bf, 8 * (D // CW),
                   scale=float(F0) ** -0.5)


def route(env, r):
    nc, xnT, bank, ident, sem, sb, ins = (env[k] for k in ("nc", "xnT", "bank", "ident", "sem", "sb", "ins"))
    W = E + 1
    loaded, lgT, lgT_s, lg, lg_s, cnt, chain, ex = (sem("r_" + n) for n in
                                                    ("loaded", "lgT", "lgTs", "lg", "lgs", "cnt", "chain", "exp"))
    with ExitStack() as ctx:
        wr = sb(ctx, "wr", [P, KD, W])
        logT = sb(ctx, "logT", [W, T])
        log = sb(ctx, "log", [P, NT, W])
        iota = sb(ctx, "iota", [P, NT, E])
        top = sb(ctx, "top", [P, NT, 8])
        topi = sb(ctx, "topi", [P, NT, 8], U32)
        topf = sb(ctx, "topf", [P, NT, 8])
        hot = sb(ctx, "hot", [P, TOPK, NT, E])
        mask = sb(ctx, "mask", [P, NT, E])
        slotv = sb(ctx, "slotv", [P, NT, E])
        base = sb(ctx, "base", [P, NT, E])
        tmp = sb(ctx, "tmp", [P, NT, E])
        exps = sb(ctx, "exps", [P, NT, TOPK])
        sums = sb(ctx, "sums", [P, 2, NT])
        slotf = sb(ctx, "slotf", [P, NT, TOPK])
        ok = sb(ctx, "ok", [P, NT, TOPK])
        with nc.Block() as block:
            @block.sync
            def _(sp):
                sp.dma_start(wr[:, :, 0:E], ins["L1_ffn_Wr"].rearrange("(k p) n -> p k n", p=P)).then_inc(loaded, 16)
                sp.dma_start(wr[:, :, E:W], ins["L1_ffn_Wse"].rearrange("(k p) n -> p k n", p=P),
                             allow_slow_non_contiguous=True).then_inc(loaded, 16)
                sp.dma_start(iota[:, :, :], env["consts"]["expert"].rearrange("p (n e) -> p n e", e=E)).then_inc(loaded, 16)
                sp.wait_ge(loaded, 48)

            @block.tensor
            def _(pe):
                pe.wait_ge(loaded, 48)
                for c in range(NC):
                    for k in range(KD):
                        mm = pe.matmul(bank[0:W, c, :], wr[:, k, :], xnT[:, k, c * CH:(c + 1) * CH],
                                       start=(k == 0), stop=(k == KD - 1))
                    mm.then_inc(lgT, 1)
                for c in range(NC):
                    pe.wait_ge(lgT_s, c + 1)
                    for s in range(CH // P):
                        n = c * (CH // P) + s
                        mm = pe.transpose(bank[:, 4 + c // 2, (n % 8) * W:(n % 8 + 1) * W],
                                          logT[:, n * P:(n + 1) * P], ident[0:W, 0:W])
                    mm.then_inc(lg, 1)
                pe.wait_ge(cnt, 1)
                pe.matmul(bank[:, 6, :], env["before"], mask[:, :, :], start=True, stop=True).then_inc(lg, 1)
                pe.matmul(bank[:, 7, :], env["ones"], mask[:, :, :], start=True, stop=True).then_inc(lg, 1)

            @block.scalar
            def _(act):
                for c in range(NC):
                    act.wait_ge(lgT, c + 1)
                    act.activation(logT[:, c * CH:(c + 1) * CH], bank[0:W, c, :], ACT.Copy).then_inc(lgT_s, 1)
                for g in range(2):
                    act.wait_ge(lg, 2 * (g + 1))
                    act.activation(log[:, 8 * g:8 * g + 8, :],
                                   bank[:, 4 + g, 0:8 * W].rearrange("p (n e) -> p n e", e=W),
                                   ACT.Copy).then_inc(lg_s, 1)
                act.wait_ge(ex, 1)
                act.activation(exps[:, :, :], slotf[:, :, :], ACT.Exp).then_inc(lg_s, 1)
                act.wait_ge(lg_s, 3)
                act.activation(r["gshared"][:, :], log[:, :, E], ACT.Sigmoid).then_inc(lg_s, 1)

            @block.vector
            def _(dve):
                steps = [0]

                def step(instruction):
                    steps[0] += 1
                    instruction.then_inc(chain, 1)
                    dve.wait_ge(chain, steps[0])
                dve.wait_ge(loaded, 48)
                dve.wait_ge(lg_s, 2)
                for n in range(NT):
                    ins_ = dve.max(top[:, n, :], log[:, n, 0:E])
                step(ins_)
                for n in range(NT):
                    ins_ = dve.max_index(topi[:, n, :], top[:, n, :], log[:, n, 0:E])
                step(ins_)
                step(dve.tensor_copy(topf[:, :, :], topi[:, :, :]))
                step(dve.tensor_tensor(slotf[:, :, :], top[:, :, 0:TOPK],
                                       top[:, :, 0:1].to_broadcast([P, NT, TOPK]), ALU.subtract))
                dve.sem_inc(ex, 1)
                for k in range(TOPK):
                    step(dve.tensor_tensor(hot[:, k], iota[:, :, :], topf[:, :, k:k + 1].to_broadcast([P, NT, E]),
                                           ALU.is_equal))
                step(dve.tensor_tensor(mask[:, :, :], hot[:, 0], hot[:, 1], ALU.add))
                step(dve.tensor_tensor(mask[:, :, :], mask[:, :, :], hot[:, 2], ALU.add))
                step(dve.tensor_tensor(mask[:, :, :], mask[:, :, :], hot[:, 3], ALU.add))
                dve.sem_inc(cnt, 1)
                dve.wait_ge(lg, NC + 2)
                step(dve.memset(base[:, 0, :], 0.0))
                for n in range(1, NT):
                    step(dve.tensor_tensor(base[:, n, :], bank[:, 7, (n - 1) * E:n * E], base[:, n - 1, :], ALU.add))
                step(dve.tensor_tensor(base[:, :, :], bank[:, 6, :].rearrange("p (n e) -> p n e", e=E),
                                       base[:, :, :], ALU.add))
                step(dve.tensor_scalar(tmp[:, :, :], base[:, :, :], float(CAP), float(OOB), ALU.is_ge, ALU.mult))
                step(dve.tensor_tensor(tmp[:, :, :], tmp[:, :, :], base[:, :, :], ALU.add))
                step(dve.scalar_tensor_tensor(out=slotv[:, :, :], in0=iota[:, :, :], scalar=float(CAP),
                                              in1=tmp[:, :, :], op0=ALU.mult, op1=ALU.add))
                dve.wait_ge(lg_s, 3)
                for k in range(TOPK):
                    step(dve.tensor_tensor(tmp[:, :, :], hot[:, k], slotv[:, :, :], ALU.mult))
                    step(dve.tensor_reduce(slotf[:, :, k], tmp[:, :, :], AX.X, ALU.add))
                step(dve.tensor_copy(r["slot"][:, :, :], slotf[:, :, :]))
                step(dve.tensor_scalar(ok[:, :, :], slotf[:, :, :], float(SLOTS), None, ALU.is_lt))
                step(dve.tensor_reduce(sums[:, 0, :], exps[:, :, :], AX.X, ALU.add))
                step(dve.reciprocal(sums[:, 1, :], sums[:, 0, :]))
                step(dve.tensor_tensor(ok[:, :, :], ok[:, :, :], exps[:, :, :], ALU.mult))
                for k in range(TOPK):
                    step(dve.tensor_tensor(r["wk"][:, :, k], ok[:, :, k], sums[:, 1, :], ALU.mult))


def dispatch(env, r, block, zero):
    zeroed, sent, z = env["sem"]("d_zeroed"), env["sem"]("d_sent"), env["sem"]("d_z")

    @block.gpsimd
    def _(pool):
        pool.memset(zero[:, :], 0.0).then_inc(z, 1)
        pool.wait_ge(z, 1)
        for m in range(SLOTS // P):
            pool.dma_start(env["xe"][m * P:(m + 1) * P, :], zero[:, :]).then_inc(zeroed, 16)
        pool.wait_ge(zeroed, 16 * SLOTS // P)
        for n in range(NT):
            for k in range(TOPK):
                pool.indirect_dma_start(env["xe"], bass.IndirectOffsetOnAxis(ap=r["slot"][:, n, k:k + 1], axis=0),
                                        r["xn"][:, n, :], None, bounds_check=SLOTS - 1,
                                        oob_is_err=False).then_inc(sent, 16)
        pool.wait_ge(sent, 16 * NT * TOPK)


def attention1(env, r):
    nc, X, xnT, bank, ident, band, sem, sb, ins = (env[k] for k in ("nc", "X", "xnT", "bank", "ident", "band", "sem",
                                                                    "sb", "ins"))
    PAIRS = H1 // 4
    scale = float(SUB) ** -0.5
    UN = 2 * NT
    S = env["h1"]
    with ExitStack() as ctx:
        wq = sb(ctx, "wq1", [P, KD, 2 * P])
        wo = sb(ctx, "wo1", [P, 2, D])
        wk = sb(ctx, "wk1", [P, KD, 2 * P])
        q = sb(ctx, "q1", [P, 2, T])
        k_ = sb(ctx, "k1", [P, 2, T])
        v = sb(ctx, "v1", [P, NT, 2 * P])
        rope = sb(ctx, "rope1", [P, 2, SEQ])
        lam = sb(ctx, "lam", [P, H1])
        tr = sb(ctx, "tr", [P, 4, CH])
        ms = sb(ctx, "ms", [P, 4, 2, 2 * P])
        mix = sb(ctx, "mix", [P, 4, 2 * P])
        pt = sb(ctx, "pt1", [P, 2, 2 * P])
        oT = sb(ctx, "oT1", [P, 2, 2, P])
        sm = sb(ctx, "sm1", [P, 4, 12])
        zero = sb(ctx, "zero", [P, D])
        wv = wq

        for g in range(2):
            with nc.Block() as block:
                @block.sync
                def _(sp):
                    for name, w, done in (("L1_attn_Wk", wk, "kw"), ("L1_attn_Wv", wv, "vw")):
                        sp.dma_start(w[:, :, :], ins[name].rearrange("(k p) n -> p k n", p=P)[
                            :, :, 2 * P * g:2 * P * (g + 1)]).then_inc(S[done], 16)
                        if g == 0 and w is wk:
                            sp.dma_start(rope[:, :, :], env["consts"]["rope1"].rearrange(
                                "p (a s) -> p a s", a=2)).then_inc(S["lam"], 16)
                            sp.dma_start(lam[:, :], ins["L1_attn_lam"].partition_broadcast(P)).then_inc(S["lam"], 16)

                project_keys_values(env, block, S, g, wk, wv, k_, v, rope, lam, tr)
            with nc.Block() as block:
                if g == 0:
                    dispatch(env, r, block, zero)
                attention1_pairs(env, block, S, g, PAIRS, UN, scale, wq, wo, q, k_, v, rope, lam, tr, ms, mix, pt,
                                 oT, sm)


def project_keys_values(env, block, S, g, wk, wv, k_, v, rope, lam, tr):
    nc, xnT, bank, ident = (env[k] for k in ("nc", "xnT", "bank", "ident"))
    STEPS = [(part, c) for part in range(2) for c in range(NC)]
    before, rounds = 2 * NC * g, NC * g

    @block.tensor
    def _(pe):
        def rows(c):
            wait(pe, S["qdone"], before + NC + c + 1)
            if c or g:
                wait(pe, S["vtaken"], rounds + c)
            for s in range(CH // P):
                for a in range(2):
                    mm = pe.transpose(bank[:, 4 + s // 2, (s % 2) * 2 * P + a * P:(s % 2) * 2 * P + (a + 1) * P],
                                      tr[:, 2 * (c % 2) + a, s * P:(s + 1) * P], ident)
            mm.then_inc(S["vrows"], 1)

        for n, (part, c) in enumerate(STEPS):
            if c == 0:
                wait(pe, S["vw" if part else "kw"], 16 * (g + 1))
            if n >= 2 or g:
                wait(pe, S["qdone"], before + n - 1)
            for a in range(2):
                for k in range(KD):
                    mm = pe.matmul(bank[:, 2 * (n % 2) + a, :], (wv if part else wk)[:, k, a * P:(a + 1) * P],
                                   xnT[:, k, c * CH:(c + 1) * CH], start=(k == 0), stop=(k == KD - 1))
            mm.then_inc(S["proj"], 1)
            if part and c:
                rows(c - 1)
        rows(NC - 1)

    @block.vector
    def _(dve):
        for n, (part, c) in enumerate(STEPS):
            if g == 0 and n == 0:
                wait(dve, S["lam"], 32)
                dve.tensor_scalar(lam[:, :], lam[:, :], -1.0, None, ALU.mult).then_inc(S["lam"], 1)
            wait(dve, S["proj"], before + n + 1)
            if n or g:
                wait(dve, S["qdone"], before + n)
            if part:
                if c > 1 or g:
                    wait(dve, S["vrows"], rounds + c - 1)
                dve.tensor_copy(tr[:, 2 * (c % 2):2 * (c % 2) + 2, :], bank[:, 2 * (n % 2):2 * (n % 2) + 2, :]).then_inc(
                    S["qdone"], 1)
            else:
                rotate(dve, S, bank[:, 2 * (n % 2), :], bank[:, 2 * (n % 2) + 1, :],
                       k_[:, 0, c * CH:(c + 1) * CH], k_[:, 1, c * CH:(c + 1) * CH],
                       rope[:, 0, (c % 2) * CH:(c % 2 + 1) * CH], rope[:, 1, (c % 2) * CH:(c % 2 + 1) * CH], tr,
                       (rounds + c) * 2, lambda n: n)

    @block.scalar
    def _(act):
        for c in range(NC):
            wait(act, S["vrows"], rounds + c + 1)
            act.activation(v[:, c * 4:(c + 1) * 4, :],
                           bank[:, 4:6, :].rearrange("p a (s n) -> p (a s) n", n=2 * P),
                           ACT.Copy).then_inc(S["vtaken"], 1)


def rotate(dve, S, first, second, out1, out2, cos, sin, tr, done, at, names=("cos", "qdone"), halves=(0, 1)):
    pa, pc = names
    for half in halves:
        x, y, op, o = (first, second, ALU.subtract, out1) if half == 0 else (second, first, ALU.add, out2)
        dve.tensor_tensor(tr[:, 2 * half, :], x, cos, ALU.mult)
        dve.tensor_tensor(tr[:, 2 * half + 1, :], y, sin, ALU.mult).then_inc(S[pa], 1)
        wait(dve, S[pa], at(done + half + 1))
        last = dve.tensor_tensor(o, tr[:, 2 * half, :], tr[:, 2 * half + 1, :], op)
        if half == 1:
            last.then_inc(S[pc], 1)


def attention1_pairs(env, block, S, g, PAIRS, UN, scale, wq, wo, q, k_, v, rope, lam, tr, ms, mix, pt, oT, sm):
    nc, X, xnT, bank, ident, band, sem, ins = (env[k] for k in ("nc", "X", "xnT", "bank", "ident", "band", "sem",
                                                                "ins"))

    def base(i, per):
        return i * per + g * PAIRS * per

    UC = UN // NC

    def pairs(engine, emit):
        with engine.Fori(0, PAIRS - 1) as i:
            emit(i, False)
        emit(PAIRS - 1, True)

    def keys(n):
        return (n, 1) if n % QB == 0 else (n - 1, 2)

    @block.sync
    def _(sp):
        wq_v = ins["L1_attn_Wq"].rearrange("(k p) n -> p k n", p=P)
        wo_v = ins["L1_attn_Wo"].rearrange("(h p) n -> p h n", p=P)
        sp.dma_start(wq[:, :, :], wq_v[:, :, g * PAIRS * 2 * P:(g * PAIRS + 1) * 2 * P]).then_inc(S["w"], 16)

        def fill(i, last):
            if not last:
                col = sp.snap(i * 2 * P + (g * PAIRS + 1) * 2 * P)
                wait(sp, S["qproj"], base(i, NC) + NC)
                sp.dma_start(wq[:, :, :], wq_v[:, :, ds(col, 2 * P)]).then_inc(S["w"], 16)
            head = i * 2 + g * PAIRS * 2
            head = head if last else sp.snap(head)
            wait(sp, S["y"], base(i, NT))
            sp.dma_start(wo[:, :, :], wo_v[:, ds(head, 2), :]).then_inc(S["wo"], 16)
        pairs(sp, fill)

    @block.tensor
    def _(pe):
        def queries(c, first_bank, part):
            a = part // 2
            for k in (part % 2 * 2, part % 2 * 2 + 1):
                mm = pe.matmul(bank[:, first_bank + a, :], wq[:, k, a * P:(a + 1) * P],
                               xnT[:, k, c * CH:(c + 1) * CH], start=(k == 0), stop=(k == KD - 1))
            if part == 3:
                mm.then_inc(S["qproj"], 1)

        wait(pe, S["w"], base(0, 16) + 16)
        for c in range(NC):
            if c > 1 or g:
                wait(pe, S["roped"], base(0, NC) + c - 1)
            for part in range(4):
                queries(c, 4 if c % 2 == 0 else 0, part)
        wait(pe, S["roped"], base(0, NC) + NC)

        def fill(i, last):
            def scores(u):
                n, h = u // 2, u % 2
                k0, kn = keys(n)
                rows = slice(SUB * h, SUB * (h + 1))
                if u % 8 == 0:
                    wait(pe, S["roped"], base(i, NC) + n // 4 + 1)
                wait(pe, S["masked"], base(i, UN) + u - 1)
                for a in range(2):
                    mm = pe.matmul(bank[:, u % 2, a * 2 * P:a * 2 * P + kn * P], q[rows, a, n * P:(n + 1) * P],
                                   k_[rows, a, k0 * P:(k0 + kn) * P], start=True, stop=True)
                mm.then_inc(S["scores"], 1)

            def turn(u):
                kn = keys(u // 2)[1]
                wait(pe, S["probs"], base(i, UN) + u + 1)
                wait(pe, S["pt"], base(i, UN) + u - 1)
                for m in range(kn):
                    mm = pe.transpose(bank[:, 2 + u % 2, m * P:(m + 1) * P], mix[:, u % 4, m * P:(m + 1) * P], ident)
                mm.then_inc(S["turned"], 1)

            def weigh(u):
                n, h = u // 2, u % 2
                k0, kn = keys(n)
                wait(pe, S["pt"], base(i, UN) + u + 1)
                wait(pe, S["ot"], base(i, UN) + u - 1)
                for m in range(kn):
                    mm = pe.matmul(bank[:, 2 + u % 2, 2 * P:3 * P], v[:, k0 + m, h * P:(h + 1) * P],
                                   pt[:, u % 2, m * P:(m + 1) * P], start=(m == 0), stop=(m == kn - 1))
                mm.then_inc(S["pv"], 1)

            def project(n):
                if n == 0:
                    wait(pe, S["wo"], base(i, 16) + 16)
                wait(pe, S["ot"], base(i, UN) + 2 * n + 2)
                wait(pe, S["added"], base(i, NT) + n - 1)
                for h in range(2):
                    mm = pe.matmul(bank[:, 6 + n % 2, :], oT[:, n % 2, h, :], wo[:, h, :], start=(h == 0), stop=(h == 1))
                mm.then_inc(S["y"], 1)

            scores(0)
            for s in range(UN + 6):
                if s + 1 < UN:
                    scores(s + 1)
                if 3 <= s < UN + 3:
                    turn(s - 3)
                if 4 <= s < UN + 4:
                    weigh(s - 4)
                if s >= 7 and s % 2 == 1:
                    project((s - 7) // 2)
                c, part = s // UC - 1, s % UC
                if not last and c >= 0 and part < 4:
                    if c == 0 and part == 0:
                        wait(pe, S["w"], base(i, 16) + 32)
                    if part == 0:
                        wait(pe, S["roped"], base(i, NC) + NC + c)
                    queries(c, 4, part)
        pairs(pe, fill)

    @block.vector
    def _(dve):
        def turn_queries(i, c, first_bank, halves):
            wait(dve, S["qproj"], base(i, NC) + c + 1)
            wait(dve, S["roped"], base(i, NC) + c)
            rotate(dve, S, bank[:, first_bank, :], bank[:, first_bank + 1, :],
                   q[:, 0, c * CH:(c + 1) * CH], q[:, 1, c * CH:(c + 1) * CH],
                   rope[:, 0, (c % 2) * CH:(c % 2 + 1) * CH], rope[:, 1, (c % 2) * CH:(c % 2 + 1) * CH], tr,
                   2 * c, lambda n: base(i, 2 * NC) + n, names=("sin", "roped"), halves=halves)

        if g:
            wait(dve, S["scores"], base(0, UN))
        for c in range(NC):
            turn_queries(0, c, 4 if c % 2 == 0 else 0, (0, 1))

        def fill(i, last):

            def mask(u):
                kn = keys(u // 2)[1]
                w = kn * P
                wait(dve, S["mixed"], base(i, UN) + u - 3)
                wait(dve, S["scores"], base(i, UN) + u + 1)
                dve.memset(sm[:, u % 4, 11:12], 0.0).then_inc(S["cleared"], 1)
                for a in range(2):
                    m = dve.tensor_tensor_reduce(ms[:, u % 4, a, 0:w], bank[:, u % 2, a * 2 * P:a * 2 * P + w],
                                                 band[:, 2 * P - w:2 * P], -scale, 3e38, ALU.add, ALU.min,
                                                 sm[:, u % 4, a:a + 1])
                m.then_inc(S["masked"], 1)

            def combine(u):
                n, h = u // 2, u % 2
                w = keys(n)[1] * P
                b = sm[:, u % 4, :]
                wait(dve, S["exps"], base(i, UN) + u + 1)
                dve.reciprocal(b[:, 6:7], b[:, 5:6]).then_inc(S["recip2"], 1)
                wait(dve, S["recip2"], base(i, UN) + u + 1)
                dve.scalar_tensor_tensor(out=b[:, 7:8], in0=b[:, 4:5], scalar=b[:, 6:7],
                                         in1=nlam(i, h), op0=ALU.mult, op1=ALU.mult).then_inc(S["coef"], 1)
                wait(dve, S["coef"], base(i, UN) + u + 1)
                wait(dve, S["turned"], base(i, UN) + u - 3)
                dve.scalar_tensor_tensor(out=mix[:, u % 4, 0:w], in0=ms[:, u % 4, 1, 0:w], scalar=b[:, 7:8],
                                         in1=ms[:, u % 4, 0, 0:w], op0=ALU.mult, op1=ALU.add).then_inc(S["mixed"], 1)

            def normalise(u):
                w = keys(u // 2)[1] * P
                b = sm[:, u % 4, :]
                wait(dve, S["relu"], base(i, UN) + u + 1)
                dve.scalar_tensor_tensor(out=b[:, 9:10], in0=b[:, 4:5], scalar=1e-6, in1=b[:, 8:9],
                                         op0=ALU.mult, op1=ALU.add).then_inc(S["den"], 1)
                wait(dve, S["den"], base(i, UN) + u + 1)
                dve.reciprocal(b[:, 10:11], b[:, 9:10]).then_inc(S["recipd"], 1)
                wait(dve, S["recipd"], base(i, UN) + u + 1)
                dve.tensor_scalar(mix[:, u % 4, 0:w], mix[:, u % 4, 0:w], b[:, 10:11], None,
                                  ALU.mult).then_inc(S["probs"], 1)

            def add(n):
                wait(dve, S["y"], base(i, NT) + n + 1)
                dve.tensor_tensor(X[:, n, :], X[:, n, :], bank[:, 6 + n % 2, :], ALU.add).then_inc(S["added"], 1)

            def nlam(i, h):
                return lam[:, ds(i + (2 * g * PAIRS + h * PAIRS), 1)]

            for s in range(UN + 7):
                if s < UN:
                    mask(s)
                if 1 <= s <= UN:
                    combine(s - 1)
                if 2 <= s < UN + 2:
                    normalise(s - 2)
                if s >= 8 and s % 2 == 0:
                    add((s - 8) // 2)
                c, half = (s - 5) // UC - 1, (s - 5) % UC
                if not last and c >= 0 and half < 2:
                    wait(dve, S["scores"], base(i, UN) + (c + 1) * UC)
                    turn_queries(i + 1, c, 4, (half,))
        pairs(dve, fill)

    @block.scalar
    def _(act):
        def fill(i, last):
            for s in range(UN + 5):
                if s < UN:
                    u = s
                    w = keys(u // 2)[1] * P
                    wait(act, S["masked"], base(i, UN) + u + 1)
                    for a in range(2):
                        ex = act.activation(ms[:, u % 4, a, 0:w], ms[:, u % 4, a, 0:w], ACT.Exp,
                                            scale=-1.0, bias=sm[:, u % 4, a:a + 1], accum_out=sm[:, u % 4, 4 + a:5 + a])
                    ex.then_inc(S["exps"], 1)
                if 1 <= s <= UN:
                    u = s - 1
                    w = keys(u // 2)[1] * P
                    wait(act, S["mixed"], base(i, UN) + u + 1)
                    act.activation(mix[:, u % 4, 0:w], mix[:, u % 4, 0:w], ACT.Relu,
                                   accum_out=sm[:, u % 4, 8:9]).then_inc(S["relu"], 1)
                if 3 <= s < UN + 3:
                    u = s - 3
                    w = keys(u // 2)[1] * P
                    wait(act, S["turned"], base(i, UN) + u + 1)
                    wait(act, S["pv"], base(i, UN) + u - 1)
                    act.activation(pt[:, u % 2, 0:w], bank[:, 2 + u % 2, 0:w], ACT.Copy).then_inc(S["pt"], 1)
                if s >= 5:
                    u = s - 5
                    n, h = u // 2, u % 2
                    wait(act, S["pv"], base(i, UN) + u + 1)
                    wait(act, S["y"], base(i, NT) + n - 1)
                    act.activation(oT[:, n % 2, h, :], bank[:, 2 + u % 2, 2 * P:3 * P], ACT.Copy).then_inc(S["ot"], 1)
        pairs(act, fill)


def feed_forward1(env, r):
    nc, sem, sb, ins = (env[k] for k in ("nc", "sem", "sb", "ins"))
    HT = FS // P
    with ExitStack() as ctx:
        loaded = sem("f1_loaded")
        wd = sb(ctx, "wsd", [P, HT, D])
        with nc.Block() as block:
            swiglu(env, "1", block, ctx, HT, (ins["L1_ffn_Wsg"], ins["L1_ffn_Wsu"]), wd, loaded, 16,
                   gate=r["gshared"], down=ins["L1_ffn_Wsd"])


def experts(env):
    nc, bank, ident, sb, ins, S = (env[k] for k in ("nc", "bank", "ident", "sb", "ins", "e"))
    FP = FT1 * P
    NB = 4
    FULL = (FT1 - 1) * P
    with ExitStack() as ctx:
        wg = sb(ctx, "ewg", [P, NB, KD, FP])
        wu = sb(ctx, "ewu", [P, NB, KD, FP])
        wd = sb(ctx, "ewd", [P, NB, FT1, D])
        xr = sb(ctx, "exr", [P, 2, D])
        xT = sb(ctx, "exT", [P, 2, KD, P])
        sg = sb(ctx, "esg", [P, 2, FT1, CAP])
        hT = sb(ctx, "ehT", [P, NB, FT1, CAP])
        ys = sb(ctx, "eys", [P, 2, D])
        with nc.Block() as block:
            @block.gpsimd
            def _(pool):
                pool.memset(wg[:, :, :, F1:], 0.0).then_inc(S["zeroed"], 1)
                pool.memset(wu[:, :, :, F1:], 0.0).then_inc(S["zeroed"], 1)
                wait(pool, S["zeroed"], 2)
                pool.memset(wd[F1R:, :, FT1 - 1, :], 0.0).then_inc(S["zeroed"], 1)

            @block.sync
            def _(sp):
                with sp.Fori(0, E // NB) as i:
                    pair = [sp.snap(i * NB * CAP + p * P) for p in range(NB // 2)]
                    expert = [sp.snap(i * NB + j) for j in range(NB)]
                    for j in range(NB):
                        if j % 2 == 0:
                            wait(sp, S["xt"], i * (NB // 2) + j // 2 - 1)
                            sp.dma_start(xr[:, j // 2, :], env["xe"][ds(pair[j // 2], P), :]).then_inc(
                                S[f"xloaded{j // 2}"], 16)
                        wait(sp, S["up"], i * NB + j - (NB - 1))
                        s = S[f"wloaded{j}"]
                        for dst, name in ((wg, "Wg"), (wu, "Wu")):
                            sp.dma_start(dst[:, j, :, 0:F1], ins["L1_ffn_" + name][ds(expert[j], 1), :, :].rearrange(
                                "a (k p) f -> p (a k) f", p=P)).then_inc(s, 16)

            @block.tensor
            def _(pe):
                wait(pe, S["zeroed"], 3)
                with pe.Fori(0, E // NB) as i:
                    def turn(p):
                        wait(pe, S[f"xloaded{p}"], i * 16 + 16)
                        wait(pe, S["xt_s"], i * (NB // 2) + p - 1)
                        for k in range(KD):
                            mm = pe.transpose(bank[:, p, k * P:(k + 1) * P], xr[:, p, k * P:(k + 1) * P], ident)
                        mm.then_inc(S["xt"], 1)

                    def up(j):
                        if j % 2 == 0:
                            wait(pe, S["xt_s"], i * (NB // 2) + j // 2 + 1)
                        wait(pe, S[f"wloaded{j}"], i * 32 + 32)
                        wait(pe, S["hidden"], i * NB + j - 1)
                        for a, w in ((0, wg), (1, wu)):
                            for t in range(FT1):
                                for k in range(KD):
                                    mm = pe.matmul(bank[:, 2 + j % 2, (a * FT1 + t) * CAP:(a * FT1 + t + 1) * CAP],
                                                   w[:, j, k, t * P:(t + 1) * P],
                                                   xT[:, j // 2, k, (j % 2) * CAP:(j % 2 + 1) * CAP],
                                                   start=(k == 0), stop=(k == KD - 1))
                        mm.then_inc(S["up"], 1)

                    def down(p):
                        for j in (2 * p, 2 * p + 1):
                            wait(pe, S[f"dloaded{j}"], i * 32 + 32)
                        wait(pe, S["hidden"], i * NB + 2 * p + 2)
                        wait(pe, S["y_s"], i * (NB // 2) + p - 1)
                        for t in range(FT1):
                            for j in (2 * p, 2 * p + 1):
                                mm = pe.matmul(bank[j % 2 * CAP:(j % 2 + 1) * CAP, 4 + p, :], hT[:, j, t, :],
                                               wd[:, j, t, :], start=(t == 0), stop=(t == FT1 - 1),
                                               skip_group_check=True)
                        mm.then_inc(S["y"], 1)

                    turn(0)
                    up(0)
                    turn(1)
                    up(1)
                    up(2)
                    up(3)
                    down(0)
                    down(1)

            @block.scalar
            def _(act):
                with act.Fori(0, E // NB) as i:
                    rows = [act.snap(i * NB * CAP + p * P) for p in range(NB // 2)]
                    expert = [act.snap(i * NB + j) for j in range(NB)]

                    def load_down(p):
                        wait(act, S["y"], i * (NB // 2) + p - 1)
                        for j in (2 * p, 2 * p + 1):
                            down = ins["L1_ffn_Wd"][ds(expert[j], 1), :, :]
                            act.dma_start(wd[:, j, 0:FT1 - 1, :], down[:, 0:FULL, :].rearrange(
                                "a (t p) d -> p (a t) d", p=P)).then_inc(S[f"dloaded{j}"], 16)
                            act.dma_start(wd[0:F1R, j, FT1 - 1, :], down[:, FULL:F1, :].rearrange(
                                "a p d -> p (a d)")).then_inc(S[f"dloaded{j}"], 16)

                    def sigmoid(j):
                        wait(act, S["up"], i * NB + j + 1)
                        wait(act, S["gated"], i * NB + j - 1)
                        act.activation(sg[:, j % 2], bank[:, 2 + j % 2, 0:FT1 * CAP].rearrange("p (t c) -> p t c", c=CAP),
                                       ACT.Sigmoid).then_inc(S["sig"], 1)

                    def store(p):
                        wait(act, S["y"], i * (NB // 2) + p + 1)
                        wait(act, S[f"stored{p}"], i * 16)
                        act.activation(ys[:, p, :], bank[:, 4 + p, :], ACT.Copy).then_inc(S["y_s"], 1)
                        wait(act, S["y_s"], i * (NB // 2) + p + 1)
                        act.dma_start(env["ye"][ds(rows[p], P), :], ys[:, p, :]).then_inc(S[f"stored{p}"], 16)

                    load_down(0)
                    sigmoid(0)
                    sigmoid(1)
                    load_down(1)
                    sigmoid(2)
                    sigmoid(3)
                    store(0)
                    store(1)
                for p in range(2):
                    wait(act, S[f"stored{p}"], 16 * E // NB)

            @block.vector
            def _(dve):
                with dve.Fori(0, E // NB) as i:
                    def rows(p):
                        wait(dve, S["xt"], i * (NB // 2) + p + 1)
                        wait(dve, S["up"], i * NB + 2 * p - 2)
                        dve.tensor_copy(xT[:, p], bank[:, p, :].rearrange("p (k c) -> p k c", k=KD)).then_inc(S["xt_s"], 1)

                    rows(0)
                    for j in range(NB):
                        wait(dve, S["sig"], i * NB + j + 1)
                        wait(dve, S["y"], i * (NB // 2) + j // 2 - 1)
                        g = bank[:, 2 + j % 2, 0:FT1 * CAP].rearrange("p (t c) -> p t c", c=CAP)
                        u = bank[:, 2 + j % 2, FT1 * CAP:2 * FT1 * CAP].rearrange("p (t c) -> p t c", c=CAP)
                        dve.tensor_tensor(hT[:, j], g, sg[:, j % 2], ALU.mult).then_inc(S["gated"], 1)
                        wait(dve, S["gated"], i * NB + j + 1)
                        dve.tensor_tensor(hT[:, j], u, hT[:, j], ALU.mult).then_inc(S["hidden"], 1)
                        if j == 0:
                            rows(1)


def combine(env, r):
    nc, X, sem, sb = (env[k] for k in ("nc", "X", "sem", "sb"))
    G = 4
    cleared, got, used, stored = sem("c_clear"), [sem(f"c_got{s}") for s in range(G)], sem("c_used"), sem("c_stored")
    out_v = env["out"].rearrange("b (n p) d -> p (b n) d", p=P)
    with ExitStack() as ctx:
        y = sb(ctx, "cy", [P, G, TOPK, D])
        with nc.Block() as block:
            @block.gpsimd
            def _(pool):
                for n in range(NT):
                    if n >= G:
                        pool.wait_ge(used, TOPK * (n - G + 1))
                    else:
                        pool.wait_ge(cleared, n + 1)
                    for k in range(TOPK):
                        pool.indirect_dma_start(y[:, n % G, k, :], None, env["ye"],
                                                bass.IndirectOffsetOnAxis(ap=r["slot"][:, n, k:k + 1], axis=0),
                                                bounds_check=SLOTS - 1, oob_is_err=False).then_inc(got[n % G], 16)

            @block.vector
            def _(dve):
                for n in range(G):
                    dve.memset(y[:, n], 0.0).then_inc(cleared, 1)
                for n in range(NT):
                    dve.wait_ge(got[n % G], 16 * TOPK * (n // G + 1))
                    for k in range(TOPK):
                        if k:
                            dve.wait_ge(used, TOPK * n + k)
                        dve.scalar_tensor_tensor(out=X[:, n, :], in0=y[:, n % G, k, :], scalar=r["wk"][:, n, k:k + 1],
                                                 in1=X[:, n, :], op0=ALU.mult, op1=ALU.add).then_inc(used, 1)

            @block.sync
            def _(sp):
                for n in range(NT):
                    sp.wait_ge(used, TOPK * (n + 1))
                    sp.dma_start(out_v[:, n, :], X[:, n, :]).then_inc(stored, 16)
                sp.wait_ge(stored, 16 * NT)


_INS = ['L0_attn_x', 'L0_attn_W_q', 'L0_attn_W_k', 'L0_attn_W_v', 'L0_attn_W_o', 'L0_ffn_W1', 'L0_ffn_W2',
        'L0_ffn_W3', 'L1_attn_Wq', 'L1_attn_Wk', 'L1_attn_Wv', 'L1_attn_Wo', 'L1_attn_lam', 'L1_ffn_Wr', 'L1_ffn_Wg',
        'L1_ffn_Wu', 'L1_ffn_Wd', 'L1_ffn_Wsg', 'L1_ffn_Wsu', 'L1_ffn_Wsd', 'L1_ffn_Wse']


def _lay_out(name, a):
    import numpy as _np
    if name in ("L0_ffn_W1", "L0_ffn_W2", "L0_ffn_W3"):
        a = a.T
    if name == "L1_attn_Wq":
        a = a.reshape(512, 2, 2, 4, 2, 64).transpose(0, 1, 3, 4, 2, 5).reshape(512, 2048)
    if name == "L1_attn_Wk":
        a = a.reshape(512, 2, 2, 2, 64).transpose(0, 1, 3, 2, 4).reshape(512, 512)
    if name == "L1_attn_Wo":
        a = a.reshape(2, 2, 4, 128, 512).transpose(0, 2, 1, 3, 4).reshape(2048, 512)
    return _np.ascontiguousarray(a)


def kernel(**inputs):
    import numpy as _np
    import concourse.bacc as _bacc
    from concourse import mybir as _mybir
    from concourse.bass_utils import run_bass_kernel_spmd as _run

    nc = _bacc.Bacc("TRN2", target_bir_lowering=False, num_devices=1)
    arrays, args = {}, {}
    for name in _INS:
        a = _lay_out(name, _np.asarray(inputs[name]))
        arrays[f"in_{name}_dram"] = a
        args[name] = nc.dram_tensor(f"in_{name}_dram", a.shape, _mybir.dt.from_np(a.dtype), kind="ExternalInput").ap()
    out = nc.dram_tensor("out_0_dram", (BATCH, SEQ, D), F32, kind="ExternalOutput").ap()
    build(nc, args, out)
    r = _run(nc, [arrays], core_ids=[0])
    return r.results[0]["out_0_dram"]
```
